# Optimizing a Trainium2 kernel written in Bass

```python
import numpy as np
import jax
import jax.numpy as jnp

def _softmax(x, axis=-1):
    return jax.nn.softmax(x, axis=axis)

def _gelu(x):
    return jax.nn.gelu(x, approximate=True)

def _silu(x):
    return jax.nn.silu(x)

def _sigmoid(x):
    return jax.nn.sigmoid(x)

def _layernorm(x, axis=-1, eps=1e-05):
    m = jnp.mean(x, axis=axis, keepdims=True)
    v = jnp.var(x, axis=axis, keepdims=True)
    return (x - m) / jnp.sqrt(v + eps)

def _scatter_add(tgt, idx, src, axis=0):
    return tgt.at[idx].add(src)

def _segment_sum(src, seg, n):
    return jax.ops.segment_sum(src, seg, n)
kernel_name = 'mk_adaln_attn_ffn_d1_seqx_r8_97d46f'

def setup_inputs(seed: int=0):
    np.random.seed(seed)
    _w = jnp.asarray

    def _rec_inputs():
        import jax
        import jax.numpy as jnp
        _rk = jax.random.key(seed)
        x = -0.0002928 + 1 * jax.random.normal(jax.random.fold_in(_rk, 1), (2, 512, 128), jnp.float32)
        _lenS = 512 - jax.random.randint(jax.random.fold_in(_rk, 7), (2,), 0, max(1, 512 // 4) + 1, jnp.int32)
        _lenS2 = 512 - jax.random.randint(jax.random.fold_in(_rk, 8), (2,), 0, max(1, 512 // 4) + 1, jnp.int32)
        itok_Sx32_0_1023 = jax.random.randint(jax.random.fold_in(_rk, 12), (512, 32), 0, 128, jnp.int32)
        condB_uprev = -0.456674 + 0.753242 * jax.random.normal(jax.random.fold_in(_rk, 14), (2,), jnp.float32)
        condB_zX = jax.random.uniform(jax.random.fold_in(_rk, 15), (2,), jnp.float32, 0.0, 0.983423)
        condB_zY = jax.random.uniform(jax.random.fold_in(_rk, 16), (2,), jnp.float32, 0.0, 0.979075)
        condB_zR = jax.random.uniform(jax.random.fold_in(_rk, 17), (2,), jnp.float32, 0.0, 0.9968)
        _validS = jnp.arange(512)[None, :] < _lenS[:, None]
        _validS2 = jnp.arange(512)[None, :] < _lenS2[:, None]
        _causal = jnp.tril(jnp.ones((512, 512), dtype=bool))
        mask_SxS_bk0 = jnp.logical_not(jnp.broadcast_to(_validS[0:1, :], (512, 512)))
        mask_Sx32_bk1 = jnp.ones((512, 32), dtype=bool)
        return (x, itok_Sx32_0_1023, condB_uprev, condB_zX, condB_zY, condB_zR, mask_SxS_bk0, mask_Sx32_bk1)
    x, itok_Sx32_0_1023, condB_uprev, condB_zX, condB_zY, condB_zR, mask_SxS_bk0, mask_Sx32_bk1 = _rec_inputs()

    def _L0_cond_setup():
        import jax, jax.numpy as jnp
        import numpy as np
        B, S, D, H = (4, 128, 128, 16)
        DH = D // H
        K_SPARSE = 32
        LAMBDA_MAX, ALPHA = (10.0, 5.0)
        SPARSE_THRESHOLD = 1.0
        key = jax.random.key(seed)
        ks = jax.random.split(key, 12)
        x = jax.random.normal(ks[0], (B, S, D), dtype=jnp.float32)
        prior_mask = jax.random.bernoulli(ks[1], 0.1, (S, S))
        prior_indices = jax.random.randint(ks[2], (S, K_SPARSE), 0, S)
        prior_index_mask = jax.random.bernoulli(ks[3], 0.9, (S, K_SPARSE))
        prior_index_mask = prior_index_mask.at[:, 0].set(True)
        u_prev = jax.random.normal(ks[4], (B, 1), dtype=jnp.float32)
        sc = 1.0 / np.sqrt(D)
        Wq = jax.random.normal(ks[5], (D, D), dtype=jnp.float32) * sc
        Wk = jax.random.normal(ks[6], (D, D), dtype=jnp.float32) * sc
        Wv = jax.random.normal(ks[7], (D, D), dtype=jnp.float32) * sc
        Wo = jax.random.normal(ks[8], (D, D), dtype=jnp.float32) * sc
        bq = jnp.zeros((D,), jnp.float32)
        bk = jnp.zeros((D,), jnp.float32)
        bv = jnp.zeros((D,), jnp.float32)
        bo = jnp.zeros((D,), jnp.float32)
        return {'x': x, 'prior_mask': prior_mask, 'prior_indices': prior_indices, 'prior_index_mask': prior_index_mask, 'u_prev': u_prev, 'Wq': Wq, 'bq': bq, 'Wk': Wk, 'bk': bk, 'Wv': Wv, 'bv': bv, 'Wo': Wo, 'bo': bo}
    _L0_cond_all = _L0_cond_setup()
    _L0_cond_in = {k: v for k, v in _L0_cond_all.items() if k in ('Wq', 'bq', 'Wk', 'bk', 'Wv', 'bv', 'Wo', 'bo')}
    del _L0_cond_all

    def _L0_attn_setup():
        import jax, jax.numpy as jnp
        import numpy as np
        D_MODEL = 128
        N_HEADS = 16
        D_HEAD = 64
        VAR_EPS = 1e-05
        INIT_RANGE = 0.02
        B, S = (2, 256)

        def _layernorm(x, w, b):
            mean = jnp.mean(x, axis=-1, keepdims=True)
            var = jnp.var(x, axis=-1, keepdims=True)
            norm = (x - mean) / jnp.sqrt(var + VAR_EPS)
            return norm * w + b
        key = jax.random.key(seed)
        ks = jax.random.split(key, 6)
        resid_stream = jax.random.normal(ks[0], (B, S, D_MODEL), dtype=jnp.float32)
        attn_mask = jnp.ones((B, S), dtype=jnp.int32)
        W_q = jax.random.normal(ks[1], (N_HEADS, D_MODEL, D_HEAD), dtype=jnp.float32) * INIT_RANGE
        W_k = jax.random.normal(ks[2], (N_HEADS, D_MODEL, D_HEAD), dtype=jnp.float32) * INIT_RANGE
        W_v = jax.random.normal(ks[3], (N_HEADS, D_MODEL, D_HEAD), dtype=jnp.float32) * INIT_RANGE
        W_o = jax.random.normal(ks[4], (N_HEADS, D_HEAD, D_MODEL), dtype=jnp.float32) * INIT_RANGE
        b_q = jnp.zeros((N_HEADS, D_HEAD), dtype=jnp.float32)
        b_k = jnp.zeros((N_HEADS, D_HEAD), dtype=jnp.float32)
        b_v = jnp.zeros((N_HEADS, D_HEAD), dtype=jnp.float32)
        b_o = jnp.zeros((D_MODEL,), dtype=jnp.float32)
        ln_w = jnp.ones((D_MODEL,), dtype=jnp.float32)
        ln_b = jnp.zeros((D_MODEL,), dtype=jnp.float32)
        return dict(resid_stream=resid_stream, attn_mask=attn_mask, W_q=W_q, W_k=W_k, W_v=W_v, W_o=W_o, b_q=b_q, b_k=b_k, b_v=b_v, b_o=b_o, ln_w=ln_w, ln_b=ln_b)
    _L0_attn_all = _L0_attn_setup()
    _L0_attn_in = {k: v for k, v in _L0_attn_all.items() if k in ('attn_mask', 'W_q', 'W_k', 'W_v', 'W_o', 'b_q', 'b_k', 'b_v', 'b_o', 'ln_w', 'ln_b')}
    del _L0_attn_all

    def _L0_cond2_setup():
        import jax, jax.numpy as jnp
        import numpy as np
        key = jax.random.key(seed)
        k1, k2, k3, k4 = jax.random.split(key, 4)
        B, H, W = (64, 128, 128)
        return {'y': jax.random.uniform(k1, (B, H, W), dtype=jnp.float32), 'zX': jax.random.uniform(k2, (B, 1), dtype=jnp.float32), 'zY': jax.random.uniform(k3, (B, 1), dtype=jnp.float32), 'zR': jax.random.uniform(k4, (B, 1), dtype=jnp.float32), 'dx': 1, 'dy': 1}
    _L0_cond2_all = _L0_cond2_setup()
    _L0_cond2_in = {k: v for k, v in _L0_cond2_all.items() if k in ()}
    del _L0_cond2_all

    def _L0_ffn_setup():
        import jax, jax.numpy as jnp
        import numpy as np
        TOP_K = 2
        key = jax.random.key(seed)
        k1, k2, k3, k4 = jax.random.split(key, 4)
        B, T, D, H, E = (4, 256, 128, 256, 8)
        scale = 0.02
        x = jax.random.normal(k1, (B, T, D), dtype=jnp.float32)
        Wg = jax.random.normal(k2, (D, E), dtype=jnp.float32) * scale
        W1 = jax.random.normal(k3, (E, D, H), dtype=jnp.float32) * scale
        W2 = jax.random.normal(k4, (E, H, D), dtype=jnp.float32) * scale
        return {'x': x, 'Wg': Wg, 'W1': W1, 'W2': W2}
    _L0_ffn_all = _L0_ffn_setup()
    _L0_ffn_in = {k: v for k, v in _L0_ffn_all.items() if k in ('Wg', 'W1', 'W2')}
    del _L0_ffn_all
    return {'x': x, 'itok_Sx32_0_1023': itok_Sx32_0_1023, 'condB_uprev': condB_uprev, 'condB_zX': condB_zX, 'condB_zY': condB_zY, 'condB_zR': condB_zR, 'mask_SxS_bk0': mask_SxS_bk0, 'mask_Sx32_bk1': mask_Sx32_bk1, 'L0_cond_Wq': _L0_cond_in['Wq'], 'L0_cond_bq': _L0_cond_in['bq'], 'L0_cond_Wk': _L0_cond_in['Wk'], 'L0_cond_bk': _L0_cond_in['bk'], 'L0_cond_Wv': _L0_cond_in['Wv'], 'L0_cond_bv': _L0_cond_in['bv'], 'L0_cond_Wo': _L0_cond_in['Wo'], 'L0_cond_bo': _L0_cond_in['bo'], 'L0_attn_attn_mask': _L0_attn_in['attn_mask'], 'L0_attn_W_q': _L0_attn_in['W_q'], 'L0_attn_W_k': _L0_attn_in['W_k'], 'L0_attn_W_v': _L0_attn_in['W_v'], 'L0_attn_W_o': _L0_attn_in['W_o'], 'L0_attn_b_q': _L0_attn_in['b_q'], 'L0_attn_b_k': _L0_attn_in['b_k'], 'L0_attn_b_v': _L0_attn_in['b_v'], 'L0_attn_b_o': _L0_attn_in['b_o'], 'L0_attn_ln_w': _L0_attn_in['ln_w'], 'L0_attn_ln_b': _L0_attn_in['ln_b'], 'L0_ffn_Wg': _L0_ffn_in['Wg'], 'L0_ffn_W1': _L0_ffn_in['W1'], 'L0_ffn_W2': _L0_ffn_in['W2']}

def reference(x, itok_Sx32_0_1023, condB_uprev, condB_zX, condB_zY, condB_zR, mask_SxS_bk0, mask_Sx32_bk1, L0_cond_Wq, L0_cond_bq, L0_cond_Wk, L0_cond_bk, L0_cond_Wv, L0_cond_bv, L0_cond_Wo, L0_cond_bo, L0_attn_attn_mask, L0_attn_W_q, L0_attn_W_k, L0_attn_W_v, L0_attn_W_o, L0_attn_b_q, L0_attn_b_k, L0_attn_b_v, L0_attn_b_o, L0_attn_ln_w, L0_attn_ln_b, L0_ffn_Wg, L0_ffn_W1, L0_ffn_W2):
    import jax
    import jax.numpy as jnp

    def _L0_cond_ref(x, prior_mask, prior_indices, prior_index_mask, u_prev, Wq, bq, Wk, bk, Wv, bv, Wo, bo):
        import jax, jax.numpy as jnp
        import numpy as np
        B, S, D, H = (4, 128, 128, 16)
        DH = D // H
        K_SPARSE = 32
        LAMBDA_MAX, ALPHA = (10.0, 5.0)
        SPARSE_THRESHOLD = 1.0
        Bb, Ss, Dd = x.shape
        scale = 1.0 / jnp.sqrt(jnp.asarray(DH, x.dtype))

        def proj(W, b):
            return (x @ W.T + b).reshape(Bb, Ss, H, DH).transpose(0, 2, 1, 3)
        Q, K, V = (proj(Wq, bq), proj(Wk, bk), proj(Wv, bv))
        lam = LAMBDA_MAX * jnp.exp(-ALPHA * u_prev.reshape(Bb))
        use_sparse = lam >= SPARSE_THRESHOLD
        scores = jnp.einsum('bhqd,bhkd->bhqk', Q, K) * scale
        prior_bias = jnp.where(prior_mask[:Ss, :Ss], 0.0, -1.0).astype(x.dtype)
        bias = lam[:, None, None, None] * prior_bias[None, None]
        dense_out = jnp.einsum('bhqk,bhkd->bhqd', jax.nn.softmax(scores + bias, axis=-1), V)
        idx = prior_indices[:Ss]
        Kg = K[:, :, idx]
        Vg = V[:, :, idx]
        s_scores = jnp.einsum('bhsd,bhskd->bhsk', Q, Kg) * scale
        s_scores = jnp.where(prior_index_mask[:Ss][None, None], s_scores, jnp.asarray(-jnp.inf, x.dtype))
        sparse_out = jnp.einsum('bhsk,bhskd->bhsd', jax.nn.softmax(s_scores, axis=-1), Vg)
        out = jnp.where(use_sparse[:, None, None, None], sparse_out, dense_out)
        out = out.transpose(0, 2, 1, 3).reshape(Bb, Ss, Dd)
        return out @ Wo.T + bo

    def _L0_attn_ref(resid_stream, attn_mask, W_q, W_k, W_v, W_o, b_q, b_k, b_v, b_o, ln_w, ln_b):
        import jax, jax.numpy as jnp
        import numpy as np
        D_MODEL = 128
        N_HEADS = 16
        D_HEAD = 64
        VAR_EPS = 1e-05
        INIT_RANGE = 0.02
        B, S = (2, 256)

        def _layernorm(x, w, b):
            mean = jnp.mean(x, axis=-1, keepdims=True)
            var = jnp.var(x, axis=-1, keepdims=True)
            norm = (x - mean) / jnp.sqrt(var + VAR_EPS)
            return norm * w + b
        x = _layernorm(resid_stream, ln_w, ln_b)
        q = jnp.einsum('bsd,hde->bshe', x, W_q) + b_q
        k = jnp.einsum('bsd,hde->bshe', x, W_k) + b_k
        v = jnp.einsum('bsd,hde->bshe', x, W_v) + b_v
        scale = D_HEAD ** (-0.5)
        scores = jnp.einsum('bqhe,bkhe->bhqk', q, k) * scale
        sq, sk = (scores.shape[-2], scores.shape[-1])
        causal = jnp.tril(jnp.ones((sq, sk), dtype=bool))
        scores = jnp.where(causal, scores, -jnp.inf)
        pattern = jax.nn.softmax(scores, axis=-1)
        z = jnp.einsum('bhqk,bkhe->bqhe', pattern, v)
        attn_out = jnp.einsum('bqhe,hed->bqd', z, W_o) + b_o
        return attn_out

    def _L0_cond2_ref(y, zX, zY, zR, dx, dy):
        import jax, jax.numpy as jnp
        import numpy as np
        yp_x = jnp.pad(y, ((0, 0), (0, 0), (1, 1)), mode='reflect')
        lap_x = (yp_x[:, :, :-2] - 2.0 * y + yp_x[:, :, 2:]) / (dx * dx)
        yp_y = jnp.pad(y, ((0, 0), (1, 1), (0, 0)), mode='reflect')
        lap_y = (yp_y[:, :-2, :] - 2.0 * y + yp_y[:, 2:, :]) / (dy * dy)
        du_dt = zX[:, :, None] * lap_x + zY[:, :, None] * lap_y + zR[:, :, None] * y * (1.0 - y)
        return du_dt

    def _L0_ffn_ref(x, Wg, W1, W2):
        import jax, jax.numpy as jnp
        import numpy as np
        TOP_K = 2
        B, T, D = x.shape
        E = Wg.shape[1]
        x_flat = x.reshape(-1, D)
        gate_logits = x_flat @ Wg
        weights = jax.nn.softmax(gate_logits, axis=-1)
        topk_w, topk_idx = jax.lax.top_k(weights, TOP_K)
        topk_w = topk_w / jnp.sum(topk_w, axis=-1, keepdims=True)
        combine = jnp.sum(topk_w[..., None] * jax.nn.one_hot(topk_idx, E, dtype=x.dtype), axis=1)
        h = jax.nn.silu(jnp.einsum('nd,edh->enh', x_flat, W1))
        y = jnp.einsum('enh,ehd->end', h, W2)
        out = jnp.einsum('end,ne->nd', y, combine)
        return out.reshape(B, T, D)
    x = x + _L0_attn_ref(_L0_cond_ref(x, mask_SxS_bk0, itok_Sx32_0_1023, mask_Sx32_bk1, condB_uprev[:, None], L0_cond_Wq, L0_cond_bq, L0_cond_Wk, L0_cond_bk, L0_cond_Wv, L0_cond_bv, L0_cond_Wo, L0_cond_bo), L0_attn_attn_mask, L0_attn_W_q, L0_attn_W_k, L0_attn_W_v, L0_attn_W_o, L0_attn_b_q, L0_attn_b_k, L0_attn_b_v, L0_attn_b_o, L0_attn_ln_w, L0_attn_ln_b)
    x = x + _L0_ffn_ref(_L0_cond2_ref(x, condB_zX[:, None], condB_zY[:, None], condB_zR[:, None], 1, 1), L0_ffn_Wg, L0_ffn_W1, L0_ffn_W2)
    return x

_drawn_inputs = setup_inputs


def setup_inputs(seed=0):
    import zlib

    import numpy as np

    out = dict(_drawn_inputs(seed))
    spreads = {'L0_cond_bq': (0.0, 0.8),
     'L0_cond_bk': (0.0, 0.8),
     'L0_cond_bv': (0.0, 0.1),
     'L0_cond_bo': (0.0, 0.1),
     'L0_attn_b_q': (0.0, 0.8),
     'L0_attn_b_k': (0.0, 0.8),
     'L0_attn_b_v': (0.0, 0.1),
     'L0_attn_b_o': (0.0, 0.1),
     'L0_attn_ln_w': (1.0, 0.6),
     'L0_attn_ln_b': (0.0, 0.517)}
    factors = {'condB_zX': 3.471,
     'condB_zY': 4.532,
     'L0_cond_Wq': 4.388,
     'L0_cond_Wk': 3.739,
     'L0_attn_W_q': 8.0,
     'L0_attn_W_k': 8.0}
    for name, (base, spread) in spreads.items():
        noise = np.random.default_rng([zlib.crc32(name.encode()), seed]).standard_normal(out[name].shape)
        drawn = base * np.exp(spread * noise) if base else spread * noise
        out[name] = jnp.asarray(drawn.astype(out[name].dtype))
    for name, factor in factors.items():
        out[name] = (out[name] * factor).astype(out[name].dtype)
    return out
```

```python
import concourse.bass as bass
from concourse import mybir
from contextlib import ExitStack

B, S, D = 2, 512, 128
T = B * S
TB = S // 128
H1, E1, KS = 16, 8, 32
H2, E2 = 16, 64
NP = H2 // 2
NE, FH = 8, 256
NT = NE * FH // 128
PAD = 32
G1 = H1 // 4
SCALE1, SCALE2 = E1 ** -0.5, E2 ** -0.5
BIG = 1e30


def program(
    nc: bass.Bass,
    xT: bass.AP, wq1: bass.AP, wk1: bass.AP, wv1: bass.AP, wo1: bass.AP,
    cols: bass.AP, bv1: bass.AP, bo1: bass.AP, idx: bass.AP, imask: bass.AP,
    pmN: bass.AP, pmT: bass.AP, scal: bass.AP,
    wq2: bass.AP, wk2: bass.AP, wv2: bass.AP, wo2: bass.AP, bv2: bass.AP,
    wg: bass.AP, w1: bass.AP, w2: bass.AP,
    consts: bass.AP, sel: bass.AP,
    out: bass.AP,
    KB: int = 4,
):
    f32 = mybir.dt.float32
    f32r = mybir.dt.float32r
    bf16 = mybir.dt.bfloat16
    i32 = mybir.dt.int32
    u8 = mybir.dt.uint8
    ALU = mybir.AluOpType
    ACT = mybir.ActivationFunctionType
    AX = mybir.AxisListType
    W = 128 * KB

    ctx = ExitStack()
    with ctx:
        def sb(name, shape, dt=f32):
            return ctx.enter_context(nc.sbuf_tensor(name, shape, dt))

        def sem(name):
            return ctx.enter_context(nc.semaphore(name))

        cst = sb("cst", [128, CONSTS])
        ident = cst[:, C_ID:C_ID + 128]
        ones_band = cst[:, C_BAND:C_BAND + 63]
        iota = cst[:, C_IOTA:C_IOTA + 512]
        row_group = cst[:, C_RG:C_RG + 4]
        half = cst[:, C_HALF:C_HALF + 2]
        lap = cst[:, C_LAP:C_LAP + 128]
        ident_r = sb("ident_r", [128, 128], f32r)
        ident_b = sb("ident_b", [128, 128], bf16)
        causal_r = sb("causal_r", [128, 128], f32r)
        causal_b = sb("causal_b", [128, 128], bf16)
        xT_s = sb("xT_s", [128, T])
        wq1_s = sb("wq1_s", [128, H1 * PAD])
        wk1_s = sb("wk1_s", [128, H1 * PAD])
        wv1_s = sb("wv1_s", [128, H1 * PAD])
        wo1_s = sb("wo1_s", [128, D])
        col_s = sb("col_s", [128, COLS])
        bv1_s = sb("bv1_s", [128, H1 * PAD])
        bo1_s = sb("bo1_s", [128, D])
        idx_s = sb("idx_s", [128, TB, KS], i32)
        im_s = sb("im_s", [128, TB, KS], u8)
        scal_s = sb("scal_s", [128, 8])
        wg_s = sb("wg_s", [128, NE])
        attn1 = ExitStack()

        def sb1(name, shape, dt=f32):
            return attn1.enter_context(nc.sbuf_tensor(name, shape, dt))

        y_s = sb("y_s", [128, TB, D])
        stats = sb("stats", [128, TB, 6])
        mv = sb("mv", [128, TB, 2])
        rstd = sb("rstd", [128, 4, TB])
        xh = sb("xh", [128, TB, D])
        xnT = sb("xnT", [128, T])
        w_q = sb("w_q", [128, H2 * E2])
        w_k = sb("w_k", [128, H2 * E2])
        negM1 = sb("negM1", [128, TB, H1], f32r)
        mraw = sb("mraw", [128, TB, H1])
        mtmp = sb("mtmp", [128, TB, H1])
        lam = sb("lam", [128, 8])

        Q1 = sb1("Q1", [128, B, G1, S])
        Qb1 = sb1("Qb1", [128, B, G1, S], bf16)
        Km = sb1("Km", [128, H1, W])
        Kmb = sb1("Kmb", [128, H1, W], bf16)
        V1 = sb1("V1", [128, B * TB, H1 * PAD])
        biasN = sb1("biasN", [128, B, TB, W], bf16)
        biasTh = sb1("biasTh", [128, B, KB, S], f32r)
        biasTl = sb1("biasTl", [128, B, KB, S], f32r)
        P1 = sb1("P1", [128, 8, S])
        zT1 = sb1("zT1", [128, G1, S])
        rec1 = sb1("rec1", [128, TB, H1])
        zc = sb1("zc", [128, TB, 128])
        zcT = sb1("zcT", [128, S])
        cntN = sb1("cntN", [128, TB, W], bf16)
        idf = sb1("idf", [128, TB, KS])
        idw = sb1("idw", [128, TB, KS])
        idm = sb1("idm", [128, TB, KS])
        oh = sb1("oh", [128, 4, W], bf16)
        tmpA = P1[:, 0:4, :]
        tmpB = P1[:, 4:8, :]
        tmpC = zT1
        pm_s = sb1("pm_s", [128, 4, S], u8)
        pmT_s = sb1("pmT_s", [128, 4, S], u8)
        attn1.close()

        attn2 = ExitStack()

        def sb2(name, shape, dt=f32):
            return attn2.enter_context(nc.sbuf_tensor(name, shape, dt))

        w_v = sb2("w_v", [128, H2 * E2])
        w_o = sb2("w_o", [128, NP, D])
        bv2_s = sb2("bv2_s", [128, H2 * E2])
        w1_s = sb2("w1_s", [128, NT, 128])
        w2_s = sb2("w2_s", [128, NT, D])
        sel_f = sb2("sel_f", [128, NP, 128])
        sel_r = sb2("sel_r", [128, NP, 128], f32r)
        V2 = sb2("V2", [128, TB, H2 * E2])
        KT = sb2("KT", [128, 2, S])
        KTb = sb2("KTb", [128, 2, S], bf16)
        Qm = sb2("Qm", [128, 2, 2, S])
        Qmb = sb2("Qmb", [128, 2, 2, S], bf16)
        P2 = sb2("P2", [128, 4, 1280])
        acc = sb2("acc", [128, 4, S])
        z2 = sb2("z2", [128, NP, S])
        negM2 = sb2("negM2", [128, TB, 2 * H2], f32r)
        sums = sb2("sums", [128, 128])
        rsum = sb2("rsum", [128, 128])
        RDh = sb2("RDh", [128, 4, 128], f32r)
        RDl = sb2("RDl", [128, 4, 128], f32r)
        x1T = sb2("x1T", [128, B, S])
        dif = sb2("dif", [128, S])
        dif2 = sb2("dif2", [128, S])
        rea = sb2("rea", [128, S])
        RDf = rea[:, :].rearrange("p (c q) -> p c q", c=4)
        duT = sb2("duT", [128, S])
        hT = sb2("hT", [128, NT, S])
        gl = sb2("gl", [128, 12, TB, NE])
        gs = sb2("gs", [128, 8, TB])
        comb = sb2("comb", [128, TB, NE])
        ya = sb2("ya", [128, 2, TB, D])
        attn2.close()

        ps = ctx.enter_context(nc.psum_tensor("ps", [128, 8, 512], f32))

        ld_x = sem("ld_x")
        ld_w1 = sem("ld_w1")
        ld_idx = sem("ld_idx")
        ld_cst = sem("ld_cst")
        ld_pm = sem("ld_pm")
        ld_w2 = sem("ld_w2")
        ld_late = sem("ld_late")
        stored = sem("stored")
        cst_ready = sem("cst_ready")
        proj1 = sem("proj1")
        qk1_out = sem("qk1_out")
        v1_out = sem("v1_out")
        onehot = sem("onehot")
        counted = sem("counted")
        cnt_out = sem("cnt_out")
        cnt_turned = sem("cnt_turned")
        ln_in = sem("ln_in")
        ln_out = sem("ln_out")
        lam_out = sem("lam_out")
        bias_out = sem("bias_out")
        kproj = sem("kproj")
        km_out = sem("km_out")
        kmb_out = sem("kmb_out")
        qb_out = sem("qb_out")
        sn1 = sem("sn1")
        max1 = sem("max1")
        negm1 = sem("negm1")
        st1 = sem("st1")
        exp1 = sem("exp1")
        pv1 = sem("pv1")
        z1_out = sem("z1_out")
        z1_turned = sem("z1_turned")
        norm1 = sem("norm1")
        zc_turned = sem("zc_turned")
        zcT_out = sem("zcT_out")
        wo1_done = sem("wo1_done")
        var_out = sem("var_out")
        rstd_out = sem("rstd_out")
        xh_out = sem("xh_out")
        xh_turned = sem("xh_turned")
        xn_out = sem("xn_out")
        vproj2 = sem("vproj2")
        v2_out = sem("v2_out")
        kproj2 = sem("kproj2")
        qproj2 = sem("qproj2")
        k2_out = sem("k2_out")
        q2_out = sem("q2_out")
        qk2b_out = sem("qk2b_out")
        sn2 = sem("sn2")
        max2 = sem("max2")
        st2 = sem("st2")
        exp2 = sem("exp2")
        acc2 = sem("acc2")
        pool_step = sem("pool_step")
        pv2 = sem("pv2")
        z2_out = sem("z2_out")
        sum2 = sem("sum2")
        sum2_out = sem("sum2_out")
        rd_out = sem("rd_out")
        r2 = sem("r2")
        zn_out = sem("zn_out")
        wo2_done = sem("wo2_done")
        x1_out = sem("x1_out")
        lap_done = sem("lap_done")
        du_out = sem("du_out")
        gate_done = sem("gate_done")
        gate_out = sem("gate_out")
        gmax_out = sem("gmax_out")
        gexp_out = sem("gexp_out")
        x1_turned = sem("x1_turned")
        ya_ready = sem("ya_ready")
        up_done = sem("up_done")
        silu_out = sem("silu_out")
        down_done = sem("down_done")
        mixed = sem("mixed")
        dve_step = sem("dve_step")
        act_step = sem("act_step")

        NQ = G1 * KB
        NU = TB if KB == 1 else H1
        KOFF = [0, 512, 1024, 896]
        QPOS = [(1, 384), (2, 0), (1, 0), (0, 0)]

        block = ctx.enter_context(nc.Block())

        @block.sync
        def _(sp):
            sp.dma_start(xT_s[:, :], xT).then_inc(ld_x, 16)
            sp.dma_start(wq1_s[:, :], wq1).then_inc(ld_w1, 16)
            sp.dma_start(wk1_s[:, :], wk1).then_inc(ld_w1, 16)
            sp.dma_start(wv1_s[:, :], wv1).then_inc(ld_w1, 16)
            sp.dma_start(bv1_s[:, :], bv1).then_inc(ld_w1, 16)
            sp.dma_start(pm_s[:, :, :], pmN.rearrange("p (b k) -> p b k", b=4)).then_inc(ld_pm, 16)
            sp.dma_start(pmT_s[:, :, :], pmT.rearrange("p (b k) -> p b k", b=4)).then_inc(ld_pm, 16)
            sp.dma_start(wo1_s[:, :], wo1).then_inc(ld_w2, 16)
            sp.dma_start(bo1_s[:, :], bo1).then_inc(ld_w2, 16)
            sp.dma_start(w_q[:, :], wq2).then_inc(ld_w2, 16)
            sp.dma_start(w_k[:, :], wk2).then_inc(ld_w2, 16)
            sp.dma_start(wg_s[:, :], wg).then_inc(ld_w2, 16)
            sp.wait_ge(xn_out, B)
            sp.dma_start(w_v[:, :], wv2).then_inc(ld_late, 16)
            sp.dma_start(bv2_s[:, :], bv2).then_inc(ld_late, 16)
            sp.dma_start(sel_f[:, :, :], sel.rearrange("p (n m) -> p n m", n=NP)).then_inc(ld_late, 16)
            sp.dma_start(w_o[:, :, :], wo2.rearrange("p (n m) -> p n m", n=NP)).then_inc(ld_late, 16)
            sp.dma_start(w1_s[:, :, :], w1.rearrange("p (n m) -> p n m", n=NT)).then_inc(ld_late, 16)
            sp.dma_start(w2_s[:, :, :], w2.rearrange("p (n m) -> p n m", n=NT)).then_inc(ld_late, 16)
            for b in range(B):
                sp.wait_ge(mixed, (b + 1) * TB * 2)
                sp.dma_start(out[b].rearrange("(t p) d -> p t d", p=128), ya[:, b, :, :]).then_inc(stored, 16)
            sp.wait_ge(stored, 16 * B)

        def pool_sum(pool, link, h):
            pool.wait_ge(exp2, h + 1)
            if h >= 4:
                pool.wait_ge(sum2, (h - 4) // 2 + 1)
            p, a = P2[:, h % 4, :], acc[:, h % 4, :]
            link(nc.gpsimd.tensor_tensor(a[:, 128:512], p[:, 128:512], p[:, KOFF[1]:KOFF[1] + 384], ALU.add))
            link(nc.gpsimd.tensor_tensor(a[:, 256:512], a[:, 256:512], p[:, KOFF[2]:KOFF[2] + 256], ALU.add))
            nc.gpsimd.tensor_tensor(a[:, 384:512], a[:, 384:512], p[:, KOFF[3]:KOFF[3] + 128], ALU.add)\
                .then_inc(acc2, 1)

        @block.gpsimd
        def _(pool):
            pool.dma_start(idx_s[:, :, :], idx.rearrange("p (b j) -> p b j", b=TB)).then_inc(ld_idx, 16)
            pool.dma_start(im_s[:, :, :], imask.rearrange("p (b j) -> p b j", b=TB)).then_inc(ld_idx, 16)
            for b in range(B):
                pool.wait_ge(qk1_out, (b + 1) * G1)
                nc.gpsimd.tensor_copy(Qb1[:, b, :, :], Q1[:, b, :, :]).then_inc(qb_out, 1)
            for b in range(B):
                for g in range(G1):
                    pool.wait_ge(km_out, b * G1 + g + 1)
                    if b and not g:
                        pool.wait_ge(sn1, NU * b)
                    nc.gpsimd.tensor_copy(Kmb[:, 4 * g:4 * g + 4, :], Km[:, 4 * g:4 * g + 4, :])\
                        .then_inc(kmb_out, 1)
            steps = [0]

            def link(ins):
                steps[0] += 1
                ins.then_inc(pool_step, 1)
                pool.wait_ge(pool_step, steps[0])

            for b in range(B):
                for p in range(NP):
                    n = b * NP + p
                    pool.wait_ge(k2_out, n + 1)
                    if n >= 2:
                        pool.wait_ge(sn2, 2 * (n - 1))
                    nc.gpsimd.tensor_copy(KTb[:, n % 2, :], KT[:, n % 2, :])
                    pool.wait_ge(q2_out, n + 1)
                    nc.gpsimd.tensor_copy(Qmb[:, n % 2, :, :], Qm[:, n % 2, :, :]).then_inc(qk2b_out, 1)
                    for h in ((2 * n - 2, 2 * n - 1) if p else ()):
                        pool_sum(pool, link, h)
                for h in (2 * n, 2 * n + 1):
                    pool_sum(pool, link, h)

        def z_out(act, b, g):
            act.wait_ge(pv1, (b * NQ) + (g + 1) * KB)
            if b:
                act.wait_ge(z1_turned, b * TB)
            nc.scalar.activation(zT1[:, g, :], ps[:, 6, :], ACT.Copy).then_inc(z1_out, 1)

        def z2_copy(act, n):
            act.wait_ge(pv2, n + 1)
            if n >= NP:
                act.wait_ge(wo2_done, n // NP)
            nc.scalar.activation(z2[:, n % NP, :], ps[:, 6, :], ACT.Copy).then_inc(z2_out, 1)

        @block.scalar
        def _(act):
            act.dma_start(cst[:, :], consts).then_inc(ld_cst, 16)
            act.dma_start(col_s[:, :], cols).then_inc(ld_cst, 16)
            act.dma_start(scal_s[:, :], scal).then_inc(ld_cst, 16)
            act.wait_ge(ld_cst, 48)
            nc.scalar.activation(lam[:, 0:B], scal_s[:, 0:B], ACT.Exp, scale=-5.0).then_inc(lam_out, 1)
            for j in range(B * G1):
                act.wait_ge(proj1, j + 1)
                nc.scalar.activation(Q1[:, j // G1, j % G1, :], ps[:, j % 8, :], ACT.Identity,
                                     bias=col_s[:, L_BQ1 + j % G1:L_BQ1 + j % G1 + 1]).then_inc(qk1_out, 1)
            for k in range(2):
                act.wait_ge(ln_in, k + 1)
                counts = tmpA[:, :, 0:W] if k == 0 else tmpA[:, 0:KB, :]
                nc.scalar.activation(counts, counts, ACT.Ln).then_inc(ln_out, 1)

            def k_masked(b):
                for g in range(G1):
                    act.wait_ge(kproj, b * G1 + g + 1)
                    for i in range(4):
                        h = 4 * g + i
                        o = nc.scalar.activation(Km[:, h, :], ps[:, g, 0:W], ACT.Identity,
                                                 bias=col_s[:, L_BK1 + h:L_BK1 + h + 1],
                                                 scale=row_group[:, i:i + 1])
                    o.then_inc(km_out, 1)

            for b in range(B):
                k_masked(b)
                for n in range(4 * NQ):
                    c = b * 4 * NQ + n
                    act.wait_ge(st1, c + 1)
                    if c >= 8:
                        act.wait_ge(pv1, c // 4 - 1)
                    nc.scalar.activation(P1[:, c % 8, :], ps[:, 4 + c % 2, :], ACT.Exp, scale=SCALE1)\
                        .then_inc(exp1, 1)
                    q = n // 4 - 1
                    if n % 4 == 3 and q >= 0 and q % KB == KB - 1:
                        z_out(act, b, q // KB)
                z_out(act, b, G1 - 1)
                act.wait_ge(zc_turned, b + 1)
                nc.scalar.activation(zcT[:, :], ps[:, 6, :], ACT.Copy).then_inc(zcT_out, 1)
                act.wait_ge(var_out, b + 1)
                nc.scalar.activation(rstd[:, 1, :], rstd[:, 0, :], ACT.Ln).then_inc(act_step, 1)
                act.wait_ge(act_step, b + 1)
                nc.scalar.activation(rstd[:, 1, :], rstd[:, 1, :], ACT.Exp, scale=-0.5).then_inc(rstd_out, 1)

            for b in range(B):
                for n in range(b * NP, (b + 1) * NP):
                    for j in range(2):
                        h = 2 * n + j
                        act.wait_ge(st2, h + 1)
                        if h >= 4:
                            act.wait_ge(pv2, (h - 4) // 2 + 1)
                            act.wait_ge(acc2, h - 3)
                            act.wait_ge(sum2, (h - 4) // 2 + 1)
                        nc.scalar.activation(P2[:, h % 4, :], ps[:, 3:6, :].rearrange("p b n -> p (b n)")[:, 0:1280],
                                             ACT.Exp, scale=SCALE2).then_inc(exp2, 1)
                        if j == 0 and n > b * NP:
                            z2_copy(act, n - 1)
                z2_copy(act, (b + 1) * NP - 1)
                act.wait_ge(gmax_out, b + 1)
                nc.scalar.activation(gl[:, 1, :, :], gl[:, 1, :, :], ACT.Exp).then_inc(gexp_out, 1)
                act.wait_ge(x1_turned, b + 1)
                nc.scalar.activation(ya[:, b, :, :], ps[:, 7, :].rearrange("p (t d) -> p t d", t=TB), ACT.Copy)\
                    .then_inc(ya_ready, 1)
                for n in range(NT):
                    act.wait_ge(up_done, b * NT + n + 1)
                    if b and n == 0:
                        act.wait_ge(down_done, b * TB * 2)
                    nc.scalar.activation(hT[:, n, :], ps[:, n % 4, :], ACT.Silu).then_inc(silu_out, 1)

        @block.vector
        def _(dve):
            steps = [0]

            def link(ins):
                steps[0] += 1
                ins.then_inc(dve_step, 1)
                dve.wait_ge(dve_step, steps[0])

            dve.wait_ge(ld_cst, 48)
            nc.vector.tensor_copy(ident_r[:, :], ident)
            nc.vector.tensor_copy(causal_r[:, :], cst[:, C_CAUT:C_CAUT + 128])
            nc.vector.tensor_copy(causal_b[:, :], cst[:, C_CAUN:C_CAUN + 128])
            nc.vector.tensor_copy(ident_b[:, :], ident).then_inc(cst_ready, 1)
            dve.wait_ge(ld_idx, 32)
            link(nc.vector.tensor_copy(idf[:, :, :], idx_s[:, :, :]))
            link(nc.vector.tensor_scalar(idw[:, :, :], idf[:, :, :], 0.0, float(S), ALU.is_lt, ALU.mult))
            link(nc.vector.tensor_tensor(idf[:, :, :], idf[:, :, :], idw[:, :, :], ALU.add))
            link(nc.vector.tensor_scalar(idf[:, :, :], idf[:, :, :], 0.0, float(S - 1), ALU.max, ALU.min))
            link(nc.vector.tensor_copy(idw[:, :, :], im_s[:, :, :]))
            link(nc.vector.scalar_tensor_tensor(idm[:, :, :], idf[:, :, :], 1.0, idw[:, :, :], ALU.add, ALU.mult))
            link(nc.vector.tensor_scalar(idm[:, :, :], idm[:, :, :], 1.0, None, ALU.subtract))

            dve.wait_ge(ld_w1, 64)
            for t in range(B * TB):
                dve.wait_ge(proj1, B * G1 + t + 1)
                nc.vector.tensor_tensor(V1[:, t, :], ps[:, t % 8, :], bv1_s[:, :], ALU.add).then_inc(v1_out, 1)

            for q in range(TB):
                for j in range(KS):
                    n = q * KS + j
                    if n >= 4:
                        dve.wait_ge(counted, n - 3)
                    nc.vector.tensor_scalar(oh[:, n % 4, :], iota[:, 0:W], idm[:, q, j:j + 1], None, ALU.is_equal)\
                        .then_inc(onehot, 1)
                dve.wait_ge(counted, (q + 1) * KS)
                nc.vector.tensor_copy(cntN[:, q, :], ps[:, q % 2, 0:W]).then_inc(cnt_out, 1)

            dve.wait_ge(lam_out, 1)
            link(nc.vector.tensor_scalar(lam[:, 2:4], lam[:, 0:2], 10.0, None, ALU.mult))
            link(nc.vector.tensor_scalar(lam[:, 4:6], lam[:, 2:4], 1.0, None, ALU.is_ge))
            link(nc.vector.tensor_scalar(lam[:, 2:4], lam[:, 2:4], 1.0, 1.0 / SCALE1, ALU.min, ALU.mult))
            link(nc.vector.tensor_scalar(lam[:, 6:8], lam[:, 4:6], -1.0, 1.0, ALU.mult, ALU.add))
            link(nc.vector.tensor_tensor(lam[:, 6:8], lam[:, 6:8], lam[:, 2:4], ALU.mult))

            dve.wait_ge(ld_pm, 32)
            dve.wait_ge(cnt_out, TB)
            A, Bb, Cc = tmpA[:, :, 0:W], tmpB[:, :, 0:W], tmpC[:, :, 0:W]
            nc.vector.tensor_scalar(A, cntN[:, :, :], 1.0, None, ALU.max).then_inc(ln_in, 1)
            link(nc.vector.tensor_scalar(Bb, cntN[:, :, :], 0.5, -BIG, ALU.is_lt, ALU.mult))
            dve.wait_ge(ln_out, 1)
            link(nc.vector.scalar_tensor_tensor(Bb, A, 1.0 / SCALE1, Bb, ALU.mult, ALU.add))
            for b in range(B):
                link(nc.vector.tensor_scalar(Cc, pm_s[:, :, 0:W], 1.0, lam[:, 6 + b:7 + b], ALU.subtract, ALU.mult))
                link(nc.vector.scalar_tensor_tensor(biasN[:, b, :, :], Bb, lam[:, 4 + b:5 + b], Cc, ALU.mult, ALU.add))
            cT = ps[:, 2:2 + KB, :].bitcast(bf16)[:, :, 0:512]
            A, Bb, Cc = tmpA[:, 0:KB, :], tmpB[:, 0:KB, :], tmpC[:, 0:KB, :]
            dve.wait_ge(cnt_turned, TB)
            nc.vector.tensor_scalar(A, cT, 1.0, None, ALU.max).then_inc(ln_in, 1)
            link(nc.vector.tensor_scalar(Bb, cT, 0.5, -BIG, ALU.is_lt, ALU.mult))
            dve.wait_ge(ln_out, 2)
            link(nc.vector.scalar_tensor_tensor(Bb, A, 1.0 / SCALE1, Bb, ALU.mult, ALU.add))
            for b in range(B):
                link(nc.vector.tensor_scalar(Cc, pmT_s[:, 0:KB, :], 1.0, lam[:, 6 + b:7 + b], ALU.subtract, ALU.mult))
                link(nc.vector.scalar_tensor_tensor(A, Bb, lam[:, 4 + b:5 + b], Cc, ALU.mult, ALU.add))
                link(nc.vector.tensor_copy(biasTh[:, b, :, :], A))
                o = nc.vector.tensor_tensor(biasTl[:, b, :, :], A, biasTh[:, b, :, :].bitcast(f32), ALU.subtract)
                if b < B - 1:
                    link(o)
            o.then_inc(bias_out, 1)

            for b in range(B):
                for u in range(NU):
                    dve.wait_ge(sn1, b * NU + u + 1)
                    if KB == 1:
                        o = nc.vector.tensor_reduce(mraw[:, u, :], ps[:, 0:4, :].rearrange("p g (i k) -> p g i k", i=4),
                                                    axis=AX.X, op=ALU.max, negate=True)
                    else:
                        o = nc.vector.tensor_reduce(mraw[:, :, u], ps[:, 0:4, :], axis=AX.X, op=ALU.max, negate=True)
                    o.then_inc(max1, 1)
                dve.wait_ge(max1, (b + 1) * NU)
                if b:
                    dve.wait_ge(st1, 4 * NQ * b)
                link(nc.vector.tensor_scalar(mtmp[:, :, :], mraw[:, :, :], BIG, None, ALU.mult))
                link(nc.vector.tensor_tensor(mtmp[:, :, :], mtmp[:, :, :], mtmp[:, :, :], ALU.subtract))
                nc.vector.tensor_tensor(negM1[:, :, :], mraw[:, :, :], mtmp[:, :, :], ALU.add).then_inc(negm1, 1)
                for q in range(TB):
                    n = b * TB + q
                    dve.wait_ge(z1_turned, n + 1)
                    z = ps[:, 6 + q % 2, :].rearrange("p (h c) -> p h c", c=PAD)
                    link(nc.vector.reciprocal(rec1[:, q, :], z[:, :, E1]))
                    nc.vector.tensor_tensor(zc[:, q, :].rearrange("p (h c) -> p h c", c=E1), z[:, :, 0:E1],
                                            rec1[:, q, :].unsqueeze(2).broadcast_to([128, H1, E1]), ALU.mult)\
                        .then_inc(norm1, 1)
                dve.wait_ge(wo1_done, b + 1)
                dve.wait_ge(ld_w2, 80)
                link(nc.vector.tensor_tensor(y_s[:, :, :], ps[:, 7, :].rearrange("p (t d) -> p t d", t=TB),
                                             bo1_s[:, :].unsqueeze(1).broadcast_to([128, TB, D]), ALU.add))
                for t in range(TB):
                    link(nc.vector.bn_stats(stats[:, t, :], y_s[:, t, :]))
                for t in range(TB):
                    link(nc.vector.bn_aggr(mv[:, t, :], stats[:, t, :]))
                nc.vector.tensor_scalar(rstd[:, 0, :], mv[:, :, 1], 1e-5, None, ALU.add).then_inc(var_out, 1)
                dve.wait_ge(rstd_out, b + 1)
                link(nc.vector.tensor_tensor(rstd[:, 2, :], rstd[:, 1, :], rstd[:, 1, :], ALU.mult))
                link(nc.vector.tensor_tensor(rstd[:, 2, :], rstd[:, 2, :], rstd[:, 0, :], ALU.mult))
                link(nc.vector.tensor_scalar(rstd[:, 2, :], rstd[:, 2, :], -0.5, 1.5, ALU.mult, ALU.add))
                link(nc.vector.tensor_tensor(rstd[:, 3, :], rstd[:, 2, :], rstd[:, 1, :], ALU.mult))
                if b:
                    dve.wait_ge(xh_turned, b)
                for t in range(TB):
                    o = nc.vector.tensor_scalar(xh[:, t, :], y_s[:, t, :], mv[:, t, 0:1], rstd[:, 3, t:t + 1],
                                                ALU.subtract, ALU.mult)
                o.then_inc(xh_out, 1)
                dve.wait_ge(xh_turned, b + 1)
                nc.vector.tensor_scalar(xnT[:, b * S:(b + 1) * S], ps[:, 6, :], col_s[:, L_LNW:L_LNW + 1],
                                        col_s[:, L_LNB:L_LNB + 1], ALU.mult, ALU.add).then_inc(xn_out, 1)

            dve.wait_ge(ld_late, 96)
            nc.vector.tensor_copy(sel_r[:, :, :], sel_f[:, :, :]).then_inc(cst_ready, 1)

            def kq_out(n):
                if n >= 2:
                    dve.wait_ge(st2, 2 * (n - 1))
                    dve.wait_ge(qk2b_out, n - 1)
                p = n % NP
                dve.wait_ge(kproj2, n + 1)
                nc.vector.tensor_scalar(KT[:, n % 2, :], ps[:, 7, :], col_s[:, L_BK2 + p:L_BK2 + p + 1], None, ALU.add)\
                    .then_inc(k2_out, 1)
                dve.wait_ge(qproj2, n + 1)
                for j in range(2):
                    o = nc.vector.tensor_scalar(Qm[:, n % 2, j, :], ps[:, 7, :], half[:, j:j + 1],
                                                col_s[:, L_BQ2 + 2 * p + j:L_BQ2 + 2 * p + j + 1], ALU.mult, ALU.add)
                o.then_inc(q2_out, 1)

            def maxima(h):
                dve.wait_ge(sn2, h + 1)
                for q in range(TB):
                    bank, at = QPOS[q]
                    o = nc.vector.tensor_reduce(negM2[:, q, h:h + 1], ps[:, bank, at:at + 128 * (q + 1)],
                                                axis=AX.X, op=ALU.max, negate=True)
                o.then_inc(max2, 1)

            def sums_out(n):
                dve.wait_ge(sum2, n + 1)
                if n % NP == 0:
                    if n:
                        dve.wait_ge(rd_out, n // NP)
                    o = nc.vector.tensor_copy(sums[:, :], ps[:, 7, 0:128])
                else:
                    dve.wait_ge(sum2_out, n)
                    o = nc.vector.tensor_tensor(sums[:, :], sums[:, :], ps[:, 7, 0:128], ALU.add)
                o.then_inc(sum2_out, 1)

            for b in range(B):
                for t in range(2 * TB):
                    dve.wait_ge(vproj2, b * 2 * TB + t + 1)
                    if b:
                        dve.wait_ge(pv2, b * NP)
                    nc.vector.tensor_tensor(V2[:, t // 2, (t % 2) * 512:(t % 2 + 1) * 512], ps[:, t % 6, :],
                                            bv2_s[:, (t % 2) * 512:(t % 2 + 1) * 512], ALU.add).then_inc(v2_out, 1)
                kq_out(b * NP)
                maxima(2 * b * NP)
                for p in range(NP):
                    n = b * NP + p
                    if p < NP - 1:
                        kq_out(n + 1)
                    maxima(2 * n + 1)
                    if p >= 1:
                        sums_out(n - 1)
                    if p < NP - 1:
                        maxima(2 * n + 2)
                sums_out((b + 1) * NP - 1)
                dve.wait_ge(sum2_out, (b + 1) * NP)
                link(nc.vector.reciprocal(rsum[:, :], sums[:, :]))
                for c in range(4):
                    link(nc.vector.tensor_scalar(RDf[:, c, :], rsum[:, :], row_group[:, c:c + 1], None, ALU.mult))
                link(nc.vector.tensor_copy(RDh[:, :, :], RDf[:, :, :]))
                nc.vector.tensor_tensor(RDl[:, :, :], RDf[:, :, :], RDh[:, :, :].bitcast(f32), ALU.subtract)\
                    .then_inc(rd_out, 1)
                dve.wait_ge(z2_out, (b + 1) * NP)
                for p in range(NP):
                    dve.wait_ge(r2, b * NP + p + 1)
                    nc.vector.tensor_tensor(z2[:, p, :], ps[:, p % 6, :], z2[:, p, :], ALU.mult).then_inc(zn_out, 1)
                y = x1T[:, b, :]
                dve.wait_ge(wo2_done, b + 1)
                nc.vector.scalar_tensor_tensor(y, ps[:, 7, :], col_s[:, L_BO2:L_BO2 + 1], xT_s[:, b * S:(b + 1) * S],
                                               ALU.add, ALU.add).then_inc(x1_out, 1)
                dve.wait_ge(x1_out, b + 1)
                link(nc.vector.tensor_tensor(dif[:, 1:S - 1], y[:, 0:S - 2], y[:, 2:S], ALU.add))
                link(nc.vector.tensor_scalar(dif[:, 0:1], y[:, 1:2], 2.0, None, ALU.mult))
                link(nc.vector.tensor_scalar(dif[:, S - 1:S], y[:, S - 2:S - 1], 2.0, None, ALU.mult))
                link(nc.vector.scalar_tensor_tensor(dif2[:, :], y, -2.0, dif[:, :], ALU.mult, ALU.add))
                link(nc.vector.tensor_scalar(dif2[:, :], dif2[:, :], scal_s[:, 4 + b:5 + b], None, ALU.mult))
                link(nc.vector.tensor_scalar(rea[:, :], y, -1.0, 1.0, ALU.mult, ALU.add))
                link(nc.vector.scalar_tensor_tensor(rea[:, :], y, scal_s[:, 6 + b:7 + b], rea[:, :], ALU.mult, ALU.mult))
                link(nc.vector.tensor_tensor(dif2[:, :], dif2[:, :], rea[:, :], ALU.add))
                dve.wait_ge(lap_done, b + 1)
                if b:
                    dve.wait_ge(up_done, b * NT)
                    dve.wait_ge(gate_done, b)
                nc.vector.scalar_tensor_tensor(duT[:, :], ps[:, 7, :], scal_s[:, 2 + b:3 + b], dif2[:, :],
                                               ALU.mult, ALU.add).then_inc(du_out, 1)
                dve.wait_ge(gate_done, b + 1)
                link(nc.vector.tensor_copy(gl[:, 0, :, :], ps[:, 6, 0:TB * NE].rearrange("p (t e) -> p t e", t=TB)))
                bc = lambda k: gs[:, k, :].unsqueeze(2).broadcast_to([128, TB, NE])
                link(nc.vector.tensor_reduce(gs[:, 0, :], gl[:, 0, :, :], axis=AX.X, op=ALU.max))
                nc.vector.tensor_tensor(gl[:, 1, :, :], gl[:, 0, :, :], bc(0), ALU.subtract).then_inc(gmax_out, 1)
                dve.wait_ge(gexp_out, b + 1)
                link(nc.vector.tensor_reduce(gs[:, 1, :], gl[:, 1, :, :], axis=AX.X, op=ALU.add))
                link(nc.vector.reciprocal(gs[:, 1, :], gs[:, 1, :]))
                link(nc.vector.tensor_tensor(gl[:, 2, :, :], gl[:, 1, :, :], bc(1), ALU.mult))
                rank = cst[:, C_RANK:C_RANK + NE].unsqueeze(1).broadcast_to([128, TB, NE])
                for k in range(2):
                    w, eq, key, hot = gl[:, 2 + 4 * k, :, :], gl[:, 3 + 4 * k, :, :], gl[:, 4 + 4 * k, :, :], gl[:, 5 + 4 * k, :, :]
                    link(nc.vector.tensor_reduce(gs[:, 2 + 2 * k, :], w, axis=AX.X, op=ALU.max))
                    link(nc.vector.tensor_tensor(eq, w, bc(2 + 2 * k), ALU.is_equal))
                    link(nc.vector.tensor_tensor(key, eq, rank, ALU.mult))
                    link(nc.vector.tensor_reduce(gs[:, 3 + 2 * k, :], key, axis=AX.X, op=ALU.max))
                    link(nc.vector.tensor_tensor(hot, key, bc(3 + 2 * k), ALU.is_equal))
                    if k == 0:
                        link(nc.vector.scalar_tensor_tensor(gl[:, 6, :, :], hot, -2.0, w, ALU.mult, ALU.add))
                link(nc.vector.tensor_tensor(gl[:, 10, :, :], gl[:, 5, :, :], gl[:, 9, :, :], ALU.add))
                link(nc.vector.tensor_tensor(gl[:, 10, :, :], gl[:, 10, :, :], gl[:, 2, :, :], ALU.mult))
                link(nc.vector.tensor_tensor(gs[:, 6, :], gs[:, 2, :], gs[:, 4, :], ALU.add))
                link(nc.vector.reciprocal(gs[:, 7, :], gs[:, 6, :]))
                link(nc.vector.tensor_tensor(comb[:, :, :], gl[:, 10, :, :], bc(7), ALU.mult))
                dve.wait_ge(ya_ready, b + 1)
                for t in range(TB):
                    for q in range(2):
                        dve.wait_ge(down_done, (b * TB + t) * 2 + q + 1)
                        for e in range(4):
                            o = nc.vector.scalar_tensor_tensor(
                                ya[:, b, t, :], ps[:, 4 + q, e * 128:(e + 1) * 128],
                                comb[:, t, 4 * q + e:4 * q + e + 1], ya[:, b, t, :], ALU.mult, ALU.add)
                            if e < 3:
                                link(o)
                        o.then_inc(mixed, 1)
                        if q == 0:
                            dve.wait_ge(mixed, (b * TB + t) * 2 + 1)

        @block.tensor
        def _(pe):
            mm = nc.tensor.matmul
            pe.wait_ge(ld_x, 16)
            pe.wait_ge(ld_w1, 64)
            for j in range(B * G1):
                b, g = j // G1, j % G1
                mm(ps[:, j % 8, :], wq1_s[:, g * 128:(g + 1) * 128], xT_s[:, b * S:(b + 1) * S],
                   start=True, stop=True).then_inc(proj1, 1)
            for t in range(B * TB):
                pe.wait_ge(qk1_out, t + 1)
                mm(ps[:, t % 8, :], xT_s[:, t * 128:(t + 1) * 128], wv1_s[:, :], start=True, stop=True).then_inc(proj1, 1)
            pe.wait_ge(cst_ready, 1)
            pe.wait_ge(v1_out, B * TB)
            for q in range(TB):
                if q >= 2:
                    pe.wait_ge(cnt_out, q - 1)
                for j in range(KS):
                    pe.wait_ge(onehot, q * KS + j + 1)
                    mm(ps[:, q % 2, 0:W], ident_b[:, :], oh[:, (q * KS + j) % 4, :], start=(j == 0), stop=(j == KS - 1))\
                        .then_inc(counted, 1)
            for q in range(TB):
                pe.wait_ge(cnt_out, q + 1)
                for k in range(KB):
                    o = nc.tensor.transpose(ps[:, 2 + k, :].bitcast(bf16)[:, q * 128:(q + 1) * 128],
                                            cntN[:, q, k * 128:(k + 1) * 128], ident_b[:, :])
                o.then_inc(cnt_turned, 1)

            pe.wait_ge(bias_out, 1)
            for b in range(B):
                if b:
                    pe.wait_ge(st1, 4 * NQ * b)
                for g in range(G1):
                    if b:
                        pe.wait_ge(max1, NU * b)
                    mm(ps[:, g, 0:W], wk1_s[:, g * 128:(g + 1) * 128], xT_s[:, b * S:b * S + W],
                       start=True, stop=True).then_inc(kproj, 1)
                pe.wait_ge(qb_out, b + 1)
                pe.wait_ge(kmb_out, (b + 1) * G1)
                for u in range(NU):
                    if b * NU + u:
                        pe.wait_ge(max1, b * NU + u)
                    for j in range(4):
                        if KB == 1:
                            mm(ps[:, j, :].rearrange("p (i k) -> p i k", i=4), ident_b[:, :],
                               biasN[:, b, u, :].unsqueeze(1).broadcast_to([128, 4, W]), start=True, stop=False)
                            o = mm(ps[:, j, :], Qb1[:, b, j, u * 128:(u + 1) * 128], Kmb[:, 4 * j:4 * j + 4, :],
                                   start=False, stop=True)
                        else:
                            mm(ps[:, j, :], ident_b[:, :], biasN[:, b, j, :], start=True, stop=False)
                            o = mm(ps[:, j, :], Qb1[:, b, u // 4, j * 128:(j + 1) * 128], Kmb[:, u, :],
                                   start=False, stop=True)
                    o.then_inc(sn1, 1)
                pe.wait_ge(negm1, b + 1)

                def weigh(q):
                    g, k = q // KB, q % KB
                    pe.wait_ge(exp1, (b * NQ + q + 1) * 4)
                    if k == 0 and b * G1 + g:
                        pe.wait_ge(z1_out, b * G1 + g)
                    for i in range(4):
                        h = 4 * g + i
                        c = (b * NQ + q) * 4 + i
                        o = mm(ps[32 * i:32 * i + 32, 6, :], V1[:, b * TB + k, h * PAD:(h + 1) * PAD], P1[:, c % 8, :],
                               start=(k == 0), stop=(k == KB - 1))
                    o.then_inc(pv1, 1)

                for q in range(NQ):
                    g, k = q // KB, q % KB
                    for i in range(4):
                        h = 4 * g + i
                        c = (b * NQ + q) * 4 + i
                        if c >= 2:
                            pe.wait_ge(exp1, c - 1)
                        bank = ps[:, 4 + c % 2, :]
                        mm(bank, ident_r[:, :], biasTh[:, b, k, :], start=True, stop=False)
                        mm(bank, ident_r[:, :], biasTl[:, b, k, :], start=False, stop=False)
                        mm(bank, Km[:, h, k * 128:(k + 1) * 128], Q1[:, b, g, :], start=False, stop=False)
                        for t in range(TB):
                            o = mm(bank[:, t * 128:(t + 1) * 128], negM1[:, t, h:h + 1].to_broadcast([128, 128]),
                                   ident_r[:, :], start=False, stop=(t == TB - 1))
                        o.then_inc(st1, 1)
                    if q:
                        weigh(q - 1)
                weigh(NQ - 1)
                pe.wait_ge(z1_out, (b + 1) * G1)
                if b:
                    pe.wait_ge(xn_out, b)
                for q in range(TB):
                    if q >= 2:
                        pe.wait_ge(norm1, b * TB + q - 1)
                    for g in range(G1):
                        o = nc.tensor.transpose(ps[:, 6 + q % 2, g * 128:(g + 1) * 128],
                                                zT1[:, g, q * 128:(q + 1) * 128], ident)
                    o.then_inc(z1_turned, 1)
                pe.wait_ge(norm1, (b + 1) * TB)
                for q in range(TB):
                    o = nc.tensor.transpose(ps[:, 6, q * 128:(q + 1) * 128], zc[:, q, :], ident)
                o.then_inc(zc_turned, 1)
                pe.wait_ge(zcT_out, b + 1)
                pe.wait_ge(ld_w2, 80)
                for q in range(TB):
                    o = mm(ps[:, 7, q * 128:(q + 1) * 128], zcT[:, q * 128:(q + 1) * 128], wo1_s[:, :],
                           start=True, stop=True)
                o.then_inc(wo1_done, 1)
                pe.wait_ge(xh_out, b + 1)
                for q in range(TB):
                    o = nc.tensor.transpose(ps[:, 6, q * 128:(q + 1) * 128], xh[:, q, :], ident)
                o.then_inc(xh_turned, 1)

            def project(n):
                b, p = n // NP, n % NP
                if n % NP == 0:
                    pe.wait_ge(xn_out, B)
                    if n:
                        pe.wait_ge(mixed, b * TB * 2)
                else:
                    pe.wait_ge(q2_out, n)
                    if p >= 3:
                        pe.wait_ge(sum2_out, n - 2)
                mm(ps[:, 7, :], w_k[:, p * 128:(p + 1) * 128], xnT[:, b * S:(b + 1) * S], start=True, stop=True)\
                    .then_inc(kproj2, 1)

            def project_q(n):
                b, p = n // NP, n % NP
                pe.wait_ge(k2_out, n + 1)
                mm(ps[:, 7, :], w_q[:, p * 128:(p + 1) * 128], xnT[:, b * S:(b + 1) * S], start=True, stop=True)\
                    .then_inc(qproj2, 1)

            def scores_max(h):
                n = h // 2
                pe.wait_ge(qk2b_out, n + 1)
                if h:
                    pe.wait_ge(max2, h)
                for q in range(TB):
                    bank, at = QPOS[q]
                    mm(ps[:, bank, at:at + 128 * (q + 1)], Qmb[:, n % 2, h % 2, q * 128:(q + 1) * 128],
                       KTb[:, n % 2, 0:128 * (q + 1)], start=True, stop=False)
                    o = mm(ps[:, bank, at + 128 * q:at + 128 * (q + 1)], ident_b[:, :], causal_b[:, :],
                           start=False, stop=True)
                o.then_inc(sn2, 1)

            def scores(h):
                n = h // 2
                pe.wait_ge(max2, h + 1)
                if h:
                    pe.wait_ge(exp2, h)
                st = ps[:, 3:6, :].rearrange("p b n -> p (b n)")
                for k in range(TB):
                    a = KOFF[k]
                    mm(st[:, a:a + 128 * (TB - k)], KT[:, n % 2, k * 128:(k + 1) * 128], Qm[:, n % 2, h % 2, k * 128:S],
                       start=True, stop=False)
                    mm(st[:, a:a + 128], ident_r[:, :], causal_r[:, :], start=False, stop=False)
                    for q in range(k, TB):
                        o = mm(st[:, a + 128 * (q - k):a + 128 * (q - k + 1)],
                               negM2[:, q, h:h + 1].to_broadcast([128, 128]), ident_r[:, :],
                               start=False, stop=(q == TB - 1))
                o.then_inc(st2, 1)

            def weigh2(n):
                pe.wait_ge(exp2, 2 * n + 2)
                if n:
                    pe.wait_ge(z2_out, n)
                for k in range(TB):
                    for j in range(2):
                        h = 2 * n + j
                        o = mm(ps[64 * j:64 * j + 64, 6, k * 128:S],
                               V2[:, k, (h % H2) * E2:(h % H2 + 1) * E2],
                               P2[:, h % 4, KOFF[k]:KOFF[k] + 128 * (TB - k)], start=(k == 0), stop=(k == TB - 1))
                o.then_inc(pv2, 1)

            def sum_rows(n):
                pe.wait_ge(acc2, 2 * n + 2)
                pe.wait_ge(q2_out, min(n + 3, (n // NP + 1) * NP))
                if n % NP:
                    pe.wait_ge(sum2_out, n)
                for j in range(2):
                    h = 2 * n + j
                    for c in range(4):
                        r = P2[:, h % 4, 0:128] if c == 0 else acc[:, h % 4, c * 128:(c + 1) * 128]
                        o = mm(ps[32 * c:32 * c + 32, 7, 0:128], ones_band[:, 31 - h % H2:63 - h % H2], r,
                               start=(j == 0), stop=(j == 1))
                o.then_inc(sum2, 1)

            for b in range(B):
                pe.wait_ge(xn_out, B)
                pe.wait_ge(ld_late, 96)
                for t in range(2 * TB):
                    if b and t == 0:
                        pe.wait_ge(mixed, b * TB * 2)
                        pe.wait_ge(silu_out, b * NT)
                    if t >= 6:
                        pe.wait_ge(v2_out, b * 2 * TB + t - 5)
                    mm(ps[:, t % 6, :], xnT[:, b * S + (t // 2) * 128:b * S + (t // 2 + 1) * 128],
                       w_v[:, (t % 2) * 512:(t % 2 + 1) * 512], start=True, stop=True).then_inc(vproj2, 1)
                project(b * NP)
                project_q(b * NP)
                pe.wait_ge(v2_out, (b + 1) * 2 * TB)
                scores_max(2 * b * NP)
                for p in range(NP):
                    n = b * NP + p
                    if p < NP - 1:
                        project(n + 1)
                    scores_max(2 * n + 1)
                    scores(2 * n)
                    if p < NP - 1:
                        project_q(n + 1)
                    if p >= 1:
                        weigh2(n - 1)
                    if p >= 1:
                        sum_rows(n - 1)
                    if p < NP - 1:
                        scores_max(2 * n + 2)
                    scores(2 * n + 1)
                weigh2((b + 1) * NP - 1)
                sum_rows((b + 1) * NP - 1)
                pe.wait_ge(cst_ready, 2)
                pe.wait_ge(rd_out, b + 1)
                for p in range(NP):
                    if p >= 6:
                        pe.wait_ge(zn_out, b * NP + p - 5)
                    mm(ps[:, p % 6, :], sel_r[:, p, :], RDh[:, :, :], start=True, stop=False)
                    mm(ps[:, p % 6, :], sel_r[:, p, :], RDl[:, :, :], start=False, stop=True).then_inc(r2, 1)
                for p in range(NP):
                    pe.wait_ge(zn_out, b * NP + p + 1)
                    o = mm(ps[:, 7, :], w_o[:, p, :], z2[:, p, :], start=(p == 0), stop=(p == NP - 1))
                o.then_inc(wo2_done, 1)
                pe.wait_ge(x1_out, b + 1)
                mm(ps[:, 7, :], lap, x1T[:, b, :], start=True, stop=True).then_inc(lap_done, 1)
                pe.wait_ge(du_out, b + 1)
                for t in range(TB):
                    o = mm(ps[:, 6, t * NE:(t + 1) * NE], duT[:, t * 128:(t + 1) * 128], wg_s[:, :], start=True, stop=True)
                o.then_inc(gate_done, 1)
                for t in range(TB):
                    o = nc.tensor.transpose(ps[:, 7, t * 128:(t + 1) * 128], x1T[:, b, t * 128:(t + 1) * 128], ident)
                o.then_inc(x1_turned, 1)
                for n in range(NT):
                    if n >= 4:
                        pe.wait_ge(silu_out, b * NT + n - 3)
                    mm(ps[:, n % 4, :], w1_s[:, n, :], duT[:, :], start=True, stop=True).then_inc(up_done, 1)
                pe.wait_ge(silu_out, (b + 1) * NT)
                for t in range(TB):
                    for q in range(2):
                        if b * TB + t:
                            pe.wait_ge(mixed, (b * TB + t - 1) * 2 + q + 1)
                        for e in range(4 * q, 4 * q + 4):
                            for k in range(2):
                                o = mm(ps[:, 4 + q, (e % 4) * 128:(e % 4 + 1) * 128],
                                       hT[:, 2 * e + k, t * 128:(t + 1) * 128], w2_s[:, 2 * e + k, :],
                                       start=(k == 0), stop=(k == 1))
                        o.then_inc(down_done, 1)


C_ID = 0
C_BAND = C_ID + 128
C_IOTA = C_BAND + 63
C_RG = C_IOTA + 512
C_HALF = C_RG + 4
C_LAP = C_HALF + 2
C_CAUT = C_LAP + 128
C_CAUN = C_CAUT + 128
C_RANK = C_CAUN + 128
CONSTS = C_RANK + NE

L_BQ1 = 0
L_BK1 = L_BQ1 + G1
L_BQ2 = L_BK1 + H1
L_BK2 = L_BQ2 + 2 * NP
L_BO2 = L_BK2 + NP
L_LNW = L_BO2 + 1
L_LNB = L_LNW + 1
COLS = L_LNB + 1


def kernel(**inputs):
    import numpy as np
    import concourse.bacc as bacc
    from concourse.bass_utils import run_bass_kernel_spmd

    f = {k: np.asarray(v) for k, v in inputs.items()}
    F = np.float32

    def rows(a):
        return np.ascontiguousarray(np.broadcast_to(a.reshape(1, -1), (128, a.size)))

    def padded(wt):
        o = np.zeros((wt.shape[0], H1, PAD), F)
        o[:, :, :E1] = wt.reshape(-1, H1, E1)
        return o.reshape(-1, H1 * PAD)

    cst = np.zeros((128, CONSTS), F)
    r = np.arange(128)
    cst[:, C_ID:C_ID + 128] = np.eye(128)
    cst[:, [C_BAND + 31, C_BAND + 31 + H2]] = 1
    cst[:, C_IOTA:C_IOTA + 512] = np.arange(512)
    cst[r, C_RG + r // 32] = 1
    cst[r, C_HALF + r // 64] = 1
    lap = -2 * np.eye(128) + np.eye(128, k=1) + np.eye(128, k=-1)
    lap[0, 1] = 2
    lap[127, 126] = 2
    cst[:, C_LAP:C_LAP + 128] = lap.T
    cst[:, C_CAUT:C_CAUT + 128] = np.where(r[:, None] > r[None, :], -BIG, 0)
    cst[:, C_CAUN:C_CAUN + 128] = np.where(r[None, :] > r[:, None], -BIG, 0)
    cst[:, C_RANK:C_RANK + NE] = np.arange(NE, 0, -1)
    sel = np.zeros((128, NP, 128), F)
    for p in range(NP):
        for j in range(2):
            sel[2 * p + j::32, p, 64 * j:64 * j + 64] = 1

    cols = np.zeros((128, COLS), F)
    cols[:, L_BQ1:L_BQ1 + G1] = padded(f["L0_cond_bq"].reshape(1, -1)).reshape(G1, 128).T
    bk = padded(f["L0_cond_bk"].reshape(1, -1)).reshape(H1, PAD)
    bq2 = f["L0_attn_b_q"].reshape(NP, 2, E2)
    for h in range(H1):
        cols[PAD * (h % 4):PAD * (h % 4 + 1), L_BK1 + h] = bk[h]
        cols[E2 * (h % 2):E2 * (h % 2 + 1), L_BQ2 + h] = bq2[h // 2, h % 2]
    cols[:, L_BK2:L_BK2 + NP] = f["L0_attn_b_k"].reshape(NP, 128).T
    cols[:, L_BO2] = f["L0_attn_b_o"]
    cols[:, L_LNW] = f["L0_attn_ln_w"]
    cols[:, L_LNB] = f["L0_attn_ln_b"]

    bv1 = padded(f["L0_cond_bv"].reshape(1, -1)).reshape(H1, PAD)
    bv1[:, E1] = 1
    idx = f["itok_Sx32_0_1023"]
    pm = f["mask_SxS_bk0"]

    def blocks(a):
        return np.ascontiguousarray(a.reshape(-1, 128, a.shape[1]).transpose(1, 0, 2).reshape(128, -1))

    def headed(w):
        return np.ascontiguousarray(w.transpose(1, 0, 2).reshape(D, H2 * E2))

    arrays = {
        "xT": np.ascontiguousarray(f["x"].reshape(T, D).T),
        "wq1": padded(f["L0_cond_Wq"].T), "wk1": padded(f["L0_cond_Wk"].T), "wv1": padded(f["L0_cond_Wv"].T),
        "wo1": np.ascontiguousarray(f["L0_cond_Wo"].T),
        "cols": cols, "bv1": rows(bv1), "bo1": rows(f["L0_cond_bo"]),
        "idx": blocks(idx), "imask": blocks(f["mask_Sx32_bk1"]),
        "pmN": blocks(pm), "pmT": blocks(pm.T),
        "scal": rows(np.concatenate([f["condB_uprev"], f["condB_zX"], f["condB_zY"], f["condB_zR"]])),
        "wq2": headed(f["L0_attn_W_q"]), "wk2": headed(f["L0_attn_W_k"]), "wv2": headed(f["L0_attn_W_v"]),
        "wo2": blocks(f["L0_attn_W_o"].reshape(H2 * E2, D)),
        "bv2": rows(f["L0_attn_b_v"]),
        "wg": np.ascontiguousarray(f["L0_ffn_Wg"]),
        "w1": np.ascontiguousarray(f["L0_ffn_W1"].transpose(1, 0, 2).reshape(D, NE * FH)),
        "w2": blocks(f["L0_ffn_W2"].reshape(NE * FH, D)),
        "consts": cst, "sel": sel.reshape(128, -1),
    }
    nc = bacc.Bacc("TRN2", target_bir_lowering=False, num_devices=1)
    args = [nc.dram_tensor(k, a.shape, mybir.dt.from_np(a.dtype), kind="ExternalInput").ap() for k, a in arrays.items()]
    args.append(nc.dram_tensor("out", (B, S, D), mybir.dt.float32, kind="ExternalOutput").ap())
    program(nc, *args)
    r = run_bass_kernel_spmd(nc, [arrays], core_ids=[0])
    return r.results[0]["out"]
```

```python
import concourse.bass as bass
from concourse import mybir
from contextlib import ExitStack

B, S, D = 2, 512, 128
T = B * S
TB = S // 128
H1, E1, KS = 16, 8, 32
H2, E2 = 16, 64
NP = H2 // 2
NE, FH = 8, 256
NT = NE * FH // 128
PAD = 32
G1 = H1 // 4
JH = 8
SCALE1, SCALE2 = E1 ** -0.5, E2 ** -0.5
BIG = 1e30


def program(
    nc: bass.Bass,
    xT: bass.AP, wq1: bass.AP, wk1: bass.AP, wv1: bass.AP, wo1: bass.AP,
    cols: bass.AP, bv1: bass.AP, bo1: bass.AP, idx: bass.AP, imask: bass.AP,
    pmN: bass.AP, pmT: bass.AP, scal: bass.AP,
    wq2: bass.AP, wk2: bass.AP, wv2: bass.AP, wo2: bass.AP,
    wg: bass.AP, w1: bass.AP, w2: bass.AP,
    consts: bass.AP, iota: bass.AP, iotaj: bass.AP, sel: bass.AP,
    out: bass.AP,
):
    f32 = mybir.dt.float32
    f32r = mybir.dt.float32r
    bf16 = mybir.dt.bfloat16
    i32 = mybir.dt.int32
    u8 = mybir.dt.uint8
    ALU = mybir.AluOpType
    ACT = mybir.ActivationFunctionType
    AX = mybir.AxisListType
    f16 = mybir.dt.float16

    ctx = ExitStack()
    with ctx:
        def sb(name, shape, dt=f32):
            return ctx.enter_context(nc.sbuf_tensor(name, shape, dt))

        def sem(name):
            return ctx.enter_context(nc.semaphore(name))

        cst = sb("cst", [128, CONSTS])
        ident = cst[:, C_ID:C_ID + 128]
        ones_band = cst[:, C_BAND:C_BAND + 63]
        row_group = cst[:, C_RG:C_RG + 4]
        head_rows = cst[:, C_HEAD:C_HEAD + 4]
        lap = cst[:, C_LAP:C_LAP + 128]
        iota_s = sb("iota_s", [128, S], f16)
        iota_j = sb("iota_j", [128, 128 * JH], f16)
        ident_r = sb("ident_r", [128, 128], f32r)
        ident_b = sb("ident_b", [128, 128], bf16)
        causal_r = sb("causal_r", [128, 128], f32r)
        sel_r = sb("sel_r", [128, NP, 128], f32r)
        xT_s = sb("xT_s", [128, T])
        w1st = sb("w1st", [128, 3, H1 * PAD])
        wq1_s, wk1_s, wv1_s = w1st[:, 0, :], w1st[:, 1, :], w1st[:, 2, :]
        bv1_s = sb("bv1_s", [128, H1 * PAD])
        wo1_s = sb("wo1_s", [128, D])
        col_s = sb("col_s", [128, COLS])
        bo1_s = sb("bo1_s", [128, D])
        scal_s = sb("scal_s", [128, 8])
        wg_s = sb("wg_s", [128, NE])
        raw = sb("raw", [128, H2 * E2])
        w_hl = sb("w_hl", [128, 2, 3, H2 * E2], f32r)
        w_h, w_l = w_hl[:, 0], w_hl[:, 1]
        xn_h = sb("xn_h", [128, T], f32r)
        xn_l = sb("xn_l", [128, T], f32r)
        stats = sb("stats", [128, TB, 6])
        mv = sb("mv", [128, TB, 2])
        rstd = sb("rstd", [128, 4, TB])
        rec1 = sb("rec1", [128, TB, H1])
        lam = sb("lam", [128, 8])
        path = sb("path", [128, 4])
        path_i = sb("path_i", [1, 1], i32)
        cvec = sb("cvec", [128, 1])
        attn1 = ExitStack()

        def sb1(name, shape, dt=f32):
            return attn1.enter_context(nc.sbuf_tensor(name, shape, dt))

        biasT = sb1("biasT", [128, B * TB * S], f32r)
        zT1 = sb1("zT1", [128, G1, S])
        zc = sb1("zc", [128, TB, 128])
        zcT = sb1("zcT", [128, S])
        xn32 = zcT[:, :]
        y_s = sb1("y_s", [128, TB, D])
        xh = sb1("xh", [128, TB, D])
        idx_s = sb1("idx_s", [128, TB, KS], i32)
        im_s = sb1("im_s", [128, TB, KS], u8)
        idf = sb1("idf", [128, TB, KS])
        idw = sb1("idw", [128, TB, KS])
        idm = sb1("idm", [128, TB, KS])
        idm_h = sb1("idm_h", [128, TB, KS], f16)
        mraw = sb1("mraw", [128, B, TB, H1])
        mtmp = sb1("mtmp", [128, TB, H1])
        negM1 = sb1("negM1", [128, B, TB, H1], f32r)
        Ks = sb1("Ks", [128, 4, S], f32r)
        Q1 = sb1("Q1", [128, B, G1, S], f32r)
        Km_s = sb1("Km_s", [128, H1 * S], f32r)
        V1 = sb1("V1", [128, B * TB, H1 * PAD])
        biasN = sb1("biasN", [128, B * TB * S], bf16)
        biasT_more = w_hl[:, :, :, :].rearrange("p a n m -> p (a n m)")
        P1 = sb1("P1", [128, 8, S])
        oh_s = V1[:, 0:4, :].rearrange("p a b -> p (a b)").bitcast(bf16)
        cnt_s = V1[:, 4:6, :].rearrange("p a b -> p (a b)").bitcast(bf16)
        pm_s = V1[:, 6:7, :].rearrange("p a b -> p (a b)").bitcast(u8)
        pmT_s = V1[:, 7:8, :].rearrange("p a b -> p (a b)").bitcast(u8)
        tmpA, tmpB, tmpC = P1[:, 0:4, :], P1[:, 4:8, :], zT1
        attn1.close()

        attn2 = ExitStack()

        def sb2(name, shape, dt=f32):
            return attn2.enter_context(nc.sbuf_tensor(name, shape, dt))

        z2 = sb2("z2", [128, B, NP, S])
        w_o = sb2("w_o", [128, NP, D])
        w1_s = sb2("w1_s", [128, NT, 128])
        w2_s = sb2("w2_s", [128, NT, D])
        V2 = sb2("V2", [128, TB, H2 * E2])
        KH = sb2("KH", [128, 2, S], f32r)
        KL = sb2("KL", [128, 2, S], f32r)
        negM2 = sb2("negM2", [128, TB, 2 * H2], f32r)
        sums = sb2("sums", [128, B, 128])
        rsum = sb2("rsum", [128, 128])
        acc = sb2("acc", [128, 4, S])
        RDh = sb2("RDh", [128, 4, 128], f32r)
        RDl = sb2("RDl", [128, 4, 128], f32r)
        x1T = sb2("x1T", [128, B, S])
        dif = sb2("dif", [128, S])
        dif2 = sb2("dif2", [128, S])
        rea = sb2("rea", [128, S])
        RDf = rea[:, :].rearrange("p (c q) -> p c q", c=4)
        duT = sb2("duT", [128, B, S])
        gl = sb2("gl", [128, 11, TB, NE])
        gs = sb2("gs", [128, 8, TB])
        comb = sb2("comb", [128, B, TB, NE])
        pairs = attn2.enter_context(ExitStack())
        QH = pairs.enter_context(nc.sbuf_tensor("QH", [128, 2, 2, S], f32r))
        QL = pairs.enter_context(nc.sbuf_tensor("QL", [128, 2, 2, S], f32r))
        P2 = pairs.enter_context(nc.sbuf_tensor("P2", [128, 4, 1280], f32))
        pairs.close()
        hT = sb2("hT", [128, NT, S])
        attn2.close()
        ya = V2[:, 0:B, 0:TB * D].rearrange("p b (t d) -> p b t d", t=TB)

        ps = ctx.enter_context(nc.psum_tensor("ps", [128, 8, 512], f32))

        ld_x = sem("ld_x")
        ld_q1 = sem("ld_q1")
        ld_w1 = sem("ld_w1")
        ld_idx = sem("ld_idx")
        ld_cst = sem("ld_cst")
        ld_iota = sem("ld_iota")
        ld_pm = sem("ld_pm")
        ld_o1 = sem("ld_o1")
        ld_raw = sem("ld_raw")
        ld_late = sem("ld_late")
        stored = sem("stored")
        cst_ready = sem("cst_ready")
        flag_in = sem("flag_in")
        flag_sum = sem("flag_sum")
        flag_ready = sem("flag_ready")
        proj1 = sem("proj1")
        qk_out = sem("qk_out")
        qk_low = sem("qk_low")
        zeroed = sem("zeroed")
        v1_proj = sem("v1_proj")
        v1_out = sem("v1_out")
        onehot = sem("onehot")
        counted = sem("counted")
        cnt_out = sem("cnt_out")
        cnt_turned = sem("cnt_turned")
        ln_in = sem("ln_in")
        ln_out = sem("ln_out")
        lam_out = sem("lam_out")
        biasN_out = sem("biasN_out")
        biasT_out = sem("biasT_out")
        km_out = sem("km_out")
        sn1 = sem("sn1")
        max1 = sem("max1")
        negm1 = sem("negm1")
        st1 = sem("st1")
        exp1 = sem("exp1")
        pv1 = sem("pv1")
        z1_out = sem("z1_out")
        z1_turned = sem("z1_turned")
        norm1 = sem("norm1")
        zc_turned = sem("zc_turned")
        zcT_out = sem("zcT_out")
        wo1_done = sem("wo1_done")
        var_out = sem("var_out")
        rstd_out = sem("rstd_out")
        xh_out = sem("xh_out")
        xh_turned = sem("xh_turned")
        xn_out = sem("xn_out")
        w_split = sem("w_split")
        vproj2 = sem("vproj2")
        v2_out = sem("v2_out")
        kproj2 = sem("kproj2")
        qproj2 = sem("qproj2")
        kh_out = sem("kh_out")
        kl_out = sem("kl_out")
        qh_out = sem("qh_out")
        ql_out = sem("ql_out")
        sn2 = sem("sn2")
        max2 = sem("max2")
        st2 = sem("st2")
        exp2 = sem("exp2")
        acc2 = sem("acc2")
        pv2 = sem("pv2")
        z2_out = sem("z2_out")
        sum2 = sem("sum2")
        sum2_out = sem("sum2_out")
        rd_out = sem("rd_out")
        r2 = sem("r2")
        zn_out = sem("zn_out")
        cvec_done = sem("cvec_done")
        cvec_out = sem("cvec_out")
        wo2_done = sem("wo2_done")
        x1_out = sem("x1_out")
        lap_done = sem("lap_done")
        du_out = sem("du_out")
        gate_done = sem("gate_done")
        gmax_out = sem("gmax_out")
        gexp_out = sem("gexp_out")
        x1_turned = sem("x1_turned")
        ya_ready = sem("ya_ready")
        up_done = sem("up_done")
        silu_out = sem("silu_out")
        down_done = sem("down_done")
        mixed = sem("mixed")
        dve_step = sem("dve_step")
        dve_step_fast = sem("dve_step_fast")
        dve_step_all = sem("dve_step_all")
        act_step = sem("act_step")
        pool_step = sem("pool_step")

        KOFF = [0, 512, 1024, 896]
        QPOS = [(1, 384), (2, 0), (1, 0), (0, 0)]
        mm = nc.tensor.matmul

        class Reach:

            def __init__(self, KB):
                self.KB, self.W = KB, 128 * KB
                self.fast = KB == 1
                self.NQ = G1 * KB
                self.NU = TB if KB == 1 else H1
                W = self.W
                self.J = JH if self.fast else 1
                self.oh = oh_s[:, 0:4 * W * self.J].rearrange("p (r k j) -> p r k j", r=4, j=self.J)
                self.cnt = cnt_s[:, 0:TB * W].rearrange("p (t k) -> p t k", t=TB)
                nb = 1 if self.fast else B
                self.biasN = biasN[:, 0:nb * TB * W].rearrange("p (b t k) -> p b t k", b=nb, t=TB)
                self.biasTh = biasT[:, 0:nb * KB * S].rearrange("p (b k q) -> p b k q", b=nb, k=KB)
                tl = biasT[:, S:2 * S] if self.fast else biasT_more[:, 0:nb * KB * S]
                self.biasTl = tl.rearrange("p (b k q) -> p b k q", b=nb, k=KB)
                nk = B if self.fast else 1
                self.Km = Km_s[:, 0:nk * H1 * W].rearrange("p (b h k) -> p b h k", b=nk, h=H1)
                self.nb, self.nk = nb, nk

        FAST, ALL = Reach(1), Reach(TB)

        block = ctx.enter_context(nc.Block())

        def branch(eng, run):
            eng.wait_ge(flag_ready, 1)
            flag = eng.value_load(path_i[0:1, 0:1])
            with eng.If(flag > 0):
                run(ALL)
            with eng.Else():
                run(FAST)

        @block.sync
        def _(sp):
            sp.dma_start(wq1_s, wq1).then_inc(ld_q1, 16)
            sp.dma_start(xT_s[:, 0:S], xT[:, 0:S]).then_inc(ld_x, 16)
            sp.dma_start(xT_s[:, S:T], xT[:, S:T]).then_inc(ld_x, 16)
            sp.dma_start(wk1_s, wk1).then_inc(ld_w1, 16)
            sp.dma_start(wv1_s, wv1).then_inc(ld_w1, 16)
            sp.dma_start(bv1_s[:, :], bv1).then_inc(ld_w1, 16)
            sp.dma_start(pm_s, pmN).then_inc(ld_pm, 16)
            sp.dma_start(pmT_s, pmT).then_inc(ld_pm, 16)
            sp.dma_start(wo1_s[:, :], wo1).then_inc(ld_o1, 16)
            sp.dma_start(bo1_s[:, :], bo1).then_inc(ld_o1, 16)
            sp.dma_start(wg_s[:, :], wg).then_inc(ld_o1, 16)
            for n, w in enumerate((wv2, wk2, wq2)):
                if n:
                    sp.wait_ge(w_split, n)
                sp.dma_start(raw[:, :], w).then_inc(ld_raw, 16)
            sp.wait_ge(w_split, 3)
            sp.dma_start(raw[:, :].rearrange("p (n m) -> p n m", n=NP), sel.rearrange("p (n m) -> p n m", n=NP))\
                .then_inc(ld_raw, 16)
            sp.wait_ge(z1_out, B * G1)
            sp.dma_start(w_o[:, :, :], wo2.rearrange("p (n m) -> p n m", n=NP)).then_inc(ld_late, 16)
            sp.dma_start(w1_s[:, :, :], w1.rearrange("p (n m) -> p n m", n=NT)).then_inc(ld_late, 16)
            sp.dma_start(w2_s[:, :, :], w2.rearrange("p (n m) -> p n m", n=NT)).then_inc(ld_late, 16)
            for b in range(B):
                for t in range(TB):
                    sp.wait_ge(mixed, (b * TB + t + 1) * 2)
                    sp.dma_start(out[b, t * 128:(t + 1) * 128, :], ya[:, b, t, :]).then_inc(stored, 16)
            sp.wait_ge(stored, 16 * B * TB)

        @block.gpsimd
        def _(pool):
            pool.dma_start(idx_s[:, :, :], idx.rearrange("p (b j) -> p b j", b=TB)).then_inc(ld_idx, 16)
            pool.dma_start(im_s[:, :, :], imask.rearrange("p (b j) -> p b j", b=TB)).then_inc(ld_idx, 16)
            pool.dma_start(iota_j[:, :], iotaj).then_inc(ld_iota, 16)
            pool.dma_start(iota_s[:, :], iota).then_inc(ld_iota, 16)

            def first(r):
                if not r.fast:
                    pool.wait_ge(st1, B * 4 * r.NQ)

            branch(pool, first)
            for n in range(3):
                pool.wait_ge(ld_raw, 16 * (n + 1))
                nc.gpsimd.tensor_copy(w_h[:, n, :], raw[:, :]).then_inc(pool_step, 1)
                pool.wait_ge(pool_step, n + 1)
                nc.gpsimd.tensor_tensor(w_l[:, n, :], raw[:, :], w_h[:, n, :].bitcast(f32), ALU.subtract)\
                    .then_inc(w_split, 1)
            pool.wait_ge(ld_raw, 64)
            nc.gpsimd.tensor_copy(sel_r[:, :, :], raw[:, :].rearrange("p (n m) -> p n m", n=NP)).then_inc(w_split, 1)
            steps = [3]

            def link(ins):
                steps[0] += 1
                ins.then_inc(pool_step, 1)
                pool.wait_ge(pool_step, steps[0])

            def pool_sum(h):
                pool.wait_ge(exp2, h + 1)
                if h >= 4:
                    pool.wait_ge(sum2, (h - 4) // 2 + 1)
                p, a = P2[:, h % 4, :], acc[:, h % 4, :]
                link(nc.gpsimd.tensor_tensor(a[:, 128:512], p[:, 128:512], p[:, KOFF[1]:KOFF[1] + 384], ALU.add))
                link(nc.gpsimd.tensor_tensor(a[:, 256:512], a[:, 256:512], p[:, KOFF[2]:KOFF[2] + 256], ALU.add))
                nc.gpsimd.tensor_tensor(a[:, 384:512], a[:, 384:512], p[:, KOFF[3]:KOFF[3] + 128], ALU.add)\
                    .then_inc(acc2, 1)

            pool.wait_ge(z1_out, B * G1)
            pool.wait_ge(w_split, 4)
            for i, (part, j) in enumerate(((QH, 0), (QL, 0), (QH, 1), (QL, 1))):
                if i == 2:
                    pool.wait_ge(zeroed, 2)
                nc.gpsimd.memset(part[64 - 64 * j:128 - 64 * j, :, j, :].bitcast(f32), 0.0).then_inc(zeroed, 1)
            pool.wait_ge(zeroed, 4)
            for h in range(B * H2):
                pool_sum(h)

        @block.scalar
        def _(act):
            act.dma_start(col_s[:, :], cols).then_inc(ld_cst, 16)
            act.dma_start(scal_s[:, :], scal).then_inc(ld_cst, 16)
            act.dma_start(cst[:, :], consts).then_inc(ld_cst, 16)
            nc.scalar.preload_act_table_set("natural_log_exp_and_others")
            act.wait_ge(ld_cst, 48)
            nc.scalar.activation(lam[:, 0:B], scal_s[:, 0:B], ACT.Exp, scale=-5.0).then_inc(lam_out, 1)

            def z_out(r, b, g):
                act.wait_ge(pv1, b * r.NQ + (g + 1) * r.KB)
                if b:
                    act.wait_ge(z1_turned, b * TB)
                nc.scalar.activation(zT1[:, g, :], ps[:, 6, :], ACT.Copy).then_inc(z1_out, 1)

            def tail_a(b):
                act.wait_ge(zc_turned, b + 1)
                nc.scalar.activation(zcT[:, :], ps[:, 0, :], ACT.Copy).then_inc(zcT_out, 1)

            def tail_b(b):
                act.wait_ge(var_out, b + 1)
                nc.scalar.activation(rstd[:, 1, :], rstd[:, 0, :], ACT.Ln).then_inc(act_step, 1)
                act.wait_ge(act_step, b + 1)
                nc.scalar.activation(rstd[:, 1, :], rstd[:, 1, :], ACT.Exp, scale=-0.5).then_inc(rstd_out, 1)

            def qk_whole(to, j, n, col):
                act.wait_ge(proj1, j + 1)
                nc.scalar.activation(to, ps[:, j if j < B * G1 else G1 + j % G1, 0:n], ACT.Identity,
                                     bias=col_s[:, col:col + 1]).then_inc(qk_out, 1)

            for j in range(B * G1):
                qk_whole(Q1[:, j // G1, j % G1, :], j, S, L_BQ1 + j % G1)

            def keys(r, b):
                if b:
                    act.wait_ge(km_out, G1)
                for g in range(G1):
                    qk_whole(Ks[:, g, 0:r.W], B * G1 + b * G1 + g, r.W, L_BK1 + g)

            def alone(r, b):
                for g in range(G1):
                    act.wait_ge(qk_low, B * G1 + b * G1 + g + 1)
                    for i in range(4):
                        o = nc.scalar.activation(r.Km[:, b % r.nk, 4 * g + i, :], Ks[:, g, 0:r.W].bitcast(f32), ACT.Copy,
                                                 scale=head_rows[:, i:i + 1])
                    o.then_inc(km_out, 1)

            def first(r):
                for q in range(TB):
                    if q >= B:
                        keys(r, q - B)
                        if q == B or r.fast:
                            alone(r, q - B)
                    if r.fast:
                        act.wait_ge(ln_in, q + 1)
                        nc.scalar.activation(tmpA[:, q, 0:r.W], tmpA[:, q, 0:r.W], ACT.Ln).then_inc(ln_out, 1)
                if not r.fast:
                    act.wait_ge(ln_in, 1)
                    nc.scalar.activation(tmpA[:, :, :], tmpA[:, :, :], ACT.Ln).then_inc(ln_out, 1)
                k = TB if r.fast else 1
                act.wait_ge(ln_in, k + 1)
                nc.scalar.activation(tmpC[:, 0:r.KB, :], tmpC[:, 0:r.KB, :], ACT.Ln).then_inc(ln_out, 1)
                for b in range(B):
                    if b and not r.fast:
                        alone(r, b)
                    for n in range(4 * r.NQ):
                        c = b * 4 * r.NQ + n
                        act.wait_ge(st1, c + 1)
                        if c >= 8:
                            act.wait_ge(pv1, c // 4 - 1)
                        nc.scalar.activation(P1[:, c % 8, :], ps[:, 4 + c % 2, :], ACT.Exp, scale=SCALE1)\
                            .then_inc(exp1, 1)
                        q = c // 4 - 1
                        if n % 4 == 1 and q >= 0 and q % r.KB == r.KB - 1:
                            z_out(r, q // r.NQ, q % r.NQ // r.KB)
                        if b and n == 8 * r.KB:
                            tail_a(0)
                        if b and n == 12 * r.KB:
                            tail_b(0)
                z_out(r, B - 1, G1 - 1)

            branch(act, first)
            tail_a(1)

            def keys_out(n):
                act.wait_ge(kproj2, n + 1)
                if n >= 2:
                    act.wait_ge(st2, 2 * (n - 1))
                p = n % NP
                nc.scalar.activation(KH[:, n % 2, :], ps[:, 7, :], ACT.Identity, bias=col_s[:, L_BK2 + p:L_BK2 + p + 1])\
                    .then_inc(kh_out, 1)

            def queries_out(n):
                act.wait_ge(qproj2, n + 1)
                p = n % NP
                for j in range(2):
                    rows = slice(64 * j, 64 * j + 64)
                    o = nc.scalar.activation(QH[rows, n % 2, j, :], ps[rows, 7, :], ACT.Identity,
                                             bias=col_s[rows, L_BQ2 + p:L_BQ2 + p + 1])
                o.then_inc(qh_out, 1)

            def exp(h):
                act.wait_ge(st2, h + 1)
                if h >= 4:
                    act.wait_ge(pv2, (h - 4) // 2 + 1)
                    act.wait_ge(acc2, h - 3)
                    act.wait_ge(sum2, (h - 4) // 2 + 1)
                nc.scalar.activation(P2[:, h % 4, :], ps[:, 3:6, :].rearrange("p b n -> p (b n)")[:, 0:1280],
                                     ACT.Exp, scale=SCALE2).then_inc(exp2, 1)

            def z2_copy(n):
                act.wait_ge(pv2, n + 1)
                nc.scalar.activation(z2[:, n // NP, n % NP, :], ps[:, 6, :], ACT.Copy).then_inc(z2_out, 1)

            for b in range(B):
                for t in range(2 * TB):
                    act.wait_ge(vproj2, b * 2 * TB + t + 1)
                    if b and t == 0:
                        act.wait_ge(pv2, b * NP)
                    nc.scalar.activation(V2[:, t // 2, (t % 2) * 512:(t % 2 + 1) * 512], ps[:, vbank(b, t), :], ACT.Copy)\
                        .then_inc(v2_out, 1)
                if b == 0:
                    tail_b(1)
                keys_out(b * NP)
                queries_out(b * NP)
                for n in range(b * NP, (b + 1) * NP):
                    p = n % NP
                    if p < NP - 1:
                        keys_out(n + 1)
                    exp(2 * n)
                    if p < NP - 1:
                        queries_out(n + 1)
                    if p:
                        z2_copy(n - 1)
                    exp(2 * n + 1)
                z2_copy(n)

            def gate_exp(b):
                act.wait_ge(gmax_out, b + 1)
                nc.scalar.activation(gl[:, 1, :, :], gl[:, 1, :, :], ACT.Exp).then_inc(gexp_out, 1)

            def residual(b):
                act.wait_ge(x1_turned, b + 1)
                nc.scalar.activation(ya[:, b, :, :], ps[:, 7, :].rearrange("p (t d) -> p t d", t=TB), ACT.Copy)\
                    .then_inc(ya_ready, 1)

            def silu(b, n):
                act.wait_ge(up_done, b * NT + n + 1)
                if b and n == 0:
                    act.wait_ge(down_done, b * TB * 2)
                nc.scalar.activation(hT[:, n, :], ps[:, n % 4, :], ACT.Silu).then_inc(silu_out, 1)

            gate_exp(0)
            residual(0)
            for n in range(NT):
                silu(0, n)
            gate_exp(1)
            residual(1)
            for n in range(NT):
                silu(1, n)

        @block.vector
        def _(dve):
            steps = {dve_step: 0, dve_step_fast: 0, dve_step_all: 0}
            now = [dve_step]

            def link(ins):
                steps[now[0]] += 1
                ins.then_inc(now[0], 1)
                dve.wait_ge(now[0], steps[now[0]])

            dve.wait_ge(ld_idx, 32)
            link(nc.vector.tensor_copy(idf[:, :, :], idx_s[:, :, :]))
            link(nc.vector.tensor_scalar(idw[:, :, :], idf[:, :, :], 0.0, float(S), ALU.is_lt, ALU.mult))
            link(nc.vector.tensor_tensor(idf[:, :, :], idf[:, :, :], idw[:, :, :], ALU.add))
            link(nc.vector.tensor_scalar(idf[:, :, :], idf[:, :, :], 0.0, float(S - 1), ALU.max, ALU.min))
            link(nc.vector.tensor_copy(idw[:, :, :], im_s[:, :, :]))
            link(nc.vector.scalar_tensor_tensor(idm[:, :, :], idf[:, :, :], 1.0, idw[:, :, :], ALU.add, ALU.mult))
            link(nc.vector.tensor_scalar(idm[:, :, :], idm[:, :, :], 1.0, None, ALU.subtract))
            nc.vector.tensor_copy(idm_h[:, :, :], idm[:, :, :])
            link(nc.vector.tensor_reduce(path[:, 0:1], idm[:, :, :], axis=AX.XY, op=ALU.max))
            link(nc.vector.tensor_scalar(path[:, 0:1], path[:, 0:1], 128.0, None, ALU.is_ge))
            dve.wait_ge(lam_out, 1)
            link(nc.vector.tensor_scalar(lam[:, 2:4], lam[:, 0:2], 10.0, None, ALU.mult))
            link(nc.vector.tensor_scalar(lam[:, 4:6], lam[:, 2:4], 1.0, None, ALU.is_ge))
            link(nc.vector.tensor_scalar(lam[:, 2:4], lam[:, 2:4], 1.0, 1.0 / SCALE1, ALU.min, ALU.mult))
            link(nc.vector.tensor_scalar(lam[:, 6:8], lam[:, 4:6], -1.0, 1.0, ALU.mult, ALU.add))
            link(nc.vector.tensor_copy(path[:, 1:3], lam[:, 6:8]))
            nc.vector.tensor_reduce(path[:, 3:4], path[:, 0:3], axis=AX.X, op=ALU.add).then_inc(flag_in, 1)
            link(nc.vector.tensor_tensor(lam[:, 6:8], lam[:, 6:8], lam[:, 2:4], ALU.mult))
            nc.vector.tensor_copy(ident_r[:, :], ident)
            nc.vector.tensor_copy(causal_r[:, :], cst[:, C_CAUT:C_CAUT + 128])
            nc.vector.tensor_copy(ident_b[:, :], ident).then_inc(cst_ready, 1)
            dve.wait_ge(flag_sum, 1)
            nc.vector.tensor_copy(path_i[:, :], ps[0:1, 7, 0:1]).then_inc(flag_ready, 1)

            def normalise(b):
                for q in range(TB):
                    dve.wait_ge(z1_turned, b * TB + q + 1)
                    z = ps[:, q, :].rearrange("p (h c) -> p h c", c=PAD)
                    link(nc.vector.reciprocal(rec1[:, q, :], z[:, :, E1]))
                    nc.vector.tensor_tensor(zc[:, q, :].rearrange("p (h c) -> p h c", c=E1), z[:, :, 0:E1],
                                            rec1[:, q, :].unsqueeze(2).broadcast_to([128, H1, E1]), ALU.mult)\
                        .then_inc(norm1, 1)

            def moments(b):
                dve.wait_ge(wo1_done, b + 1)
                dve.wait_ge(ld_o1, 48)
                link(nc.vector.tensor_tensor(y_s[:, :, :], ps[:, 1, :].rearrange("p (t d) -> p t d", t=TB),
                                             bo1_s[:, :].unsqueeze(1).broadcast_to([128, TB, D]), ALU.add))
                for t in range(TB):
                    link(nc.vector.bn_stats(stats[:, t, :], y_s[:, t, :]))
                for t in range(TB):
                    o = nc.vector.bn_aggr(mv[:, t, :], stats[:, t, :])
                    if t == TB - 1:
                        link(o)
                nc.vector.tensor_scalar(rstd[:, 0, :], mv[:, :, 1], 1e-5, None, ALU.add).then_inc(var_out, 1)

            def standardise(b):
                dve.wait_ge(rstd_out, b + 1)
                link(nc.vector.tensor_tensor(rstd[:, 2, :], rstd[:, 1, :], rstd[:, 1, :], ALU.mult))
                link(nc.vector.tensor_tensor(rstd[:, 2, :], rstd[:, 2, :], rstd[:, 0, :], ALU.mult))
                link(nc.vector.tensor_scalar(rstd[:, 2, :], rstd[:, 2, :], -0.5, 1.5, ALU.mult, ALU.add))
                link(nc.vector.tensor_tensor(rstd[:, 3, :], rstd[:, 2, :], rstd[:, 1, :], ALU.mult))
                for t in range(TB):
                    o = nc.vector.tensor_scalar(xh[:, t, :], y_s[:, t, :], mv[:, t, 0:1], rstd[:, 3, t:t + 1],
                                                ALU.subtract, ALU.mult)
                o.then_inc(xh_out, 1)

            def xn_split(b, bank):
                dve.wait_ge(xh_turned, b + 1)
                link(nc.vector.tensor_scalar(xn32, ps[:, bank, :], col_s[:, L_LNW:L_LNW + 1],
                                             col_s[:, L_LNB:L_LNB + 1], ALU.mult, ALU.add))
                link(nc.vector.tensor_copy(xn_h[:, b * S:(b + 1) * S], xn32))
                nc.vector.tensor_tensor(xn_l[:, b * S:(b + 1) * S], xn32, xn_h[:, b * S:(b + 1) * S].bitcast(f32),
                                        ALU.subtract).then_inc(xn_out, 1)

            def first(r):
                KB, W, NU, NQ = r.KB, r.W, r.NU, r.NQ
                now[0] = dve_step_fast if r.fast else dve_step_all

                def onehots(q):
                    for j in range(KS // r.J):
                        n = q * (KS // r.J) + j
                        if n >= 4:
                            dve.wait_ge(counted, (n - 3) * r.J)
                        if r.fast:
                            o = nc.vector.tensor_tensor(
                                r.oh[:, n % 4, :, :], iota_j[:, :].rearrange("p (k j) -> p k j", j=JH),
                                idm_h[:, q, j * JH:(j + 1) * JH].unsqueeze(1).broadcast_to([128, W, JH]), ALU.is_equal)
                        else:
                            o = nc.vector.tensor_scalar(r.oh[:, n % 4, :, 0], iota_s[:, 0:W], idm[:, q, j:j + 1], None,
                                                        ALU.is_equal)
                        o.then_inc(onehot, 1)

                def cnt_copy(q):
                    dve.wait_ge(counted, (q + 1) * KS)
                    nc.vector.tensor_copy(r.cnt[:, q, :], ps[:, q, 0:W]).then_inc(cnt_out, 1)
                    dve.wait_ge(cnt_out, q + 1)

                def log_in(a, cnt, c):
                    link(nc.vector.tensor_scalar(c, cnt, 0.5, -BIG, ALU.is_lt, ALU.mult))
                    nc.vector.tensor_scalar(a, cnt, 1.0, None, ALU.max).then_inc(ln_in, 1)

                def bias_n(q):
                    dve.wait_ge(ln_out, q + 1)
                    nc.vector.scalar_tensor_tensor(r.biasN[:, 0, q, :], tmpA[:, q, 0:W], 1.0 / SCALE1, tmpB[:, q, 0:W],
                                                   ALU.mult, ALU.add).then_inc(biasN_out, 1)

                dve.wait_ge(ld_iota, 32)
                if r.fast:
                    for q in range(TB):
                        onehots(q)
                        splits(r, q)
                        if q:
                            bias_n(q - 1)
                        cnt_copy(q)
                        log_in(tmpA[:, q, 0:W], r.cnt[:, q, :], tmpB[:, q, 0:W])
                    bias_n(TB - 1)
                else:
                    for q in range(B):
                        splits(r, q)
                    for q in range(TB):
                        onehots(q)
                        cnt_copy(q)
                        if q >= B:
                            splits(r, q)
                    log_in(tmpA, r.cnt, tmpB)
                    dve.wait_ge(ln_out, 1)
                    link(nc.vector.scalar_tensor_tensor(tmpB, tmpA, 1.0 / SCALE1, tmpB, ALU.mult, ALU.add))
                    dve.wait_ge(ld_pm, 32)
                    pm = pm_s.rearrange("p (t k) -> p t k", t=TB)
                    for b in range(B):
                        link(nc.vector.tensor_scalar(tmpA, pm, 1.0, lam[:, 6 + b:7 + b], ALU.subtract, ALU.mult))
                        link(nc.vector.scalar_tensor_tensor(r.biasN[:, b, :, :], tmpB, lam[:, 4 + b:5 + b], tmpA,
                                                            ALU.mult, ALU.add))
                    dve.wait_ge(cnt_turned, TB)
                dve.wait_ge(cnt_turned, TB)
                A, Bt, Cc = tmpC[:, 0:KB, :], tmpB[:, 0:KB, :], tmpA[:, 0:KB, :]
                if r.fast:
                    dve.wait_ge(biasN_out, TB)
                log_in(A, ps[:, 4:4 + KB, :].bitcast(bf16)[:, :, 0:512], Bt)
                dve.wait_ge(ln_out, (TB if r.fast else 1) + 1)
                link(nc.vector.scalar_tensor_tensor(Bt, A, 1.0 / SCALE1, Bt, ALU.mult, ALU.add))
                pm = pmT_s.rearrange("p (t k) -> p t k", t=TB)
                for b in range(r.nb):
                    if not r.fast:
                        link(nc.vector.tensor_scalar(A, pm, 1.0, lam[:, 6 + b:7 + b], ALU.subtract, ALU.mult))
                        link(nc.vector.scalar_tensor_tensor(Cc, Bt, lam[:, 4 + b:5 + b], A, ALU.mult, ALU.add))
                    whole = Bt if r.fast else Cc
                    link(nc.vector.tensor_copy(r.biasTh[:, b, :, :], whole))
                    o = nc.vector.tensor_tensor(r.biasTl[:, b, :, :], whole, r.biasTh[:, b, :, :].bitcast(f32),
                                                ALU.subtract)
                    if b < r.nb - 1:
                        link(o)
                o.then_inc(biasT_out, 1)

                def maxima(b, u):
                    dve.wait_ge(sn1, b * NU + u + 1)
                    k = 4 * (u % 2) if (r.fast and b == 0) else 0
                    if r.fast:
                        o = nc.vector.tensor_reduce(mraw[:, b, u, :],
                                                    ps[:, k:k + 4, :].rearrange("p g (i k) -> p g i k", i=4),
                                                    axis=AX.X, op=ALU.max, negate=True)
                    else:
                        o = nc.vector.tensor_reduce(mraw[:, b, :, u], ps[:, 0:4, :], axis=AX.X, op=ALU.max, negate=True)
                    o.then_inc(max1, 1)

                def negate(b):
                    dve.wait_ge(max1, (b + 1) * NU)
                    link(nc.vector.tensor_scalar(mtmp[:, :, :], mraw[:, b, :, :], BIG, None, ALU.mult))
                    link(nc.vector.tensor_tensor(mtmp[:, :, :], mtmp[:, :, :], mtmp[:, :, :], ALU.subtract))
                    nc.vector.tensor_tensor(negM1[:, b, :, :], mraw[:, b, :, :], mtmp[:, :, :], ALU.add)\
                        .then_inc(negm1, 1)

                def values(b):
                    dve.wait_ge(ld_pm, 32)
                    for k in range(KB):
                        n = b * KB + k
                        dve.wait_ge(v1_proj, n + 1)
                        nc.vector.tensor_tensor(V1[:, b * TB + k, :], ps[:, n % 4, :], bv1_s[:, :], ALU.add)\
                            .then_inc(v1_out, 1)

                for u in range(NU):
                    maxima(0, u)
                negate(0)
                values(0)
                values(1)
                for u in range(NU):
                    maxima(1, u)
                negate(1)
                normalise(0)
                moments(0)
                standardise(0)
                xn_split(0, 2)
                now[0] = dve_step

            def splits(r, q):
                for g in range(G1):
                    j = q * G1 + g
                    dve.wait_ge(qk_out, j + 1)
                    if q < B:
                        parts, to, n, col = ((64, 128),), Q1[:, q, g, :], S, L_BQ1
                    else:
                        parts, to, n, col = ((32, 64), (64, 96)), Ks[:, g, 0:r.W], r.W, L_BK1
                    bank = ps[:, j if q < B else G1 + g, 0:n]
                    for i, e in parts:
                        o = nc.vector.scalar_tensor_tensor(to[i:e], bank[i:e], col_s[i:e, col + g:col + g + 1],
                                                           to[i:e].bitcast(f32), ALU.add, ALU.subtract)
                    o.then_inc(qk_low, 1)

            branch(dve, first)
            normalise(1)
            moments(1)
            standardise(1)

            def keys_low(n):
                p = n % NP
                dve.wait_ge(kh_out, n + 1)
                nc.vector.scalar_tensor_tensor(KL[:, n % 2, :], ps[:, 7, :], col_s[:, L_BK2 + p:L_BK2 + p + 1],
                                               KH[:, n % 2, :].bitcast(f32), ALU.add, ALU.subtract).then_inc(kl_out, 1)

            def queries_low(n):
                p = n % NP
                dve.wait_ge(qh_out, n + 1)
                for j in range(2):
                    rows = slice(64 * j, 64 * j + 64)
                    o = nc.vector.scalar_tensor_tensor(QL[rows, n % 2, j, :], ps[rows, 7, :],
                                                       col_s[rows, L_BQ2 + p:L_BQ2 + p + 1],
                                                       QH[rows, n % 2, j, :].bitcast(f32), ALU.add, ALU.subtract)
                o.then_inc(ql_out, 1)

            def maxima2(h):
                dve.wait_ge(sn2, h + 1)
                for q in range(TB):
                    bank, at = QPOS[q]
                    o = nc.vector.tensor_reduce(negM2[:, q, h:h + 1], ps[:, bank, at:at + 128 * (q + 1)],
                                                axis=AX.X, op=ALU.max, negate=True)
                o.then_inc(max2, 1)

            def sums_out(n):
                dve.wait_ge(sum2, n + 1)
                b = n // NP
                if n % NP == 0:
                    o = nc.vector.tensor_copy(sums[:, b, :], ps[:, 7, 0:128])
                else:
                    dve.wait_ge(sum2_out, n)
                    o = nc.vector.tensor_tensor(sums[:, b, :], sums[:, b, :], ps[:, 7, 0:128], ALU.add)
                o.then_inc(sum2_out, 1)

            def reciprocals(b):
                dve.wait_ge(sum2_out, (b + 1) * NP)
                if b:
                    dve.wait_ge(r2, b * NP)
                link(nc.vector.reciprocal(rsum[:, :], sums[:, b, :]))
                for c in range(4):
                    o = nc.vector.tensor_scalar(RDf[:, c, :], rsum[:, :], row_group[:, c:c + 1], None, ALU.mult)
                link(o)
                link(nc.vector.tensor_copy(RDh[:, :, :], RDf[:, :, :]))
                nc.vector.tensor_tensor(RDl[:, :, :], RDf[:, :, :], RDh[:, :, :].bitcast(f32), ALU.subtract)\
                    .then_inc(rd_out, 1)

            def scaled(b, p, bank):
                dve.wait_ge(r2, b * NP + p + 1)
                dve.wait_ge(z2_out, b * NP + p + 1)
                nc.vector.tensor_tensor(z2[:, b, p, :], ps[:, bank, :], z2[:, b, p, :], ALU.mult).then_inc(zn_out, 1)

            def diffuse(b):
                y = x1T[:, b, :]
                dve.wait_ge(wo2_done, b + 1)
                nc.vector.scalar_tensor_tensor(y, ps[:, 7, :], cvec[:, 0:1], xT_s[:, b * S:(b + 1) * S],
                                               ALU.add, ALU.add).then_inc(x1_out, 1)
                dve.wait_ge(x1_out, b + 1)
                nc.vector.tensor_tensor(dif[:, 1:S - 1], y[:, 0:S - 2], y[:, 2:S], ALU.add)
                nc.vector.tensor_scalar(dif[:, 0:1], y[:, 1:2], 2.0, None, ALU.mult)
                link(nc.vector.tensor_scalar(dif[:, S - 1:S], y[:, S - 2:S - 1], 2.0, None, ALU.mult))
                link(nc.vector.scalar_tensor_tensor(dif2[:, :], y, -2.0, dif[:, :], ALU.mult, ALU.add))
                link(nc.vector.tensor_scalar(rea[:, :], y, -1.0, 1.0, ALU.mult, ALU.add))
                link(nc.vector.scalar_tensor_tensor(rea[:, :], y, scal_s[:, 6 + b:7 + b], rea[:, :], ALU.mult, ALU.mult))
                link(nc.vector.scalar_tensor_tensor(dif2[:, :], dif2[:, :], scal_s[:, 4 + b:5 + b], rea[:, :],
                                                    ALU.mult, ALU.add))
                dve.wait_ge(lap_done, b + 1)
                nc.vector.scalar_tensor_tensor(duT[:, b, :], ps[:, 7, :], scal_s[:, 2 + b:3 + b], dif2[:, :],
                                               ALU.mult, ALU.add).then_inc(du_out, 1)

            bc = lambda k: gs[:, k, :].unsqueeze(2).broadcast_to([128, TB, NE])

            def gates(b):
                dve.wait_ge(gate_done, b + 1)
                link(nc.vector.tensor_copy(gl[:, 0, :, :], ps[:, 6, 0:TB * NE].rearrange("p (t e) -> p t e", t=TB)))
                link(nc.vector.tensor_reduce(gs[:, 0, :], gl[:, 0, :, :], axis=AX.X, op=ALU.max))
                nc.vector.tensor_tensor(gl[:, 1, :, :], gl[:, 0, :, :], bc(0), ALU.subtract).then_inc(gmax_out, 1)
                dve.wait_ge(gexp_out, b + 1)
                link(nc.vector.tensor_reduce(gs[:, 1, :], gl[:, 1, :, :], axis=AX.X, op=ALU.add))
                link(nc.vector.reciprocal(gs[:, 1, :], gs[:, 1, :]))
                link(nc.vector.tensor_tensor(gl[:, 2, :, :], gl[:, 1, :, :], bc(1), ALU.mult))
                rank = cst[:, C_RANK:C_RANK + NE].unsqueeze(1).broadcast_to([128, TB, NE])
                for k in range(2):
                    w, eq, key, hot = gl[:, 2 + 4 * k, :, :], gl[:, 3 + 4 * k, :, :], gl[:, 4 + 4 * k, :, :], gl[:, 5 + 4 * k, :, :]
                    link(nc.vector.tensor_reduce(gs[:, 2 + 2 * k, :], w, axis=AX.X, op=ALU.max))
                    link(nc.vector.tensor_tensor(eq, w, bc(2 + 2 * k), ALU.is_equal))
                    link(nc.vector.tensor_tensor(key, eq, rank, ALU.mult))
                    link(nc.vector.tensor_reduce(gs[:, 3 + 2 * k, :], key, axis=AX.X, op=ALU.max))
                    link(nc.vector.tensor_tensor(hot, key, bc(3 + 2 * k), ALU.is_equal))
                    if k == 0:
                        link(nc.vector.scalar_tensor_tensor(gl[:, 6, :, :], hot, -2.0, w, ALU.mult, ALU.add))
                link(nc.vector.tensor_tensor(gl[:, 10, :, :], gl[:, 5, :, :], gl[:, 9, :, :], ALU.add))
                link(nc.vector.tensor_tensor(gl[:, 10, :, :], gl[:, 10, :, :], gl[:, 2, :, :], ALU.mult))
                link(nc.vector.tensor_tensor(gs[:, 6, :], gs[:, 2, :], gs[:, 4, :], ALU.add))
                link(nc.vector.reciprocal(gs[:, 7, :], gs[:, 6, :]))
                link(nc.vector.tensor_tensor(comb[:, b, :, :], gl[:, 10, :, :], bc(7), ALU.mult))

            def mix(b):
                dve.wait_ge(ya_ready, b + 1)
                for t in range(TB):
                    for q in range(2):
                        dve.wait_ge(down_done, (b * TB + t) * 2 + q + 1)
                        for e in range(4):
                            o = nc.vector.scalar_tensor_tensor(
                                ya[:, b, t, :], ps[:, 4 + q, e * 128:(e + 1) * 128],
                                comb[:, b, t, 4 * q + e:4 * q + e + 1], ya[:, b, t, :], ALU.mult, ALU.add)
                            if e < 3:
                                link(o)
                        o.then_inc(mixed, 1)
                        if q == 0:
                            dve.wait_ge(mixed, (b * TB + t) * 2 + 1)

            for b in range(B):
                keys_low(b * NP)
                queries_low(b * NP)
                maxima2(2 * b * NP)
                if b:
                    reciprocals(0)
                for n in range(b * NP, (b + 1) * NP):
                    p = n % NP
                    if p < NP - 1:
                        keys_low(n + 1)
                    maxima2(2 * n + 1)
                    if p < NP - 1:
                        queries_low(n + 1)
                    if n == 0:
                        xn_split(1, 6)
                    if n == 1:
                        dve.wait_ge(cvec_done, 1)
                        nc.vector.tensor_scalar(cvec[:, :], ps[:, 7, 0:1], col_s[:, L_BO2:L_BO2 + 1], None, ALU.add)\
                            .then_inc(cvec_out, 1)
                    if p:
                        sums_out(n - 1)
                    if b:
                        scaled(0, p, 7)
                    if p < NP - 1:
                        maxima2(2 * n + 2)
                sums_out(n)
            reciprocals(1)
            diffuse(0)
            gates(0)
            for p in range(NP):
                scaled(1, p, p % 4)
            diffuse(1)
            mix(0)
            gates(1)
            mix(1)

        @block.tensor
        def _(pe):
            pe.wait_ge(ld_q1, 16)
            for j in range(B * G1):
                b, g = j // G1, j % G1
                if g == 0:
                    pe.wait_ge(ld_x, 16 * B)
                if j == G1:
                    pe.wait_ge(flag_in, 1)
                    mm(ps[0:1, 7, 0:1], path[:, 3:4], ones_band[:, 31:32], start=True, stop=True).then_inc(flag_sum, 1)
                if j == B * G1 - 1:
                    pe.wait_ge(flag_ready, 1)
                mm(ps[:, j % 8, :], wq1_s[:, g * 128:(g + 1) * 128], xT_s[:, b * S:(b + 1) * S],
                   start=True, stop=True).then_inc(proj1, 1)

            def turn_z(b):
                pe.wait_ge(z1_out, (b + 1) * G1)
                for q in range(TB):
                    for g in range(G1):
                        o = nc.tensor.transpose(ps[:, q, g * 128:(g + 1) * 128],
                                                zT1[:, g, q * 128:(q + 1) * 128], ident)
                    o.then_inc(z1_turned, 1)

            def turn_zc(b):
                pe.wait_ge(norm1, (b + 1) * TB)
                for q in range(TB):
                    o = nc.tensor.transpose(ps[:, 0, q * 128:(q + 1) * 128], zc[:, q, :], ident)
                o.then_inc(zc_turned, 1)

            def project_out1(b):
                pe.wait_ge(zcT_out, b + 1)
                pe.wait_ge(ld_o1, 48)
                for q in range(TB):
                    o = mm(ps[:, 1, q * 128:(q + 1) * 128], zcT[:, q * 128:(q + 1) * 128], wo1_s[:, :],
                           start=True, stop=True)
                o.then_inc(wo1_done, 1)

            def turn_xh(b, bank):
                pe.wait_ge(xh_out, b + 1)
                for q in range(TB):
                    o = nc.tensor.transpose(ps[:, bank, q * 128:(q + 1) * 128], xh[:, q, :], ident)
                o.then_inc(xh_turned, 1)

            def first(r):
                KB, W, NU, NQ = r.KB, r.W, r.NU, r.NQ
                def project_keys(b):
                    for g in range(G1):
                        pe.wait_ge(qk_low, G1 + b * G1 + g + 1)
                        mm(ps[:, 4 + g, 0:W], wk1_s[:, g * 128:(g + 1) * 128], xT_s[:, b * S:b * S + W],
                           start=True, stop=True).then_inc(proj1, 1)

                pe.wait_ge(cst_ready, 1)
                for q in range(TB):
                    pe.wait_ge(qk_low, q + 1)
                    for j in range(KS):
                        n = q * (KS // r.J) + j // r.J
                        pe.wait_ge(onehot, n + 1)
                        mm(ps[:, q, 0:W], ident_b[:, :], r.oh[:, n % 4, :, j % r.J], start=(j == 0),
                           stop=(j == KS - 1)).then_inc(counted, 1)
                    if q == 1:
                        pe.wait_ge(ld_w1, 48)
                    if 1 <= q <= B:
                        project_keys(q - 1)
                pe.wait_ge(qk_low, 2 * B * G1)
                for q in range(TB):
                    pe.wait_ge(cnt_out, q + 1)
                    for k in range(KB):
                        o = nc.tensor.transpose(ps[:, 4 + k, :].bitcast(bf16)[:, q * 128:(q + 1) * 128],
                                                r.cnt[:, q, k * 128:(k + 1) * 128], ident_b[:, :])
                    o.then_inc(cnt_turned, 1)

                def scores_max(b, u):
                    n = b * NU + u
                    k = 4 * (u % 2) if (r.fast and b == 0) else 0
                    if r.fast and b == 0:
                        if u >= 2:
                            pe.wait_ge(max1, u - 1)
                        if u == 1:
                            pe.wait_ge(ln_in, TB + 1)
                            pe.wait_ge(biasT_out, 1)
                    elif n:
                        pe.wait_ge(max1, n)
                    bn = r.biasN[:, b % r.nb]
                    km = r.Km[:, b % r.nk]
                    for j in range(4):
                        if r.fast:
                            mm(ps[:, k + j, :].rearrange("p (i k) -> p i k", i=4), ident_b[:, :],
                               bn[:, u, :].unsqueeze(1).broadcast_to([128, 4, W]), start=True, stop=False)
                            o = mm(ps[:, k + j, :], Q1[:, b, j, u * 128:(u + 1) * 128], km[:, 4 * j:4 * j + 4, :],
                                   start=False, stop=True)
                        else:
                            mm(ps[:, j, :], ident_b[:, :], bn[:, j, :], start=True, stop=False)
                            o = mm(ps[:, j, :], Q1[:, b, u // 4, j * 128:(j + 1) * 128], km[:, u, :],
                                   start=False, stop=True)
                    o.then_inc(sn1, 1)

                def scores(b, q):
                    g, k = q // KB, q % KB
                    for i in range(4):
                        h = 4 * g + i
                        c = (b * NQ + q) * 4 + i
                        if c >= 2:
                            pe.wait_ge(exp1, c - 1)
                        bank = ps[:, 4 + c % 2, :]
                        mm(bank, ident_r[:, :], r.biasTh[:, b % r.nb, k, :], start=True, stop=False)
                        mm(bank, ident_r[:, :], r.biasTl[:, b % r.nb, k, :], start=False, stop=False)
                        mm(bank, r.Km[:, b % r.nk, h, k * 128:(k + 1) * 128], Q1[:, b, g, :], start=False, stop=False)
                        for t in range(TB):
                            o = mm(bank[:, t * 128:(t + 1) * 128], negM1[:, b, t, h:h + 1].to_broadcast([128, 128]),
                                   ident_r[:, :], start=False, stop=(t == TB - 1))
                        o.then_inc(st1, 1)

                def weigh(b, q):
                    g, k = q // KB, q % KB
                    pe.wait_ge(exp1, (b * NQ + q + 1) * 4)
                    pe.wait_ge(v1_out, B * KB)
                    if k == 0 and b * G1 + g:
                        pe.wait_ge(z1_out, b * G1 + g)
                    for i in range(4):
                        h = 4 * g + i
                        c = (b * NQ + q) * 4 + i
                        o = mm(ps[32 * i:32 * i + 32, 6, :], V1[:, b * TB + k, h * PAD:(h + 1) * PAD], P1[:, c % 8, :],
                               start=(k == 0), stop=(k == KB - 1))
                    o.then_inc(pv1, 1)

                def values():
                    for b in range(B):
                        for k in range(KB):
                            n = b * KB + k
                            t = b * TB + k
                            if n == 0:
                                pe.wait_ge(max1, NU)
                                pe.wait_ge(biasT_out, 1)
                            if n >= 4:
                                pe.wait_ge(v1_out, n - 3)
                            mm(ps[:, n % 4, :], xT_s[:, t * 128:(t + 1) * 128], wv1_s, start=True, stop=True)\
                                .then_inc(v1_proj, 1)

                pe.wait_ge(km_out, G1)
                for u in range(NU):
                    if r.fast:
                        pe.wait_ge(biasN_out, u + 1)
                    elif u == 0:
                        pe.wait_ge(biasT_out, 1)
                    scores_max(0, u)
                values()
                pe.wait_ge(negm1, 1)
                for q in range(NQ):
                    scores(0, q)
                    if q:
                        weigh(0, q - 1)
                    if r.fast:
                        if q == 0:
                            pe.wait_ge(v1_out, B * KB)
                            pe.wait_ge(km_out, 2 * G1)
                        scores_max(1, q)
                if not r.fast:
                    pe.wait_ge(v1_out, B * KB)
                    pe.wait_ge(km_out, 2 * G1)
                    for u in range(NU):
                        scores_max(1, u)
                pe.wait_ge(negm1, 2)
                for q in range(NQ):
                    scores(1, q)
                    weigh(*((1, q - 1) if q else (0, NQ - 1)))
                    if q == 0:
                        pe.wait_ge(max1, 2 * NU)
                        turn_z(0)
                    if q == KB:
                        turn_zc(0)
                    if q == 2 * KB:
                        project_out1(0)
                weigh(1, NQ - 1)
                turn_xh(0, 2)

            branch(pe, first)

            def value_unit(b, t):
                bank = vbank(b, t)
                if b == 0 and t >= 4:
                    pe.wait_ge(v2_out, t - 3)
                if b and t >= 6:
                    pe.wait_ge(v2_out, 2 * TB + t - 5)
                at = slice(b * S + (t // 2) * 128, b * S + (t // 2 + 1) * 128)
                c = slice((t % 2) * 512, (t % 2 + 1) * 512)
                mm(ps[:, bank, :], xn_h[:, at], w_h[:, 0, c], start=True, stop=False)
                mm(ps[:, bank, :], xn_h[:, at], w_l[:, 0, c], start=False, stop=False)
                mm(ps[:, bank, :], xn_l[:, at], w_h[:, 0, c], start=False, stop=True).then_inc(vproj2, 1)

            def project(w, n, done):
                b, p = n // NP, n % NP
                c, t = slice(p * 128, (p + 1) * 128), slice(b * S, (b + 1) * S)
                mm(ps[:, 7, :], w_h[:, w, c], xn_h[:, t], start=True, stop=False)
                mm(ps[:, 7, :], w_l[:, w, c], xn_h[:, t], start=False, stop=False)
                mm(ps[:, 7, :], w_h[:, w, c], xn_l[:, t], start=False, stop=True).then_inc(done, 1)

            def scores_max2(h):
                n = h // 2
                pe.wait_ge(kh_out, n + 1)
                pe.wait_ge(qh_out, n + 1)
                if h == 0:
                    pe.wait_ge(zeroed, 4)
                if h:
                    pe.wait_ge(max2, h)
                for q in range(TB):
                    bank, at = QPOS[q]
                    mm(ps[:, bank, at:at + 128 * (q + 1)], QH[:, n % 2, h % 2, q * 128:(q + 1) * 128],
                       KH[:, n % 2, 0:128 * (q + 1)], start=True, stop=False)
                    o = mm(ps[:, bank, at + 128 * q:at + 128 * (q + 1)], causal_r[:, :], ident_r[:, :],
                           start=False, stop=True)
                o.then_inc(sn2, 1)

            def scores2(h):
                n, s, j = h // 2, (h // 2) % 2, h % 2
                pe.wait_ge(max2, h + 1)
                pe.wait_ge(kl_out, n + 1)
                pe.wait_ge(ql_out, n + 1)
                if h:
                    pe.wait_ge(exp2, h)
                st = ps[:, 3:6, :].rearrange("p b n -> p (b n)")
                for k in range(TB):
                    a, e = KOFF[k], KOFF[k] + 128 * (TB - k)
                    kc = slice(k * 128, (k + 1) * 128)
                    mm(st[:, a:e], KH[:, s, kc], QH[:, s, j, k * 128:S], start=True, stop=False)
                    mm(st[:, a:e], KH[:, s, kc], QL[:, s, j, k * 128:S], start=False, stop=False)
                    mm(st[:, a:e], KL[:, s, kc], QH[:, s, j, k * 128:S], start=False, stop=False)
                    mm(st[:, a:a + 128], ident_r[:, :], causal_r[:, :], start=False, stop=False)
                    for q in range(k, TB):
                        o = mm(st[:, a + 128 * (q - k):a + 128 * (q - k + 1)],
                               negM2[:, q, h:h + 1].to_broadcast([128, 128]), ident_r[:, :],
                               start=False, stop=(q == TB - 1))
                o.then_inc(st2, 1)

            def weigh2(n):
                pe.wait_ge(exp2, 2 * n + 2)
                pe.wait_ge(v2_out, (n // NP + 1) * 2 * TB)
                if n:
                    pe.wait_ge(z2_out, n)
                else:
                    pe.wait_ge(xn_out, B)
                for k in range(TB):
                    for j in range(2):
                        h = 2 * n + j
                        o = mm(ps[64 * j:64 * j + 64, 6, k * 128:S],
                               V2[:, k, (h % H2) * E2:(h % H2 + 1) * E2],
                               P2[:, h % 4, KOFF[k]:KOFF[k] + 128 * (TB - k)], start=(k == 0), stop=(k == TB - 1))
                o.then_inc(pv2, 1)

            def sum_rows(n):
                pe.wait_ge(acc2, 2 * n + 2)
                for j in range(2):
                    h = 2 * n + j
                    for c in range(4):
                        r = P2[:, h % 4, 0:128] if c == 0 else acc[:, h % 4, c * 128:(c + 1) * 128]
                        o = mm(ps[32 * c:32 * c + 32, 7, 0:128], ones_band[:, 31 - h % H2:63 - h % H2], r,
                               start=(j == 0), stop=(j == 1))
                o.then_inc(sum2, 1)

            def spread(b, p, bank):
                mm(ps[:, bank, :], sel_r[:, p, :], RDh[:, :, :], start=True, stop=False)
                mm(ps[:, bank, :], sel_r[:, p, :], RDl[:, :, :], start=False, stop=True).then_inc(r2, 1)

            def project_out2(b):
                for p in range(NP):
                    pe.wait_ge(zn_out, b * NP + p + 1)
                    o = mm(ps[:, 7, :], w_o[:, p, :], z2[:, b, p, :], start=(p == 0), stop=(p == NP - 1))
                o.then_inc(wo2_done, 1)

            def second_difference(b):
                pe.wait_ge(x1_out, b + 1)
                mm(ps[:, 7, :], lap, x1T[:, b, :], start=True, stop=True).then_inc(lap_done, 1)

            def gate(b):
                pe.wait_ge(du_out, b + 1)
                for t in range(TB):
                    o = mm(ps[:, 6, t * NE:(t + 1) * NE], duT[:, b, t * 128:(t + 1) * 128], wg_s[:, :],
                           start=True, stop=True)
                o.then_inc(gate_done, 1)
                for t in range(TB):
                    o = nc.tensor.transpose(ps[:, 7, t * 128:(t + 1) * 128], x1T[:, b, t * 128:(t + 1) * 128], ident)
                o.then_inc(x1_turned, 1)

            def up(b, n):
                if n >= 4 or b:
                    pe.wait_ge(silu_out, b * NT + n - 3)
                mm(ps[:, n % 4, :], w1_s[:, n, :], duT[:, b, :], start=True, stop=True).then_inc(up_done, 1)

            def down(b, t):
                for q in range(2):
                    if b * TB + t:
                        pe.wait_ge(mixed, (b * TB + t - 1) * 2 + q + 1)
                    for e in range(4 * q, 4 * q + 4):
                        for k in range(2):
                            o = mm(ps[:, 4 + q, (e % 4) * 128:(e % 4 + 1) * 128],
                                   hT[:, 2 * e + k, t * 128:(t + 1) * 128], w2_s[:, 2 * e + k, :],
                                   start=(k == 0), stop=(k == 1))
                    o.then_inc(down_done, 1)

            pe.wait_ge(xn_out, 1)
            pe.wait_ge(w_split, 1)
            turn_z(1)
            for t in range(3):
                value_unit(0, t)
            turn_zc(1)
            for t in range(3, 6):
                value_unit(0, t)
            project_out1(1)
            for t in range(6, 2 * TB):
                value_unit(0, t)
            pe.wait_ge(w_split, 3)
            for b in range(B):
                n = b * NP
                if b:
                    weigh2(n - 1)
                    pe.wait_ge(sum2_out, n - 1)
                    sum_rows(n - 1)
                    pe.wait_ge(max2, 2 * n)
                    pe.wait_ge(exp2, 2 * n)
                    for t in range(2 * TB):
                        value_unit(1, t)
                    pe.wait_ge(sum2_out, n)
                else:
                    pe.wait_ge(v2_out, 2 * TB)
                project(1, n, kproj2)
                pe.wait_ge(kl_out, n + 1)
                project(2, n, qproj2)
                pe.wait_ge(wo1_done, 2)
                pe.wait_ge(var_out, 2)
                pe.wait_ge(v2_out, (b + 1) * 2 * TB)
                scores_max2(2 * n)
                for n in range(b * NP, (b + 1) * NP):
                    p = n % NP
                    if p < NP - 1:
                        pe.wait_ge(ql_out, n + 1)
                        if n == 2:
                            pe.wait_ge(cvec_out, 1)
                        if p >= 2:
                            pe.wait_ge(sum2_out, n - 1)
                        if b and p:
                            pe.wait_ge(zn_out, p)
                        project(1, n + 1, kproj2)
                    scores_max2(2 * n + 1)
                    scores2(2 * n)
                    if p < NP - 1:
                        pe.wait_ge(kl_out, n + 2)
                        project(2, n + 1, qproj2)
                    if n == 0:
                        turn_xh(1, 6)
                    if p:
                        weigh2(n - 1)
                        if p < NP - 1:
                            pe.wait_ge(ql_out, n + 2)
                        elif b:
                            pe.wait_ge(zn_out, p)
                        if n == 1:
                            pe.wait_ge(ld_late, 48)
                            for i in range(NP):
                                o = mm(ps[:, 7, 0:1], w_o[:, i, :], col_s[:, L_BV2 + i:L_BV2 + i + 1],
                                       start=(i == 0), stop=(i == NP - 1))
                            o.then_inc(cvec_done, 1)
                            pe.wait_ge(cvec_out, 1)
                        sum_rows(n - 1)
                    if b:
                        if p == 0:
                            pe.wait_ge(rd_out, 1)
                            pe.wait_ge(w_split, 4)
                            pe.wait_ge(ql_out, n + 2)
                        else:
                            pe.wait_ge(sum2_out, n)
                        spread(0, p, 7)
                    if p < NP - 1:
                        scores_max2(2 * n + 2)
                    scores2(2 * n + 1)
            weigh2(2 * NP - 1)
            pe.wait_ge(zn_out, NP)
            sum_rows(2 * NP - 1)
            pe.wait_ge(sum2_out, 2 * NP)
            project_out2(0)
            second_difference(0)
            pe.wait_ge(z2_out, 2 * NP)
            pe.wait_ge(max2, 4 * NP)
            pe.wait_ge(rd_out, 2)
            for p in range(NP):
                if p == 4:
                    gate(0)
                if p >= 4:
                    pe.wait_ge(zn_out, NP + p - 3)
                spread(1, p, p % 4)
            for n in range(NT):
                if n < 4:
                    pe.wait_ge(zn_out, 2 * NP - 3 + n)
                up(0, n)
                if n == 8:
                    pe.wait_ge(ya_ready, 1)
                    project_out2(1)
                if n == 12:
                    second_difference(1)
            for t in range(TB):
                if t == 0:
                    pe.wait_ge(silu_out, NT)
                down(0, t)
                if t == 1:
                    gate(1)
            for n in range(NT):
                up(1, n)
            pe.wait_ge(silu_out, 2 * NT)
            for t in range(TB):
                down(1, t)


def vbank(b, t):
    return t % 6 if b else 4 + t % 4


C_ID = 0
C_BAND = C_ID + 128
C_RG = C_BAND + 63
C_HALF = C_RG + 4
C_LAP = C_HALF + 2
C_CAUT = C_LAP + 128
C_RANK = C_CAUT + 128
C_HEAD = C_RANK + NE
CONSTS = C_HEAD + 4

L_BQ1 = 0
L_BK1 = L_BQ1 + G1
L_BQ2 = L_BK1 + G1
L_BK2 = L_BQ2 + NP
L_BO2 = L_BK2 + NP
L_LNW = L_BO2 + 1
L_LNB = L_LNW + 1
L_BV2 = L_LNB + 1
COLS = L_BV2 + NP


def kernel(**inputs):
    import numpy as np
    import concourse.bacc as bacc
    from concourse.bass_utils import run_bass_kernel_spmd

    f = {k: np.asarray(v) for k, v in inputs.items()}
    F = np.float32

    def rows(a):
        return np.ascontiguousarray(np.broadcast_to(a.reshape(1, -1), (128, a.size)))

    def padded(wt):
        o = np.zeros((wt.shape[0], H1, PAD), F)
        o[:, :, :E1] = wt.reshape(-1, H1, E1)
        return o.reshape(-1, H1 * PAD)

    def repeated(wt):
        return np.ascontiguousarray(np.repeat(wt.reshape(-1, G1, 1, 4 * E1), 4, axis=2).reshape(-1, H1 * PAD))

    cst = np.zeros((128, CONSTS), F)
    r = np.arange(128)
    cst[:, C_ID:C_ID + 128] = np.eye(128)
    cst[:, [C_BAND + 31, C_BAND + 31 + H2]] = 1
    cst[r, C_HEAD + r % 32 // E1] = 1
    cst[r, C_RG + r // 32] = 1
    cst[r, C_HALF + r // 64] = 1
    lap = -2 * np.eye(128) + np.eye(128, k=1) + np.eye(128, k=-1)
    lap[0, 1] = 2
    lap[127, 126] = 2
    cst[:, C_LAP:C_LAP + 128] = lap.T
    cst[:, C_CAUT:C_CAUT + 128] = np.where(r[:, None] > r[None, :], -BIG, 0)
    cst[:, C_RANK:C_RANK + NE] = np.arange(NE, 0, -1)
    sel = np.zeros((128, NP, 128), F)
    for p in range(NP):
        for j in range(2):
            sel[2 * p + j::32, p, 64 * j:64 * j + 64] = 1

    cols = np.zeros((128, COLS), F)
    cols[:, L_BQ1:L_BQ1 + G1] = repeated(f["L0_cond_bq"].reshape(1, -1)).reshape(G1, 128).T
    cols[:, L_BK1:L_BK1 + G1] = repeated(f["L0_cond_bk"].reshape(1, -1)).reshape(G1, 128).T
    cols[:, L_BQ2:L_BQ2 + NP] = f["L0_attn_b_q"].reshape(NP, 128).T
    cols[:, L_BK2:L_BK2 + NP] = f["L0_attn_b_k"].reshape(NP, 128).T
    cols[:, L_BO2] = f["L0_attn_b_o"]
    cols[:, L_LNW] = f["L0_attn_ln_w"]
    cols[:, L_LNB] = f["L0_attn_ln_b"]
    cols[:, L_BV2:L_BV2 + NP] = f["L0_attn_b_v"].reshape(NP, 128).T

    bv1 = padded(f["L0_cond_bv"].reshape(1, -1)).reshape(H1, PAD)
    bv1[:, E1] = 1
    idx = f["itok_Sx32_0_1023"]
    pm = f["mask_SxS_bk0"]

    def blocks(a):
        return np.ascontiguousarray(a.reshape(-1, 128, a.shape[1]).transpose(1, 0, 2).reshape(128, -1))

    def headed(w):
        return np.ascontiguousarray(w.transpose(1, 0, 2).reshape(D, H2 * E2))

    arrays = {
        "xT": np.ascontiguousarray(f["x"].reshape(T, D).T),
        "wq1": repeated(f["L0_cond_Wq"].T), "wk1": repeated(f["L0_cond_Wk"].T), "wv1": padded(f["L0_cond_Wv"].T),
        "wo1": np.ascontiguousarray(f["L0_cond_Wo"].T),
        "cols": cols, "bv1": rows(bv1), "bo1": rows(f["L0_cond_bo"]),
        "idx": blocks(idx), "imask": blocks(f["mask_Sx32_bk1"]),
        "pmN": blocks(pm), "pmT": blocks(pm.T),
        "scal": rows(np.concatenate([f["condB_uprev"], f["condB_zX"], f["condB_zY"], f["condB_zR"]])),
        "wq2": headed(f["L0_attn_W_q"]), "wk2": headed(f["L0_attn_W_k"]), "wv2": headed(f["L0_attn_W_v"]),
        "wo2": blocks(f["L0_attn_W_o"].reshape(H2 * E2, D)),
        "wg": np.ascontiguousarray(f["L0_ffn_Wg"]),
        "w1": np.ascontiguousarray(f["L0_ffn_W1"].transpose(1, 0, 2).reshape(D, NE * FH)),
        "w2": blocks(f["L0_ffn_W2"].reshape(NE * FH, D)),
        "consts": cst, "iota": rows(np.arange(S, dtype=np.float16)),
        "iotaj": rows(np.repeat(np.arange(128, dtype=np.float16), JH)), "sel": sel.reshape(128, -1),
    }
    nc = bacc.Bacc("TRN2", target_bir_lowering=False, num_devices=1)
    args = [nc.dram_tensor(k, a.shape, mybir.dt.from_np(a.dtype), kind="ExternalInput").ap() for k, a in arrays.items()]
    args.append(nc.dram_tensor("out", (B, S, D), mybir.dt.float32, kind="ExternalOutput").ap())
    program(nc, *args)
    r = run_bass_kernel_spmd(nc, [arrays], core_ids=[0])
    return r.results[0]["out"]
```

```python
import concourse.bass as bass
from concourse import mybir
from contextlib import ExitStack

B, S, D = 2, 512, 128
T = B * S
TB = S // 128
H1, E1, KS = 16, 8, 32
H2, E2 = 16, 64
NP = H2 // 2
NE, FH = 8, 256
NT = NE * FH // 128
PAD = 32
G1 = H1 // 4
JH = 8
SCALE1, SCALE2 = E1 ** -0.5, E2 ** -0.5
BIG = 1e30


def program(
    nc: bass.Bass,
    xT: bass.AP, wq1: bass.AP, wk1: bass.AP, wv1: bass.AP, wo1: bass.AP,
    cols: bass.AP, bv1: bass.AP, bo1: bass.AP, idx: bass.AP, imask: bass.AP,
    pmN: bass.AP, pmT: bass.AP, scal: bass.AP,
    wq2: bass.AP, wk2: bass.AP, wv2: bass.AP, wo2: bass.AP,
    wg: bass.AP, w1: bass.AP, w2: bass.AP,
    consts: bass.AP, iota: bass.AP, iotaj: bass.AP, sel: bass.AP,
    out: bass.AP,
):
    f32 = mybir.dt.float32
    f32r = mybir.dt.float32r
    bf16 = mybir.dt.bfloat16
    i32 = mybir.dt.int32
    u8 = mybir.dt.uint8
    ALU = mybir.AluOpType
    ACT = mybir.ActivationFunctionType
    AX = mybir.AxisListType
    f16 = mybir.dt.float16

    ctx = ExitStack()
    with ctx:
        def sb(name, shape, dt=f32):
            return ctx.enter_context(nc.sbuf_tensor(name, shape, dt))

        def sem(name):
            return ctx.enter_context(nc.semaphore(name))

        cst = sb("cst", [128, CONSTS])
        ident = cst[:, C_ID:C_ID + 128]
        ones_band = cst[:, C_BAND:C_BAND + 63]
        row_group = cst[:, C_RG:C_RG + 4]
        head_rows = cst[:, C_HEAD:C_HEAD + 4]
        lap = cst[:, C_LAP:C_LAP + 128]
        iota_s = sb("iota_s", [128, S], f16)
        iota_j = sb("iota_j", [128, 128 * JH], f16)
        ident_r = sb("ident_r", [128, 128], f32r)
        ident_b = sb("ident_b", [128, 128], bf16)
        causal_r = sb("causal_r", [128, 128], f32r)
        ones_r = sb("ones_r", [128, 128], f32r)
        sel_r = sb("sel_r", [128, NP, 128], f32r)
        xT_s = sb("xT_s", [128, T])
        w1st = sb("w1st", [128, 3, H1 * PAD])
        wq1_s, wk1_s, wv1_s = w1st[:, 0, :], w1st[:, 1, :], w1st[:, 2, :]
        bv1_s = sb("bv1_s", [128, H1 * PAD])
        wo1_s = sb("wo1_s", [128, D])
        col_s = sb("col_s", [128, COLS])
        bo1_s = sb("bo1_s", [128, D])
        scal_s = sb("scal_s", [128, 8])
        wg_s = sb("wg_s", [128, NE])
        raw = sb("raw", [128, H2 * E2])
        w_hl = sb("w_hl", [128, 2, 3, H2 * E2], f32r)
        w_h, w_l = w_hl[:, 0], w_hl[:, 1]
        xn_h = sb("xn_h", [128, T], f32r)
        xn_l = sb("xn_l", [128, T], f32r)
        stats = sb("stats", [128, TB, 6])
        mv = sb("mv", [128, TB, 2])
        rstd = sb("rstd", [128, 4, TB])
        rec1 = sb("rec1", [128, TB, H1])
        lam = sb("lam", [128, 8])
        path = sb("path", [128, 4])
        path_i = sb("path_i", [1, 1], i32)
        cvec = sb("cvec", [128, 1])
        attn1 = ExitStack()

        def sb1(name, shape, dt=f32):
            return attn1.enter_context(nc.sbuf_tensor(name, shape, dt))

        biasT = sb1("biasT", [128, B * TB * S], f32r)
        zT1 = sb1("zT1", [128, G1, S])
        zc = sb1("zc", [128, TB, 128])
        zcT = sb1("zcT", [128, S])
        xn32 = zcT[:, :]
        y_s = sb1("y_s", [128, TB, D])
        xh = sb1("xh", [128, TB, D])
        idx_s = sb1("idx_s", [128, TB, KS], i32)
        im_s = sb1("im_s", [128, TB, KS], u8)
        idf = sb1("idf", [128, TB, KS])
        idw = sb1("idw", [128, TB, KS])
        idm = sb1("idm", [128, TB, KS])
        idm_h = sb1("idm_h", [128, TB, KS], f16)
        mraw = sb1("mraw", [128, B, TB, H1])
        mtmp = sb1("mtmp", [128, TB, H1])
        negM1 = sb1("negM1", [128, B, TB, H1], f32r)
        Ks = sb1("Ks", [128, 4, S], f32r)
        Q1 = sb1("Q1", [128, B, G1, S], f32r)
        Km_s = sb1("Km_s", [128, H1 * S], f32r)
        V1 = sb1("V1", [128, B * TB, H1 * PAD])
        biasN = sb1("biasN", [128, B * TB * S], bf16)
        biasT_more = w_hl[:, :, :, :].rearrange("p a n m -> p (a n m)")
        P1 = sb1("P1", [128, 8, S])
        cntT = sb1("cntT", [128, S])
        oh_s = V1[:, 0:4, :].rearrange("p a b -> p (a b)").bitcast(bf16)
        cnt_s = V1[:, 4:6, :].rearrange("p a b -> p (a b)").bitcast(bf16)
        pm_s = V1[:, 6:7, :].rearrange("p a b -> p (a b)").bitcast(u8)
        pmT_s = V1[:, 7:8, :].rearrange("p a b -> p (a b)").bitcast(u8)
        tmpA, tmpB, tmpC = P1[:, 0:4, :], P1[:, 4:8, :], zT1
        attn1.close()

        attn2 = ExitStack()

        def sb2(name, shape, dt=f32):
            return attn2.enter_context(nc.sbuf_tensor(name, shape, dt))

        z2 = sb2("z2", [128, B, NP, S])
        w_o = sb2("w_o", [128, NP, D])
        w1_s = sb2("w1_s", [128, NT, 128])
        w2_s = sb2("w2_s", [128, NT, D])
        V2 = sb2("V2", [128, TB, H2 * E2])
        KK = sb2("KK", [128, 3, 2, S], f32r)
        diag = sb2("diag", [128, 2, TB, 128], f32r)
        negM2 = sb2("negM2", [128, TB, 2 * H2])
        sums = sb2("sums", [128, B, 128])
        rsum = sb2("rsum", [128, 128])
        acc = sb2("acc", [128, 4, S])
        RDh = sb2("RDh", [128, 4, 128], f32r)
        RDl = sb2("RDl", [128, 4, 128], f32r)
        x1T = sb2("x1T", [128, B, S])
        rea = sb2("rea", [128, S])
        RDf = rea[:, :].rearrange("p (c q) -> p c q", c=4)
        duT = sb2("duT", [128, B, S])
        gl = sb2("gl", [128, 12, TB, NE])
        gs = sb2("gs", [128, 8, TB])
        comb = sb2("comb", [128, B, TB, NE])
        pairs = attn2.enter_context(ExitStack())
        QH = pairs.enter_context(nc.sbuf_tensor("QH", [128, 2, 2, S], f32r))
        QL = pairs.enter_context(nc.sbuf_tensor("QL", [128, 2, 2, S], f32r))
        P2 = pairs.enter_context(nc.sbuf_tensor("P2", [128, 4, 1280], f32))
        pairs.close()
        hT = sb2("hT", [128, NT, S])
        attn2.close()
        w1_h = w_hl[:, 0, 0:2, :].rearrange("p a n -> p (a n)")
        w1_l = w_hl[:, 1, 0:2, :].rearrange("p a n -> p (a n)")
        du_h, du_l = KK[:, 0:B, 0, :], KK[:, 0:B, 1, :]
        ya = V2[:, 0:B, 0:TB * D].rearrange("p b (t d) -> p b t d", t=TB)
        dif, dif2 = V2[:, B, 0:S], V2[:, B, S:2 * S]

        ps = ctx.enter_context(nc.psum_tensor("ps", [128, 8, 512], f32))

        ld_x = sem("ld_x")
        ld_q1 = sem("ld_q1")
        ld_w1 = sem("ld_w1")
        ld_idx = sem("ld_idx")
        ld_cst = sem("ld_cst")
        ld_iota = sem("ld_iota")
        ld_pm = sem("ld_pm")
        ld_o1 = sem("ld_o1")
        ld_raw = sem("ld_raw")
        ld_o2 = sem("ld_o2")
        ld_late = sem("ld_late")
        stored = sem("stored")
        cst_ready = sem("cst_ready")
        flag_in = sem("flag_in")
        flag_sum = sem("flag_sum")
        flag_ready = sem("flag_ready")
        proj1 = sem("proj1")
        qk_out = sem("qk_out")
        qk_low = sem("qk_low")
        zeroed = sem("zeroed")
        v1_proj = sem("v1_proj")
        v1_out = sem("v1_out")
        onehot = sem("onehot")
        counted = sem("counted")
        cnt_out = sem("cnt_out")
        cnt_turned = sem("cnt_turned")
        ln_in = sem("ln_in")
        ln_out = sem("ln_out")
        lam_out = sem("lam_out")
        biasN_out = sem("biasN_out")
        biasT_out = sem("biasT_out")
        km_out = sem("km_out")
        sn1 = sem("sn1")
        max1 = sem("max1")
        negm1 = sem("negm1")
        st1 = sem("st1")
        exp1 = sem("exp1")
        bounded = sem("bounded")
        pool_named = sem("pool_named")
        dve_named = sem("dve_named")
        pv1 = sem("pv1")
        z1_out = sem("z1_out")
        z1_turned = sem("z1_turned")
        norm1 = sem("norm1")
        zc_turned = sem("zc_turned")
        zcT_out = sem("zcT_out")
        wo1_done = sem("wo1_done")
        y_out = sem("y_out")
        var_out = sem("var_out")
        rstd_out = sem("rstd_out")
        xh_out = sem("xh_out")
        xh_turned = sem("xh_turned")
        xn_out = sem("xn_out")
        w_split = sem("w_split")
        vproj2 = sem("vproj2")
        v2_out = sem("v2_out")
        kproj2 = sem("kproj2")
        qproj2 = sem("qproj2")
        kh_out = sem("kh_out")
        kl_out = sem("kl_out")
        qh_own = sem("qh_own")
        qh_out = sem("qh_out")
        ql_out = sem("ql_out")
        sn2 = sem("sn2")
        max2 = sem("max2")
        diag_out = sem("diag_out")
        st2 = sem("st2")
        exp2 = sem("exp2")
        acc2 = sem("acc2")
        pv2 = sem("pv2")
        z2_out = sem("z2_out")
        sum2 = sem("sum2")
        sum2_out = sem("sum2_out")
        rd_out = sem("rd_out")
        r2 = sem("r2")
        zn_out = sem("zn_out")
        cvec_done = sem("cvec_done")
        cvec_out = sem("cvec_out")
        wo2_done = sem("wo2_done")
        x1_out = sem("x1_out")
        lap_done = sem("lap_done")
        du_out = sem("du_out")
        du_split = sem("du_split")
        w1_whole = sem("w1_whole")
        w1_split = sem("w1_split")
        gate_done = sem("gate_done")
        gmax_out = sem("gmax_out")
        gexp_out = sem("gexp_out")
        x1_turned = sem("x1_turned")
        ya_ready = sem("ya_ready")
        up_done = sem("up_done")
        silu_out = sem("silu_out")
        down_done = sem("down_done")
        mixed = sem("mixed")
        dve_step = sem("dve_step")
        dve_step_fast = sem("dve_step_fast")
        dve_step_all = sem("dve_step_all")
        act_step = sem("act_step")
        pool_step = sem("pool_step")

        KOFF = [0, 640, 1024, 512]
        QPOS = [(1, 384), (2, 0), (1, 0), (0, 0)]
        SPREAD = [0, 1, 2, 3, 4, 5, 0, 1]
        X1_BANK = [7, 6]
        GATE_BANK = [4, 6]
        mm = nc.tensor.matmul

        class Reach:

            def __init__(self, KB):
                self.KB, self.W = KB, 128 * KB
                self.fast = KB == 1
                self.NQ = G1 * KB
                self.NU = TB if KB == 1 else H1
                W = self.W
                self.J = JH if self.fast else 1
                self.oh = oh_s[:, 0:4 * W * self.J].rearrange("p (r k j) -> p r k j", r=4, j=self.J)
                self.cnt = cnt_s[:, 0:TB * W].rearrange("p (t k) -> p t k", t=TB)
                nb = 1 if self.fast else B
                self.biasN = biasN[:, 0:nb * TB * W].rearrange("p (b t k) -> p b t k", b=nb, t=TB)
                self.biasTh = biasT[:, 0:nb * KB * S].rearrange("p (b k q) -> p b k q", b=nb, k=KB)
                tl = biasT[:, S:2 * S] if self.fast else biasT_more[:, 0:nb * KB * S]
                self.biasTl = tl.rearrange("p (b k q) -> p b k q", b=nb, k=KB)
                nk = B if self.fast else 1
                self.Km = Km_s[:, 0:nk * H1 * W].rearrange("p (b h k) -> p b h k", b=nk, h=H1)
                self.nb, self.nk = nb, nk

            def cbank(self, q):
                return q % 2 if self.fast else q

            def vbank(self, n):
                return 6 + n if self.fast else n % 4

        FAST, ALL = Reach(1), Reach(TB)

        block = ctx.enter_context(nc.Block())

        def branch(eng, run):
            eng.wait_ge(flag_ready, 1)
            flag = eng.value_load(path_i[0:1, 0:1])
            with eng.If(flag > 0):
                run(ALL)
            with eng.Else():
                run(FAST)

        @block.sync
        def _(sp):
            sp.dma_start(wq1_s, wq1).then_inc(ld_q1, 16)
            sp.dma_start(xT_s[:, 0:S], xT[:, 0:S]).then_inc(ld_x, 16)
            sp.dma_start(xT_s[:, S:T], xT[:, S:T]).then_inc(ld_x, 16)
            sp.dma_start(wk1_s, wk1).then_inc(ld_w1, 16)
            sp.dma_start(wv1_s, wv1).then_inc(ld_w1, 16)
            sp.dma_start(bv1_s[:, :], bv1).then_inc(ld_w1, 16)
            sp.dma_start(pm_s, pmN).then_inc(ld_pm, 16)
            sp.dma_start(pmT_s, pmT).then_inc(ld_pm, 16)
            sp.dma_start(wo1_s[:, :], wo1).then_inc(ld_o1, 16)
            sp.dma_start(bo1_s[:, :], bo1).then_inc(ld_o1, 16)
            sp.dma_start(wg_s[:, :], wg).then_inc(ld_o1, 16)
            for n, w in enumerate((wv2, wk2, wq2)):
                if n:
                    sp.wait_ge(w_split, n)
                sp.dma_start(raw[:, :], w).then_inc(ld_raw, 16)
            sp.wait_ge(w_split, 3)
            sp.dma_start(raw[:, :].rearrange("p (n m) -> p n m", n=NP), sel.rearrange("p (n m) -> p n m", n=NP))\
                .then_inc(ld_raw, 16)
            sp.wait_ge(z1_out, B * G1)
            sp.dma_start(w_o[:, :, :], wo2.rearrange("p (n m) -> p n m", n=NP)).then_inc(ld_o2, 16)
            sp.dma_start(w1_s[:, :, :], w1.rearrange("p (n m) -> p n m", n=NT)).then_inc(ld_late, 16)
            sp.dma_start(w2_s[:, :, :], w2.rearrange("p (n m) -> p n m", n=NT)).then_inc(ld_late, 16)
            for b in range(B):
                for t in range(TB):
                    sp.wait_ge(mixed, (b * TB + t + 1) * 2)
                    sp.dma_start(out[b, t * 128:(t + 1) * 128, :], ya[:, b, t, :]).then_inc(stored, 16)
            sp.wait_ge(stored, 16 * B * TB)

        @block.gpsimd
        def _(pool):
            pool.dma_start(idx_s[:, :, :], idx.rearrange("p (b j) -> p b j", b=TB)).then_inc(ld_idx, 16)
            pool.dma_start(im_s[:, :, :], imask.rearrange("p (b j) -> p b j", b=TB)).then_inc(ld_idx, 16)
            pool.dma_start(iota_j[:, :], iotaj).then_inc(ld_iota, 16)
            pool.dma_start(iota_s[:, :], iota).then_inc(ld_iota, 16)

            def split_weights():
                for n in range(3):
                    pool.wait_ge(ld_raw, 16 * (n + 1))
                    nc.gpsimd.tensor_copy(w_h[:, n, :], raw[:, :]).then_inc(pool_step, 1)
                    pool.wait_ge(pool_step, n + 1)
                    nc.gpsimd.tensor_tensor(w_l[:, n, :], raw[:, :], w_h[:, n, :].bitcast(f32), ALU.subtract)\
                        .then_inc(w_split, 1)
                pool.wait_ge(ld_raw, 64)
                nc.gpsimd.tensor_copy(sel_r[:, :, :], raw[:, :].rearrange("p (n m) -> p n m", n=NP)).then_inc(w_split, 1)

            def first(r):
                if r.fast:
                    split_weights()
                    for c in range(1, B * H1, 4):
                        pool.wait_ge(exp1, c + 1)
                        nc.gpsimd.tensor_scalar(P1[:, c % 8, :], P1[:, c % 8, :], 2.0, None, ALU.min)\
                            .then_inc(bounded, 1)
                        pool.wait_ge(bounded, c // 4 + 1)
                        nc.gpsimd.tensor_tensor(P1[:, c % 8, :], P1[:, c % 8, :], cntT[:, :], ALU.mult)\
                            .then_inc(pool_named, 1)
                else:
                    pool.wait_ge(st1, B * 4 * r.NQ)
                    split_weights()

            branch(pool, first)
            steps = [3]

            def link(ins):
                steps[0] += 1
                ins.then_inc(pool_step, 1)
                pool.wait_ge(pool_step, steps[0])

            def pool_sum(h):
                pool.wait_ge(exp2, h + 1)
                if h >= 4:
                    pool.wait_ge(sum2, (h - 4) // 2 + 1)
                p, a = P2[:, h % 4, :], acc[:, h % 4, :]
                link(nc.gpsimd.tensor_tensor(a[:, 128:512], p[:, 128:512], p[:, KOFF[1]:KOFF[1] + 384], ALU.add))
                link(nc.gpsimd.tensor_tensor(a[:, 256:512], a[:, 256:512], p[:, KOFF[2]:KOFF[2] + 256], ALU.add))
                nc.gpsimd.tensor_tensor(a[:, 384:512], a[:, 384:512], p[:, KOFF[3]:KOFF[3] + 128], ALU.add)\
                    .then_inc(acc2, 1)

            pool.wait_ge(z1_out, B * G1)
            pool.wait_ge(w_split, 4)
            nc.gpsimd.memset(QL[64:128, :, 0, :].bitcast(f32), 0.0).then_inc(zeroed, 1)
            pool.wait_ge(zeroed, 1)
            nc.gpsimd.memset(QL[0:64, :, 1, :].bitcast(f32), 0.0).then_inc(zeroed, 1)
            pool.wait_ge(zeroed, 2)

            def diagonal(h):
                pool.wait_ge(max2, h + 1)
                if h >= 2:
                    pool.wait_ge(st2, h - 1)
                nc.gpsimd.tensor_tensor(diag[:, h % 2, :, :], ident.unsqueeze(1).broadcast_to([128, TB, 128]),
                                        negM2[:, :, h:h + 1].broadcast_to([128, TB, 128]), ALU.mult)\
                    .then_inc(diag_out, 1)

            diagonal(0)
            for h in range(B * H2):
                if h + 1 < B * H2:
                    diagonal(h + 1)
                pool_sum(h)
                i = h - (B * H2 - 4)
                if i >= 0:
                    pool.wait_ge(ld_late, 32)
                    pool.wait_ge(qproj2, B * NP)
                    c = slice(i * 4, i * 4 + 4)
                    q = slice(i * 512, i * 512 + 512)
                    whole = w1_s[:, c, :].rearrange("p n m -> p (n m)")
                    nc.gpsimd.tensor_scalar(w1_h[:, q], whole, 1.0, None, ALU.mult).then_inc(w1_whole, 1)
                    pool.wait_ge(w1_whole, i + 1)
                    nc.gpsimd.tensor_tensor(w1_l[:, q], whole, w1_h[:, q].bitcast(f32), ALU.subtract)\
                        .then_inc(w1_split, 1)

        @block.scalar
        def _(act):
            act.dma_start(col_s[:, :], cols).then_inc(ld_cst, 16)
            act.dma_start(scal_s[:, :], scal).then_inc(ld_cst, 16)
            act.dma_start(cst[:, :], consts).then_inc(ld_cst, 16)
            nc.scalar.preload_act_table_set("natural_log_exp_and_others")
            act.wait_ge(ld_cst, 48)
            nc.scalar.activation(lam[:, 0:B], scal_s[:, 0:B], ACT.Exp, scale=-5.0).then_inc(lam_out, 1)

            def z_out(r, b, g):
                act.wait_ge(pv1, b * r.NQ + (g + 1) * r.KB)
                if b:
                    act.wait_ge(z1_turned, b * TB)
                nc.scalar.activation(zT1[:, g, :], ps[:, 6, :], ACT.Copy).then_inc(z1_out, 1)

            def tail_a(b):
                act.wait_ge(zc_turned, b + 1)
                nc.scalar.activation(zcT[:, :], ps[:, 0, :], ACT.Copy).then_inc(zcT_out, 1)

            def tail_b(b):
                act.wait_ge(var_out, b + 1)
                nc.scalar.activation(rstd[:, 1, :], rstd[:, 0, :], ACT.Ln).then_inc(act_step, 1)
                act.wait_ge(act_step, b + 1)
                nc.scalar.activation(rstd[:, 1, :], rstd[:, 1, :], ACT.Exp, scale=-0.5).then_inc(rstd_out, 1)

            def qk_whole(to, j, n, col):
                act.wait_ge(proj1, j + 1)
                nc.scalar.activation(to, ps[:, j if j < B * G1 else G1 + j % G1, 0:n], ACT.Identity,
                                     bias=col_s[:, col:col + 1]).then_inc(qk_out, 1)

            for j in range(B * G1):
                qk_whole(Q1[:, j // G1, j % G1, :], j, S, L_BQ1 + j % G1)

            def keys(r, b):
                if b:
                    act.wait_ge(km_out, G1)
                for g in range(G1):
                    qk_whole(Ks[:, g, 0:r.W], B * G1 + b * G1 + g, r.W, L_BK1 + g)

            def alone(r, b):
                for g in range(G1):
                    act.wait_ge(qk_low, B * G1 + b * G1 + g + 1)
                    for i in range(4):
                        o = nc.scalar.activation(r.Km[:, b % r.nk, 4 * g + i, :], Ks[:, g, 0:r.W].bitcast(f32), ACT.Copy,
                                                 scale=head_rows[:, i:i + 1])
                    o.then_inc(km_out, 1)

            def first(r):
                for q in range(TB):
                    if q >= B:
                        keys(r, q - B)
                        if q == B or r.fast:
                            alone(r, q - B)
                if not r.fast:
                    act.wait_ge(ln_in, 1)
                    nc.scalar.activation(tmpA[:, :, :], tmpA[:, :, :], ACT.Ln).then_inc(ln_out, 1)
                    act.wait_ge(ln_in, 2)
                    nc.scalar.activation(tmpC[:, 0:r.KB, :], tmpC[:, 0:r.KB, :], ACT.Ln).then_inc(ln_out, 1)
                for b in range(B):
                    if b and not r.fast:
                        alone(r, b)
                    for n in range(4 * r.NQ):
                        c = b * 4 * r.NQ + n
                        act.wait_ge(st1, c + 1)
                        if c >= 8:
                            act.wait_ge(pv1, c // 4 - 1)
                        nc.scalar.activation(P1[:, c % 8, :], ps[:, 4 + c % 2, :], ACT.Exp, scale=SCALE1)\
                            .then_inc(exp1, 1)
                        q = c // 4 - 1
                        if n % 4 == 3 and q >= 0 and q % r.KB == r.KB - 1:
                            z_out(r, q // r.NQ, q % r.NQ // r.KB)
                        if b and n == 8 * r.KB:
                            tail_a(0)
                        if b and n == 15 * r.KB:
                            tail_b(0)
                z_out(r, B - 1, G1 - 1)

            branch(act, first)

            def keys_out(n):
                act.wait_ge(kproj2, n + 1)
                if n >= 3:
                    act.wait_ge(st2, 2 * (n - 2))
                p = n % NP
                for j in range(2):
                    own = slice(64 * j, 64 * j + 64)
                    o = nc.scalar.activation(KK[own, n % 3, j, :], ps[own, 7, :], ACT.Identity,
                                             bias=col_s[own, L_BK2 + p:L_BK2 + p + 1])
                o.then_inc(kh_out, 1)

            def queries_out(n):
                act.wait_ge(qproj2, n + 1)
                p = n % NP
                for j in range(2):
                    own = slice(64 * j, 64 * j + 64)
                    o = nc.scalar.activation(QH[own, n % 2, j, :], ps[own, 7, :], ACT.Identity,
                                             bias=col_s[own, L_BQ2 + p:L_BQ2 + p + 1])
                o.then_inc(qh_own, 1)
                act.wait_ge(qh_own, n + 1)
                for j in range(2):
                    own, other = slice(64 * j, 64 * j + 64), slice(64 - 64 * j, 128 - 64 * j)
                    o = nc.scalar.activation(QH[other, n % 2, j, :], QH[own, n % 2, j, :].bitcast(f32), ACT.Copy)
                o.then_inc(qh_out, 1)

            def exp(h):
                act.wait_ge(st2, h + 1)
                if h >= 4:
                    act.wait_ge(pv2, (h - 4) // 2 + 1)
                    act.wait_ge(acc2, h - 3)
                    act.wait_ge(sum2, (h - 4) // 2 + 1)
                nc.scalar.activation(P2[:, h % 4, :], ps[:, 3:6, :].rearrange("p b n -> p (b n)")[:, 0:1280],
                                     ACT.Exp, scale=SCALE2).then_inc(exp2, 1)

            def z2_copy(n):
                act.wait_ge(pv2, n + 1)
                nc.scalar.activation(z2[:, n // NP, n % NP, :], ps[:, 6, :], ACT.Copy).then_inc(z2_out, 1)

            def v2_copy(b, t):
                act.wait_ge(vproj2, b * 2 * TB + t + 1)
                if b and t == 0:
                    act.wait_ge(pv2, b * NP)
                nc.scalar.activation(V2[:, t // 2, (t % 2) * 512:(t % 2 + 1) * 512], ps[:, vbank(b, t), :], ACT.Copy)\
                    .then_inc(v2_out, 1)

            keys_out(0)
            for t in range(3):
                v2_copy(0, t)
            tail_a(1)
            queries_out(0)
            for t in range(3, 6):
                v2_copy(0, t)
            keys_out(1)
            for t in range(6, 2 * TB):
                v2_copy(0, t)
            queries_out(1)
            for n in range(B * NP):
                if n == NP:
                    z2_copy(n - 1)
                    for t in range(2 * TB):
                        v2_copy(1, t)
                if n == 1:
                    tail_b(1)
                exp(2 * n)
                if n < B * NP - 2:
                    keys_out(n + 2)
                exp(2 * n + 1)
                if n % NP:
                    z2_copy(n - 1)
                if n < B * NP - 2:
                    queries_out(n + 2)
            z2_copy(n)

            def gate_exp(b):
                act.wait_ge(gmax_out, b + 1)
                nc.scalar.activation(gl[:, 1, :, :], gl[:, 1, :, :], ACT.Exp).then_inc(gexp_out, 1)

            def residual(b):
                act.wait_ge(x1_turned, b + 1)
                nc.scalar.activation(ya[:, b, :, :], ps[:, 7, :].rearrange("p (t d) -> p t d", t=TB), ACT.Copy)\
                    .then_inc(ya_ready, 1)

            def silu(b, n):
                act.wait_ge(up_done, b * NT + n + 1)
                if b and n == 0:
                    act.wait_ge(down_done, b * TB * 2)
                nc.scalar.activation(hT[:, n, :], ps[:, n % 4, :], ACT.Silu).then_inc(silu_out, 1)

            for b in range(B):
                gate_exp(b)
                residual(b)
                for n in range(NT):
                    silu(b, n)

        @block.vector
        def _(dve):
            steps = {dve_step: 0, dve_step_fast: 0, dve_step_all: 0}
            now = [dve_step]

            def link(ins):
                steps[now[0]] += 1
                ins.then_inc(now[0], 1)
                dve.wait_ge(now[0], steps[now[0]])

            dve.wait_ge(ld_idx, 32)
            link(nc.vector.tensor_copy(idf[:, :, :], idx_s[:, :, :]))
            link(nc.vector.tensor_scalar(idw[:, :, :], idf[:, :, :], 0.0, float(S), ALU.is_lt, ALU.mult))
            link(nc.vector.tensor_tensor(idf[:, :, :], idf[:, :, :], idw[:, :, :], ALU.add))
            link(nc.vector.tensor_scalar(idf[:, :, :], idf[:, :, :], 0.0, float(S - 1), ALU.max, ALU.min))
            link(nc.vector.tensor_copy(idw[:, :, :], im_s[:, :, :]))
            link(nc.vector.scalar_tensor_tensor(idm[:, :, :], idf[:, :, :], 1.0, idw[:, :, :], ALU.add, ALU.mult))
            link(nc.vector.tensor_scalar(idm[:, :, :], idm[:, :, :], 1.0, None, ALU.subtract))
            nc.vector.tensor_copy(idm_h[:, :, :], idm[:, :, :])
            link(nc.vector.tensor_reduce(path[:, 0:1], idm[:, :, :], axis=AX.XY, op=ALU.max))
            link(nc.vector.tensor_scalar(path[:, 0:1], path[:, 0:1], 128.0, None, ALU.is_ge))
            dve.wait_ge(lam_out, 1)
            link(nc.vector.tensor_scalar(lam[:, 2:4], lam[:, 0:2], 10.0, None, ALU.mult))
            link(nc.vector.tensor_scalar(lam[:, 4:6], lam[:, 2:4], 1.0, None, ALU.is_ge))
            link(nc.vector.tensor_scalar(lam[:, 2:4], lam[:, 2:4], 1.0, 1.0 / SCALE1, ALU.min, ALU.mult))
            link(nc.vector.tensor_scalar(lam[:, 6:8], lam[:, 4:6], -1.0, 1.0, ALU.mult, ALU.add))
            link(nc.vector.tensor_copy(path[:, 1:3], lam[:, 6:8]))
            nc.vector.tensor_reduce(path[:, 3:4], path[:, 0:3], axis=AX.X, op=ALU.add).then_inc(flag_in, 1)
            link(nc.vector.tensor_tensor(lam[:, 6:8], lam[:, 6:8], lam[:, 2:4], ALU.mult))
            nc.vector.tensor_copy(ident_r[:, :], ident)
            nc.vector.tensor_copy(causal_r[:, :], cst[:, C_CAUT:C_CAUT + 128])
            nc.vector.tensor_scalar(ones_r[:, :], ident, 0.0, 1.0, ALU.mult, ALU.add)
            nc.vector.tensor_copy(ident_b[:, :], ident).then_inc(cst_ready, 1)
            dve.wait_ge(flag_sum, 1)
            nc.vector.tensor_copy(path_i[:, :], ps[0:1, 7, 0:1]).then_inc(flag_ready, 1)

            def normalise(b):
                for q in range(TB):
                    dve.wait_ge(z1_turned, b * TB + q + 1)
                    z = ps[:, q, :].rearrange("p (h c) -> p h c", c=PAD)
                    link(nc.vector.reciprocal(rec1[:, q, :], z[:, :, E1]))
                    nc.vector.tensor_tensor(zc[:, q, :].rearrange("p (h c) -> p h c", c=E1), z[:, :, 0:E1],
                                            rec1[:, q, :].unsqueeze(2).broadcast_to([128, H1, E1]), ALU.mult)\
                        .then_inc(norm1, 1)

            def projected(b):
                dve.wait_ge(wo1_done, b + 1)
                dve.wait_ge(ld_o1, 48)
                nc.vector.tensor_tensor(y_s[:, :, :], ps[:, 1, :].rearrange("p (t d) -> p t d", t=TB),
                                        bo1_s[:, :].unsqueeze(1).broadcast_to([128, TB, D]), ALU.add)\
                    .then_inc(y_out, 1)

            def moments(b):
                dve.wait_ge(y_out, b + 1)
                for t in range(TB):
                    link(nc.vector.bn_stats(stats[:, t, :], y_s[:, t, :]))
                for t in range(TB):
                    o = nc.vector.bn_aggr(mv[:, t, :], stats[:, t, :])
                    if t == TB - 1:
                        link(o)
                nc.vector.tensor_scalar(rstd[:, 0, :], mv[:, :, 1], 1e-5, None, ALU.add).then_inc(var_out, 1)

            def standardise(b):
                dve.wait_ge(rstd_out, b + 1)
                link(nc.vector.tensor_tensor(rstd[:, 2, :], rstd[:, 1, :], rstd[:, 1, :], ALU.mult))
                link(nc.vector.tensor_tensor(rstd[:, 2, :], rstd[:, 2, :], rstd[:, 0, :], ALU.mult))
                link(nc.vector.tensor_scalar(rstd[:, 2, :], rstd[:, 2, :], -0.5, 1.5, ALU.mult, ALU.add))
                link(nc.vector.tensor_tensor(rstd[:, 3, :], rstd[:, 2, :], rstd[:, 1, :], ALU.mult))
                for t in range(TB):
                    o = nc.vector.tensor_scalar(xh[:, t, :], y_s[:, t, :], mv[:, t, 0:1], rstd[:, 3, t:t + 1],
                                                ALU.subtract, ALU.mult)
                o.then_inc(xh_out, 1)

            def xn_split(b, bank):
                dve.wait_ge(xh_turned, b + 1)
                link(nc.vector.tensor_scalar(xn32, ps[:, bank, :], col_s[:, L_LNW:L_LNW + 1],
                                             col_s[:, L_LNB:L_LNB + 1], ALU.mult, ALU.add))
                link(nc.vector.tensor_copy(xn_h[:, b * S:(b + 1) * S], xn32))
                nc.vector.tensor_tensor(xn_l[:, b * S:(b + 1) * S], xn32, xn_h[:, b * S:(b + 1) * S].bitcast(f32),
                                        ALU.subtract).then_inc(xn_out, 1)

            def first(r):
                KB, W, NU, NQ = r.KB, r.W, r.NU, r.NQ
                now[0] = dve_step_fast if r.fast else dve_step_all

                def onehots(q):
                    for j in range(KS // r.J):
                        n = q * (KS // r.J) + j
                        if n >= 4:
                            dve.wait_ge(counted, (n - 3) * r.J)
                        if r.fast:
                            o = nc.vector.tensor_tensor(
                                r.oh[:, n % 4, :, :], iota_j[:, :].rearrange("p (k j) -> p k j", j=JH),
                                idm_h[:, q, j * JH:(j + 1) * JH].unsqueeze(1).broadcast_to([128, W, JH]), ALU.is_equal)
                        else:
                            o = nc.vector.tensor_scalar(r.oh[:, n % 4, :, 0], iota_s[:, 0:W], idm[:, q, j:j + 1], None,
                                                        ALU.is_equal)
                        o.then_inc(onehot, 1)

                def cnt_copy(q):
                    dve.wait_ge(counted, (q + 1) * KS)
                    nc.vector.tensor_copy(r.cnt[:, q, :], ps[:, r.cbank(q), 0:W]).then_inc(cnt_out, 1)
                    dve.wait_ge(cnt_out, q + 1)

                def log_in(a, cnt, c):
                    link(nc.vector.tensor_scalar(c, cnt, 0.5, -BIG, ALU.is_lt, ALU.mult))
                    nc.vector.tensor_scalar(a, cnt, 1.0, None, ALU.max).then_inc(ln_in, 1)

                dve.wait_ge(ld_iota, 32)
                if r.fast:
                    for q in range(TB):
                        onehots(q)
                        if q < TB - 1:
                            splits(r, q)
                        cnt_copy(q)
                        nc.vector.tensor_scalar(r.biasN[:, 0, q, :], r.cnt[:, q, :], 0.5, -BIG, ALU.is_lt, ALU.mult)\
                            .then_inc(biasN_out, 1)
                    splits(r, TB - 1)
                    dve.wait_ge(cnt_turned, TB)
                    nc.vector.tensor_copy(cntT[:, :], ps[:, 2, :].bitcast(bf16)[:, 0:512]).then_inc(biasT_out, 1)
                else:
                    for q in range(B):
                        splits(r, q)
                    for q in range(TB):
                        onehots(q)
                        cnt_copy(q)
                        if q >= B:
                            splits(r, q)
                    log_in(tmpA, r.cnt, tmpB)
                    dve.wait_ge(ln_out, 1)
                    link(nc.vector.scalar_tensor_tensor(tmpB, tmpA, 1.0 / SCALE1, tmpB, ALU.mult, ALU.add))
                    dve.wait_ge(ld_pm, 32)
                    pm = pm_s.rearrange("p (t k) -> p t k", t=TB)
                    for b in range(B):
                        link(nc.vector.tensor_scalar(tmpA, pm, 1.0, lam[:, 6 + b:7 + b], ALU.subtract, ALU.mult))
                        link(nc.vector.scalar_tensor_tensor(r.biasN[:, b, :, :], tmpB, lam[:, 4 + b:5 + b], tmpA,
                                                            ALU.mult, ALU.add))
                    dve.wait_ge(cnt_turned, TB)
                    A, Bt, Cc = tmpC[:, :, :], tmpB[:, :, :], tmpA[:, :, :]
                    log_in(A, ps[:, 4:4 + KB, :].bitcast(bf16)[:, :, 0:512], Bt)
                    dve.wait_ge(ln_out, 2)
                    link(nc.vector.scalar_tensor_tensor(Bt, A, 1.0 / SCALE1, Bt, ALU.mult, ALU.add))
                    pm = pmT_s.rearrange("p (t k) -> p t k", t=TB)
                    for b in range(B):
                        link(nc.vector.tensor_scalar(A, pm, 1.0, lam[:, 6 + b:7 + b], ALU.subtract, ALU.mult))
                        link(nc.vector.scalar_tensor_tensor(Cc, Bt, lam[:, 4 + b:5 + b], A, ALU.mult, ALU.add))
                        link(nc.vector.tensor_copy(r.biasTh[:, b, :, :], Cc))
                        o = nc.vector.tensor_tensor(r.biasTl[:, b, :, :], Cc, r.biasTh[:, b, :, :].bitcast(f32),
                                                    ALU.subtract)
                        if b < B - 1:
                            link(o)
                    o.then_inc(biasT_out, 1)

                def maxima(b, u):
                    dve.wait_ge(sn1, b * NU + u + 1)
                    k = 4 * (u % 2) if (r.fast and b == 0) else 0
                    if r.fast:
                        o = nc.vector.tensor_reduce(mraw[:, b, u, :],
                                                    ps[:, k:k + 4, :].rearrange("p g (i k) -> p g i k", i=4),
                                                    axis=AX.X, op=ALU.max, negate=True)
                    else:
                        o = nc.vector.tensor_reduce(mraw[:, b, :, u], ps[:, 0:4, :], axis=AX.X, op=ALU.max, negate=True)
                    o.then_inc(max1, 1)

                def negate(b):
                    dve.wait_ge(max1, (b + 1) * NU)
                    link(nc.vector.tensor_scalar(mtmp[:, :, :], mraw[:, b, :, :], BIG, None, ALU.mult))
                    link(nc.vector.tensor_tensor(mtmp[:, :, :], mtmp[:, :, :], mtmp[:, :, :], ALU.subtract))
                    nc.vector.tensor_tensor(negM1[:, b, :, :], mraw[:, b, :, :], mtmp[:, :, :], ALU.add)\
                        .then_inc(negm1, 1)

                def values(b):
                    dve.wait_ge(ld_pm, 32)
                    for k in range(KB):
                        n = b * KB + k
                        dve.wait_ge(v1_proj, n + 1)
                        nc.vector.tensor_tensor(V1[:, b * TB + k, :], ps[:, r.vbank(n), :], bv1_s[:, :], ALU.add)\
                            .then_inc(v1_out, 1)

                for u in range(NU):
                    maxima(0, u)
                negate(0)
                values(0)
                values(1)
                def named(n, heads):
                    for i in heads if r.fast else ():
                        c = 4 * n + i
                        dve.wait_ge(exp1, c + 1)
                        nc.vector.scalar_tensor_tensor(P1[:, c % 8, :], P1[:, c % 8, :], 2.0, cntT[:, :],
                                                       ALU.min, ALU.mult).then_inc(dve_named, 1)

                for u in range(NU):
                    maxima(1, u)
                    if u < G1 - 1:
                        named(u, (0, 2, 3))
                negate(1)
                named(G1 - 1, (0, 2, 3))
                named(G1, (0, 2, 3))
                normalise(0)
                named(G1 + 1, (0, 2, 3))
                named(G1 + 2, (0, 2, 3))
                projected(0)
                moments(0)
                named(G1 + 3, (0, 2, 3))
                standardise(0)
                xn_split(0, 7)
                now[0] = dve_step

            def splits(r, q):
                for g in range(G1):
                    j = q * G1 + g
                    dve.wait_ge(qk_out, j + 1)
                    if q < B:
                        parts, to, n, col = ((64, 128),), Q1[:, q, g, :], S, L_BQ1
                    else:
                        parts, to, n, col = ((32, 64), (64, 96)), Ks[:, g, 0:r.W], r.W, L_BK1
                    bank = ps[:, j if q < B else G1 + g, 0:n]
                    for i, e in parts:
                        o = nc.vector.scalar_tensor_tensor(to[i:e], bank[i:e], col_s[i:e, col + g:col + g + 1],
                                                           to[i:e].bitcast(f32), ALU.add, ALU.subtract)
                    o.then_inc(qk_low, 1)

            branch(dve, first)

            def keys_low(n):
                p = n % NP
                dve.wait_ge(kh_out, n + 1)
                for j in range(2):
                    own, other = slice(64 * j, 64 * j + 64), slice(64 - 64 * j, 128 - 64 * j)
                    o = nc.vector.scalar_tensor_tensor(KK[other, n % 3, j, :], ps[own, 7, :],
                                                       col_s[own, L_BK2 + p:L_BK2 + p + 1],
                                                       KK[own, n % 3, j, :].bitcast(f32), ALU.add, ALU.subtract)
                o.then_inc(kl_out, 1)

            def queries_low(n):
                p = n % NP
                dve.wait_ge(qh_own, n + 1)
                for j in range(2):
                    rows = slice(64 * j, 64 * j + 64)
                    o = nc.vector.scalar_tensor_tensor(QL[rows, n % 2, j, :], ps[rows, 7, :],
                                                       col_s[rows, L_BQ2 + p:L_BQ2 + p + 1],
                                                       QH[rows, n % 2, j, :].bitcast(f32), ALU.add, ALU.subtract)
                o.then_inc(ql_out, 1)

            def maxima2(h):
                dve.wait_ge(sn2, h + 1)
                for q in range(TB):
                    bank, at = QPOS[q]
                    o = nc.vector.tensor_reduce(negM2[:, q, h:h + 1], ps[:, bank, at:at + 128 * (q + 1)],
                                                axis=AX.X, op=ALU.max, negate=True)
                o.then_inc(max2, 1)

            def sums_out(n):
                dve.wait_ge(sum2, n + 1)
                b = n // NP
                if n % NP == 0:
                    o = nc.vector.tensor_copy(sums[:, b, :], ps[:, 5, 384:512])
                else:
                    dve.wait_ge(sum2_out, n)
                    o = nc.vector.tensor_tensor(sums[:, b, :], sums[:, b, :], ps[:, 5, 384:512], ALU.add)
                o.then_inc(sum2_out, 1)

            def reciprocals(b):
                dve.wait_ge(sum2_out, (b + 1) * NP)
                if b:
                    dve.wait_ge(r2, b * NP)
                link(nc.vector.reciprocal(rsum[:, :], sums[:, b, :]))
                for c in range(4):
                    o = nc.vector.tensor_scalar(RDf[:, c, :], rsum[:, :], row_group[:, c:c + 1], None, ALU.mult)
                link(o)
                link(nc.vector.tensor_copy(RDh[:, :, :], RDf[:, :, :]))
                nc.vector.tensor_tensor(RDl[:, :, :], RDf[:, :, :], RDh[:, :, :].bitcast(f32), ALU.subtract)\
                    .then_inc(rd_out, 1)

            def scaled(b, p, bank):
                dve.wait_ge(r2, b * NP + p + 1)
                dve.wait_ge(z2_out, b * NP + p + 1)
                nc.vector.tensor_tensor(z2[:, b, p, :], ps[:, bank, :], z2[:, b, p, :], ALU.mult).then_inc(zn_out, 1)

            def diffuse(b):
                y = x1T[:, b, :]
                dve.wait_ge(wo2_done, b + 1)
                nc.vector.scalar_tensor_tensor(y, ps[:, X1_BANK[b], :], cvec[:, 0:1], xT_s[:, b * S:(b + 1) * S],
                                               ALU.add, ALU.add).then_inc(x1_out, 1)
                dve.wait_ge(x1_out, b + 1)
                nc.vector.tensor_tensor(dif[:, 1:S - 1], y[:, 0:S - 2], y[:, 2:S], ALU.add)
                nc.vector.tensor_scalar(dif[:, 0:1], y[:, 1:2], 2.0, None, ALU.mult)
                link(nc.vector.tensor_scalar(dif[:, S - 1:S], y[:, S - 2:S - 1], 2.0, None, ALU.mult))
                link(nc.vector.scalar_tensor_tensor(dif2, y, -2.0, dif, ALU.mult, ALU.add))
                link(nc.vector.tensor_scalar(rea[:, :], y, -1.0, 1.0, ALU.mult, ALU.add))
                link(nc.vector.scalar_tensor_tensor(rea[:, :], y, scal_s[:, 6 + b:7 + b], rea[:, :], ALU.mult, ALU.mult))
                link(nc.vector.scalar_tensor_tensor(dif2, dif2, scal_s[:, 4 + b:5 + b], rea[:, :],
                                                    ALU.mult, ALU.add))
                dve.wait_ge(lap_done, b + 1)
                nc.vector.scalar_tensor_tensor(duT[:, b, :], ps[:, X1_BANK[b], :], scal_s[:, 2 + b:3 + b], dif2,
                                               ALU.mult, ALU.add).then_inc(du_out, 1)
                dve.wait_ge(du_out, b + 1)
                link(nc.vector.tensor_copy(du_h[:, b, :], duT[:, b, :]))
                nc.vector.tensor_tensor(du_l[:, b, :], duT[:, b, :], du_h[:, b, :].bitcast(f32), ALU.subtract)\
                    .then_inc(du_split, 1)

            bc = lambda k: gs[:, k, :].unsqueeze(2).broadcast_to([128, TB, NE])

            def gates_in(b):
                dve.wait_ge(gate_done, b + 1)
                link(nc.vector.tensor_copy(gl[:, 0, :, :],
                                           ps[:, GATE_BANK[b], 0:TB * NE].rearrange("p (t e) -> p t e", t=TB)))
                link(nc.vector.tensor_reduce(gs[:, 0, :], gl[:, 0, :, :], axis=AX.X, op=ALU.max))
                nc.vector.tensor_tensor(gl[:, 1, :, :], gl[:, 0, :, :], bc(0), ALU.subtract).then_inc(gmax_out, 1)

            def gates(b):
                dve.wait_ge(gexp_out, b + 1)
                link(nc.vector.tensor_reduce(gs[:, 1, :], gl[:, 1, :, :], axis=AX.X, op=ALU.add))
                link(nc.vector.reciprocal(gs[:, 1, :], gs[:, 1, :]))
                link(nc.vector.tensor_tensor(gl[:, 2, :, :], gl[:, 1, :, :], bc(1), ALU.mult))
                rank = cst[:, C_RANK:C_RANK + NE].unsqueeze(1).broadcast_to([128, TB, NE])
                for k in range(2):
                    w, eq, key, hot = gl[:, 2 + 4 * k, :, :], gl[:, 3 + 4 * k, :, :], gl[:, 4 + 4 * k, :, :], gl[:, 5 + 4 * k, :, :]
                    link(nc.vector.tensor_reduce(gs[:, 2 + 2 * k, :], w, axis=AX.X, op=ALU.max))
                    link(nc.vector.tensor_tensor(eq, w, bc(2 + 2 * k), ALU.is_equal))
                    link(nc.vector.tensor_tensor(key, eq, rank, ALU.mult))
                    link(nc.vector.tensor_reduce(gs[:, 3 + 2 * k, :], key, axis=AX.X, op=ALU.max))
                    link(nc.vector.tensor_tensor(hot, key, bc(3 + 2 * k), ALU.is_equal))
                    if k == 0:
                        link(nc.vector.scalar_tensor_tensor(gl[:, 6, :, :], hot, -2.0, w, ALU.mult, ALU.add))
                link(nc.vector.tensor_tensor(gl[:, 10, :, :], gl[:, 5, :, :], gl[:, 9, :, :], ALU.add))
                link(nc.vector.tensor_tensor(gl[:, 10, :, :], gl[:, 10, :, :], gl[:, 2, :, :], ALU.mult))
                link(nc.vector.tensor_tensor(gs[:, 6, :], gs[:, 2, :], gs[:, 4, :], ALU.add))
                link(nc.vector.reciprocal(gs[:, 7, :], gs[:, 6, :]))
                link(nc.vector.tensor_tensor(comb[:, b, :, :], gl[:, 10, :, :], bc(7), ALU.mult))

            def mix(b):
                dve.wait_ge(ya_ready, b + 1)
                for t in range(TB):
                    for q in range(2):
                        dve.wait_ge(down_done, (b * TB + t) * 2 + q + 1)
                        for e in range(4):
                            o = nc.vector.scalar_tensor_tensor(
                                ya[:, b, t, :], ps[:, 4 + q, e * 128:(e + 1) * 128],
                                comb[:, b, t, 4 * q + e:4 * q + e + 1], ya[:, b, t, :], ALU.mult, ALU.add)
                            if e < 3:
                                link(o)
                        o.then_inc(mixed, 1)
                        if q == 0:
                            dve.wait_ge(mixed, (b * TB + t) * 2 + 1)

            normalise(1)
            keys_low(0)
            queries_low(0)
            projected(1)
            keys_low(1)
            maxima2(0)
            for n in range(B * NP):
                maxima2(2 * n + 1)
                if n < B * NP - 1:
                    queries_low(n + 1)
                if n == 1:
                    standardise(1)
                if n == 2:
                    xn_split(1, 6)
                if n == NP:
                    sums_out(n - 1)
                    reciprocals(0)
                if n < B * NP - 1:
                    maxima2(2 * n + 2)
                if n < B * NP - 2:
                    keys_low(n + 2)
                if n > NP:
                    scaled(0, n - NP - 1, 7)
                if n == 0:
                    moments(1)
                if n == 1:
                    dve.wait_ge(cvec_done, 1)
                    nc.vector.tensor_scalar(cvec[:, :], ps[:, 7, 0:1], col_s[:, L_BO2:L_BO2 + 1], None, ALU.add)\
                        .then_inc(cvec_out, 1)
                if n % NP:
                    sums_out(n - 1)
            scaled(0, NP - 1, 7)
            sums_out(n)
            reciprocals(1)
            for p in range(NP):
                scaled(1, p, SPREAD[p])
            diffuse(0)
            gates_in(0)
            diffuse(1)
            gates(0)
            gates_in(1)
            mix(0)
            gates(1)
            mix(1)

        @block.tensor
        def _(pe):
            pe.wait_ge(ld_q1, 16)
            for j in range(B * G1):
                b, g = j // G1, j % G1
                if g == 0:
                    pe.wait_ge(ld_x, 16 * B)
                if j == G1 - 1:
                    pe.wait_ge(flag_in, 1)
                    mm(ps[0:1, 7, 0:1], path[:, 3:4], ones_band[:, 31:32], start=True, stop=True).then_inc(flag_sum, 1)
                if j == B * G1 - 1:
                    pe.wait_ge(flag_ready, 1)
                mm(ps[:, j % 8, :], wq1_s[:, g * 128:(g + 1) * 128], xT_s[:, b * S:(b + 1) * S],
                   start=True, stop=True).then_inc(proj1, 1)

            def turn_z(b):
                pe.wait_ge(z1_out, (b + 1) * G1)
                for q in range(TB):
                    for g in range(G1):
                        o = nc.tensor.transpose(ps[:, q, g * 128:(g + 1) * 128],
                                                zT1[:, g, q * 128:(q + 1) * 128], ident)
                    o.then_inc(z1_turned, 1)

            def turn_zc(b):
                pe.wait_ge(norm1, (b + 1) * TB)
                for q in range(TB):
                    o = nc.tensor.transpose(ps[:, 0, q * 128:(q + 1) * 128], zc[:, q, :], ident)
                o.then_inc(zc_turned, 1)

            def project_out1(b):
                pe.wait_ge(zcT_out, b + 1)
                pe.wait_ge(ld_o1, 48)
                for q in range(TB):
                    o = mm(ps[:, 1, q * 128:(q + 1) * 128], zcT[:, q * 128:(q + 1) * 128], wo1_s[:, :],
                           start=True, stop=True)
                o.then_inc(wo1_done, 1)

            def turn_xh(b, bank):
                pe.wait_ge(xh_out, b + 1)
                for q in range(TB):
                    o = nc.tensor.transpose(ps[:, bank, q * 128:(q + 1) * 128], xh[:, q, :], ident)
                o.then_inc(xh_turned, 1)

            def first(r):
                KB, W, NU, NQ = r.KB, r.W, r.NU, r.NQ
                def project_keys(b):
                    for g in range(G1):
                        pe.wait_ge(qk_low, G1 + b * G1 + g + 1)
                        mm(ps[:, 4 + g, 0:W], wk1_s[:, g * 128:(g + 1) * 128], xT_s[:, b * S:b * S + W],
                           start=True, stop=True).then_inc(proj1, 1)

                pe.wait_ge(cst_ready, 1)
                for q in range(TB):
                    pe.wait_ge(qk_low, q + 1)
                    if r.fast and q >= 2:
                        pe.wait_ge(cnt_out, q - 1)
                    for j in range(KS):
                        n = q * (KS // r.J) + j // r.J
                        pe.wait_ge(onehot, n + 1)
                        mm(ps[:, r.cbank(q), 0:W], ident_b[:, :], r.oh[:, n % 4, :, j % r.J], start=(j == 0),
                           stop=(j == KS - 1)).then_inc(counted, 1)
                    if q == 1:
                        pe.wait_ge(ld_w1, 48)
                    if 1 <= q <= B:
                        project_keys(q - 1)
                if not r.fast:
                    pe.wait_ge(qk_low, 2 * B * G1)
                for q in range(TB):
                    pe.wait_ge(cnt_out, q + 1)
                    for k in range(KB):
                        o = nc.tensor.transpose(ps[:, 2 if r.fast else 4 + k, :].bitcast(bf16)[:, q * 128:(q + 1) * 128],
                                                r.cnt[:, q, k * 128:(k + 1) * 128], ident_b[:, :])
                    o.then_inc(cnt_turned, 1)

                def scores_max(b, u):
                    n = b * NU + u
                    k = 4 * (u % 2) if (r.fast and b == 0) else 0
                    if r.fast and b == 0:
                        if u >= 2:
                            pe.wait_ge(max1, u - 1)
                        if u == 1:
                            pe.wait_ge(qk_low, 2 * B * G1)
                    elif n:
                        pe.wait_ge(max1, n - 1 if r.fast and u == 0 else n)
                    bn = r.biasN[:, b % r.nb]
                    km = r.Km[:, b % r.nk]
                    for j in (0, 1, 3, 2):
                        if r.fast and n == 0 and j == 2:
                            pe.wait_ge(biasT_out, 1)
                        if r.fast:
                            mm(ps[:, k + j, :].rearrange("p (i k) -> p i k", i=4), ident_b[:, :],
                               bn[:, u, :].unsqueeze(1).broadcast_to([128, 4, W]), start=True, stop=False)
                            o = mm(ps[:, k + j, :], Q1[:, b, j, u * 128:(u + 1) * 128], km[:, 4 * j:4 * j + 4, :],
                                   start=False, stop=True)
                        else:
                            mm(ps[:, j, :], ident_b[:, :], bn[:, j, :], start=True, stop=False)
                            o = mm(ps[:, j, :], Q1[:, b, u // 4, j * 128:(j + 1) * 128], km[:, u, :],
                                   start=False, stop=True)
                    o.then_inc(sn1, 1)

                def scores(b, q):
                    g, k = q // KB, q % KB
                    for i in range(4):
                        h = 4 * g + i
                        c = (b * NQ + q) * 4 + i
                        if c >= 2:
                            pe.wait_ge(exp1, c - 1)
                        bank = ps[:, 4 + c % 2, :]
                        mm(bank, r.Km[:, b % r.nk, h, k * 128:(k + 1) * 128], Q1[:, b, g, :], start=True, stop=False)
                        if not r.fast:
                            mm(bank, ident_r[:, :], r.biasTh[:, b % r.nb, k, :], start=False, stop=False)
                            mm(bank, ident_r[:, :], r.biasTl[:, b % r.nb, k, :], start=False, stop=False)
                        for t in range(TB):
                            o = mm(bank[:, t * 128:(t + 1) * 128], negM1[:, b, t, h:h + 1].to_broadcast([128, 128]),
                                   ident_r[:, :], start=False, stop=(t == TB - 1))
                        o.then_inc(st1, 1)

                def weigh(b, q):
                    g, k = q // KB, q % KB
                    if r.fast:
                        pe.wait_ge(dve_named, (b * NQ + q + 1) * 3)
                        pe.wait_ge(pool_named, b * NQ + q + 1)
                    else:
                        pe.wait_ge(exp1, (b * NQ + q + 1) * 4)
                    pe.wait_ge(v1_out, B * KB)
                    if k == 0 and b * G1 + g:
                        pe.wait_ge(z1_out, b * G1 + g)
                    for i in range(4):
                        h = 4 * g + i
                        c = (b * NQ + q) * 4 + i
                        o = mm(ps[32 * i:32 * i + 32, 6, :], V1[:, b * TB + k, h * PAD:(h + 1) * PAD], P1[:, c % 8, :],
                               start=(k == 0), stop=(k == KB - 1))
                    o.then_inc(pv1, 1)

                def values():
                    for b in range(B):
                        for k in range(KB):
                            n = b * KB + k
                            t = b * TB + k
                            if n == 0:
                                pe.wait_ge(max1, NU)
                            if n >= 4:
                                pe.wait_ge(v1_out, n - 3)
                            mm(ps[:, r.vbank(n), :], xT_s[:, t * 128:(t + 1) * 128], wv1_s, start=True, stop=True)\
                                .then_inc(v1_proj, 1)

                pe.wait_ge(km_out, G1)
                for u in range(NU):
                    if r.fast:
                        pe.wait_ge(biasN_out, u + 1)
                    elif u == 0:
                        pe.wait_ge(biasT_out, 1)
                    scores_max(0, u)
                if r.fast:
                    pe.wait_ge(km_out, 2 * G1)
                    scores_max(1, 0)
                values()
                pe.wait_ge(negm1, 1)
                for q in range(NQ):
                    if r.fast and q:
                        scores_max(1, q)
                    scores(0, q)
                    if q:
                        weigh(0, q - 1)
                if not r.fast:
                    pe.wait_ge(v1_out, B * KB)
                    pe.wait_ge(km_out, 2 * G1)
                    for u in range(NU):
                        scores_max(1, u)
                pe.wait_ge(negm1, 2)
                for q in range(NQ):
                    scores(1, q)
                    weigh(*((1, q - 1) if q else (0, NQ - 1)))
                    if q == 0:
                        pe.wait_ge(max1, 2 * NU)
                        turn_z(0)
                    if q == KB:
                        turn_zc(0)
                    if q == 2 * KB:
                        project_out1(0)
                weigh(1, NQ - 1)
                turn_xh(0, 7)

            branch(pe, first)

            def value_unit(b, t):
                bank = vbank(b, t)
                if b == 0 and t >= 4:
                    pe.wait_ge(v2_out, t - 3)
                if b and t >= 3:
                    pe.wait_ge(v2_out, 2 * TB + t - 2)
                at = slice(b * S + (t // 2) * 128, b * S + (t // 2 + 1) * 128)
                c = slice((t % 2) * 512, (t % 2 + 1) * 512)
                mm(ps[:, bank, :], xn_h[:, at], w_h[:, 0, c], start=True, stop=False)
                mm(ps[:, bank, :], xn_h[:, at], w_l[:, 0, c], start=False, stop=False)
                mm(ps[:, bank, :], xn_l[:, at], w_h[:, 0, c], start=False, stop=True).then_inc(vproj2, 1)

            def project(w, n, done):
                b, p = n // NP, n % NP
                c, t = slice(p * 128, (p + 1) * 128), slice(b * S, (b + 1) * S)
                mm(ps[:, 7, :], w_h[:, w, c], xn_h[:, t], start=True, stop=False)
                mm(ps[:, 7, :], w_l[:, w, c], xn_h[:, t], start=False, stop=False)
                mm(ps[:, 7, :], w_h[:, w, c], xn_l[:, t], start=False, stop=True).then_inc(done, 1)

            def scores_max2(h):
                n, s, j = h // 2, (h // 2) % 2, h % 2
                pe.wait_ge(kl_out, n + 1)
                pe.wait_ge(qh_out, n + 1)
                if h:
                    pe.wait_ge(max2, h)
                for q in range(TB):
                    bank, at = QPOS[q]
                    mm(ps[:, bank, at:at + 128 * (q + 1)], QH[:, s, j, q * 128:(q + 1) * 128],
                       KK[:, n % 3, j, 0:128 * (q + 1)], start=(q != 2), stop=False)
                two = ident_r[:, :].unsqueeze(1).broadcast_to([128, 2, 128])
                for bank, at, w in ((0, 384, 1), (1, 256, 2), (2, 128, 1)):
                    o = mm(ps[:, bank, at:at + 128 * w].rearrange("p (w k) -> p w k", w=w), causal_r[:, :],
                           two[:, 0:w, :], start=False, stop=True)
                o.then_inc(sn2, 1)

            def scores2(h):
                n, s, j = h // 2, (h // 2) % 2, h % 2
                pe.wait_ge(ql_out, n + 1)
                if h == 0:
                    pe.wait_ge(zeroed, 2)
                if h:
                    pe.wait_ge(exp2, h)
                if n == NP and j == 0:
                    pe.wait_ge(v2_out, B * 2 * TB)
                if n % NP > 1 and j == 0:
                    pe.wait_ge(sum2_out, n - 1)
                st = ps[:, 3:6, :].rearrange("p b n -> p (b n)")
                for k in range(TB):
                    a, e = KOFF[k], KOFF[k] + 128 * (TB - k)
                    kc = slice(k * 128, (k + 1) * 128)
                    mm(st[:, a:e], KK[:, n % 3, j, kc], QH[:, s, j, k * 128:S], start=(k != 3), stop=False)
                    mm(st[:, a:e], KK[:, n % 3, j, kc], QL[:, s, j, k * 128:S], start=False, stop=False)
                two = causal_r[:, :].unsqueeze(1).broadcast_to([128, 2, 128])
                for a, n in ((KOFF[0], 1), (KOFF[3], 2), (KOFF[2], 1)):
                    mm(st[:, a:a + 128 * n].rearrange("p (n q) -> p n q", n=n), ident_r[:, :], two[:, 0:n, :],
                       start=False, stop=False)
                pe.wait_ge(diag_out, h + 1)
                for k in range(TB):
                    a, e = KOFF[k], KOFF[k] + 128 * (TB - k)
                    o = mm(st[:, a:e].rearrange("p (t q) -> p t q", q=128), ones_r[:, :], diag[:, h % 2, k:TB, :],
                           start=False, stop=(k != 1))
                o.then_inc(st2, 1)

            def weigh2(n):
                pe.wait_ge(exp2, 2 * n + 2)
                pe.wait_ge(v2_out, (n // NP + 1) * 2 * TB)
                if n:
                    pe.wait_ge(z2_out, n)
                if n == 1:
                    pe.wait_ge(xn_out, B)
                for k in range(TB):
                    for j in range(2):
                        h = 2 * n + j
                        o = mm(ps[64 * j:64 * j + 64, 6, k * 128:S],
                               V2[:, k, (h % H2) * E2:(h % H2 + 1) * E2],
                               P2[:, h % 4, KOFF[k]:KOFF[k] + 128 * (TB - k)], start=(k == 0), stop=(k == TB - 1))
                o.then_inc(pv2, 1)

            def sum_rows(n):
                pe.wait_ge(acc2, 2 * n + 2)
                if n % NP == NP - 1:
                    pe.wait_ge(sum2_out, n)
                pe.wait_ge(exp2, 2 * n + (4 if n % NP < NP - 1 else 2))
                for j in range(2):
                    h = 2 * n + j
                    for c in range(4):
                        r = P2[:, h % 4, 0:128] if c == 0 else acc[:, h % 4, c * 128:(c + 1) * 128]
                        o = mm(ps[32 * c:32 * c + 32, 5, 384:512], ones_band[:, 31 - h % H2:63 - h % H2], r,
                               start=(j == 0), stop=(j == 1))
                o.then_inc(sum2, 1)

            def spread(b, p, bank):
                mm(ps[:, bank, :], sel_r[:, p, :], RDh[:, :, :], start=True, stop=False)
                mm(ps[:, bank, :], sel_r[:, p, :], RDl[:, :, :], start=False, stop=True).then_inc(r2, 1)

            def project_out2(b, p):
                pe.wait_ge(zn_out, b * NP + p + 1)
                o = mm(ps[:, X1_BANK[b], :], w_o[:, p, :], z2[:, b, p, :], start=(p == 0), stop=(p == NP - 1))
                if p == NP - 1:
                    o.then_inc(wo2_done, 1)

            def second_difference(b):
                pe.wait_ge(x1_out, b + 1)
                mm(ps[:, X1_BANK[b], :], lap, x1T[:, b, :], start=True, stop=True).then_inc(lap_done, 1)

            def gate(b):
                pe.wait_ge(du_out, b + 1)
                for t in range(TB):
                    o = mm(ps[:, GATE_BANK[b], t * NE:(t + 1) * NE], duT[:, b, t * 128:(t + 1) * 128], wg_s[:, :],
                           start=True, stop=True)
                o.then_inc(gate_done, 1)
                if b:
                    pe.wait_ge(ya_ready, b)
                for t in range(TB):
                    o = nc.tensor.transpose(ps[:, 7, t * 128:(t + 1) * 128], x1T[:, b, t * 128:(t + 1) * 128], ident)
                o.then_inc(x1_turned, 1)

            def up(b, n):
                if n >= 4 or b:
                    pe.wait_ge(silu_out, b * NT + n - 3)
                c = slice(n * 128, (n + 1) * 128)
                pe.wait_ge(du_split, b + 1)
                mm(ps[:, n % 4, :], w1_h[:, c], du_h[:, b, :], start=True, stop=False)
                mm(ps[:, n % 4, :], w1_l[:, c], du_h[:, b, :], start=False, stop=False)
                mm(ps[:, n % 4, :], w1_h[:, c], du_l[:, b, :], start=False, stop=True).then_inc(up_done, 1)

            def down(b, t):
                for q in range(2):
                    if b * TB + t:
                        pe.wait_ge(mixed, (b * TB + t - 1) * 2 + q + 1)
                    for e in range(4 * q, 4 * q + 4):
                        for k in range(2):
                            o = mm(ps[:, 4 + q, (e % 4) * 128:(e % 4 + 1) * 128],
                                   hT[:, 2 * e + k, t * 128:(t + 1) * 128], w2_s[:, 2 * e + k, :],
                                   start=(k == 0), stop=(k == 1))
                    o.then_inc(down_done, 1)

            turn_z(1)
            pe.wait_ge(xn_out, 1)
            pe.wait_ge(w_split, 1)
            pe.wait_ge(w_split, 3)
            project(1, 0, kproj2)
            for t in range(3):
                value_unit(0, t)
            turn_zc(1)
            pe.wait_ge(kl_out, 1)
            project(2, 0, qproj2)
            for t in range(3, 5):
                value_unit(0, t)
            project_out1(1)
            value_unit(0, 5)
            pe.wait_ge(ql_out, 1)
            project(1, 1, kproj2)
            for t in range(6, 2 * TB):
                value_unit(0, t)
            pe.wait_ge(y_out, 2)
            pe.wait_ge(v2_out, 2 * TB)
            scores_max2(0)
            pe.wait_ge(kl_out, 2)
            project(2, 1, qproj2)
            for n in range(B * NP):
                b, p = n // NP, n % NP
                scores_max2(2 * n + 1)
                if n == NP:
                    weigh2(n - 1)
                    sum_rows(n - 1)
                    for t in range(2 * TB):
                        if t == 2:
                            pe.wait_ge(sum2_out, n)
                        value_unit(1, t)
                scores2(2 * n)
                if n == 2:
                    pe.wait_ge(z2_out, 1)
                    turn_xh(1, 6)
                if n < B * NP - 1:
                    scores_max2(2 * n + 2)
                if n < B * NP - 2:
                    pe.wait_ge(ql_out, n + 2)
                    project(1, n + 2, kproj2)
                scores2(2 * n + 1)
                if p:
                    weigh2(n - 1)
                if n < B * NP - 2:
                    pe.wait_ge(kl_out, n + 3)
                if n > NP:
                    if p == 1:
                        pe.wait_ge(rd_out, 1)
                        pe.wait_ge(w_split, 4)
                    elif n >= B * NP - 2:
                        pe.wait_ge(zn_out, p - 1)
                        pe.wait_ge(ql_out, B * NP)
                    spread(0, p - 1, 7)
                if n == 1:
                    pe.wait_ge(ld_o2, 16)
                    for i in range(NP):
                        o = mm(ps[:, 7, 0:1], w_o[:, i, :], col_s[:, L_BV2 + i:L_BV2 + i + 1],
                               start=(i == 0), stop=(i == NP - 1))
                    o.then_inc(cvec_done, 1)
                    pe.wait_ge(cvec_out, 1)
                if n > NP:
                    sum_rows(n - 1)
                    if n < B * NP - 2:
                        pe.wait_ge(zn_out, p)
                if n < B * NP - 2:
                    project(2, n + 2, qproj2)
                if p and n < NP:
                    sum_rows(n - 1)
            pe.wait_ge(zn_out, NP - 1)
            spread(0, NP - 1, 7)
            weigh2(2 * NP - 1)
            sum_rows(2 * NP - 1)
            pe.wait_ge(zn_out, NP)
            for p in range(NP):
                if p == NP // 2:
                    pe.wait_ge(rd_out, 2)
                    for i in range(NP // 2):
                        spread(1, i, SPREAD[i])
                project_out2(0, p)
            for p in range(NP // 2, NP):
                if p >= 6:
                    pe.wait_ge(zn_out, NP + p - 5)
                spread(1, p, SPREAD[p])
            pe.wait_ge(z2_out, 2 * NP)
            for p in range(NP):
                project_out2(1, p)
                if p == NP // 2:
                    second_difference(0)
            gate(0)
            pe.wait_ge(ld_late, 32)
            pe.wait_ge(w1_split, 4)
            for n in range(NT):
                up(0, n)
                if n == 4:
                    second_difference(1)
                if n == 12:
                    gate(1)
            for n in range(3):
                up(1, n)
            pe.wait_ge(silu_out, NT)
            pe.wait_ge(gmax_out, 1)
            for t in range(TB):
                down(0, t)
            for n in range(3, NT):
                up(1, n)
            pe.wait_ge(silu_out, 2 * NT)
            for t in range(TB):
                down(1, t)


def vbank(b, t):
    return 3 + t % 3 if b else (4, 5, 6, 3)[t % 4]


C_ID = 0
C_BAND = C_ID + 128
C_RG = C_BAND + 63
C_LAP = C_RG + 4
C_CAUT = C_LAP + 128
C_RANK = C_CAUT + 128
C_HEAD = C_RANK + NE
CONSTS = C_HEAD + 4

L_BQ1 = 0
L_BK1 = L_BQ1 + G1
L_BQ2 = L_BK1 + G1
L_BK2 = L_BQ2 + NP
L_BO2 = L_BK2 + NP
L_LNW = L_BO2 + 1
L_LNB = L_LNW + 1
L_BV2 = L_LNB + 1
COLS = L_BV2 + NP


def kernel(**inputs):
    import numpy as np
    import concourse.bacc as bacc
    from concourse.bass_utils import run_bass_kernel_spmd

    f = {k: np.asarray(v) for k, v in inputs.items()}
    F = np.float32

    def rows(a):
        return np.ascontiguousarray(np.broadcast_to(a.reshape(1, -1), (128, a.size)))

    def padded(wt):
        o = np.zeros((wt.shape[0], H1, PAD), F)
        o[:, :, :E1] = wt.reshape(-1, H1, E1)
        return o.reshape(-1, H1 * PAD)

    def repeated(wt):
        return np.ascontiguousarray(np.repeat(wt.reshape(-1, G1, 1, 4 * E1), 4, axis=2).reshape(-1, H1 * PAD))

    cst = np.zeros((128, CONSTS), F)
    r = np.arange(128)
    cst[:, C_ID:C_ID + 128] = np.eye(128)
    cst[:, [C_BAND + 31, C_BAND + 31 + H2]] = 1
    cst[r, C_HEAD + r % 32 // E1] = 1
    cst[r, C_RG + r // 32] = 1
    lap = -2 * np.eye(128) + np.eye(128, k=1) + np.eye(128, k=-1)
    lap[0, 1] = 2
    lap[127, 126] = 2
    cst[:, C_LAP:C_LAP + 128] = lap.T
    cst[:, C_CAUT:C_CAUT + 128] = np.where(r[:, None] > r[None, :], -BIG, 0)
    cst[:, C_RANK:C_RANK + NE] = np.arange(NE, 0, -1)
    sel = np.zeros((128, NP, 128), F)
    for p in range(NP):
        for j in range(2):
            sel[2 * p + j::32, p, 64 * j:64 * j + 64] = 1

    cols = np.zeros((128, COLS), F)
    cols[:, L_BQ1:L_BQ1 + G1] = repeated(f["L0_cond_bq"].reshape(1, -1)).reshape(G1, 128).T
    cols[:, L_BK1:L_BK1 + G1] = repeated(f["L0_cond_bk"].reshape(1, -1)).reshape(G1, 128).T
    cols[:, L_BQ2:L_BQ2 + NP] = f["L0_attn_b_q"].reshape(NP, 128).T
    cols[:, L_BK2:L_BK2 + NP] = f["L0_attn_b_k"].reshape(NP, 128).T
    cols[:, L_BO2] = f["L0_attn_b_o"]
    cols[:, L_LNW] = f["L0_attn_ln_w"]
    cols[:, L_LNB] = f["L0_attn_ln_b"]
    cols[:, L_BV2:L_BV2 + NP] = f["L0_attn_b_v"].reshape(NP, 128).T

    bv1 = padded(f["L0_cond_bv"].reshape(1, -1)).reshape(H1, PAD)
    bv1[:, E1] = 1
    idx = f["itok_Sx32_0_1023"]
    pm = f["mask_SxS_bk0"]

    def blocks(a):
        return np.ascontiguousarray(a.reshape(-1, 128, a.shape[1]).transpose(1, 0, 2).reshape(128, -1))

    def headed(w):
        return np.ascontiguousarray(w.transpose(1, 0, 2).reshape(D, H2 * E2))

    arrays = {
        "xT": np.ascontiguousarray(f["x"].reshape(T, D).T),
        "wq1": repeated(f["L0_cond_Wq"].T), "wk1": repeated(f["L0_cond_Wk"].T), "wv1": padded(f["L0_cond_Wv"].T),
        "wo1": np.ascontiguousarray(f["L0_cond_Wo"].T),
        "cols": cols, "bv1": rows(bv1), "bo1": rows(f["L0_cond_bo"]),
        "idx": blocks(idx), "imask": blocks(f["mask_Sx32_bk1"]),
        "pmN": blocks(pm), "pmT": blocks(pm.T),
        "scal": rows(np.concatenate([f["condB_uprev"], f["condB_zX"], f["condB_zY"], f["condB_zR"]])),
        "wq2": headed(f["L0_attn_W_q"]), "wk2": headed(f["L0_attn_W_k"]), "wv2": headed(f["L0_attn_W_v"]),
        "wo2": blocks(f["L0_attn_W_o"].reshape(H2 * E2, D)),
        "wg": np.ascontiguousarray(f["L0_ffn_Wg"]),
        "w1": np.ascontiguousarray(f["L0_ffn_W1"].transpose(1, 0, 2).reshape(D, NE * FH)),
        "w2": blocks(f["L0_ffn_W2"].reshape(NE * FH, D)),
        "consts": cst, "iota": rows(np.arange(S, dtype=np.float16)),
        "iotaj": rows(np.repeat(np.arange(128, dtype=np.float16), JH)), "sel": sel.reshape(128, -1),
    }
    nc = bacc.Bacc("TRN2", target_bir_lowering=False, num_devices=1)
    args = [nc.dram_tensor(k, a.shape, mybir.dt.from_np(a.dtype), kind="ExternalInput").ap() for k, a in arrays.items()]
    args.append(nc.dram_tensor("out", (B, S, D), mybir.dt.float32, kind="ExternalOutput").ap())
    program(nc, *args)
    r = run_bass_kernel_spmd(nc, [arrays], core_ids=[0])
    return r.results[0]["out"]
```
